# Optimizing a Trainium2 kernel written in Bass

```python
import numpy as np
import jax
import jax.numpy as jnp

def _softmax(x, axis=-1):
    return jax.nn.softmax(x, axis=axis)

def _gelu(x):
    return jax.nn.gelu(x, approximate=True)

def _silu(x):
    return jax.nn.silu(x)

def _sigmoid(x):
    return jax.nn.sigmoid(x)

def _layernorm(x, axis=-1, eps=1e-05):
    m = jnp.mean(x, axis=axis, keepdims=True)
    v = jnp.var(x, axis=axis, keepdims=True)
    return (x - m) / jnp.sqrt(v + eps)

def _scatter_add(tgt, idx, src, axis=0):
    return tgt.at[idx].add(src)

def _segment_sum(src, seg, n):
    return jax.ops.segment_sum(src, seg, n)
kernel_name = 'mk_early_fusion_d2_tok_img1024_r4_f647a9'

def setup_inputs(seed: int=0):
    np.random.seed(seed)
    _w = jnp.asarray

    def _rec_inputs():
        import jax
        import jax.numpy as jnp
        _rk = jax.random.key(seed)
        x = -4.65018e-05 + 0.999886 * jax.random.normal(jax.random.fold_in(_rk, 1), (32, 3, 128, 128), jnp.float32)
        txt = 0.419162 + 1.15059 * jax.random.normal(jax.random.fold_in(_rk, 2), (32, 32, 256), jnp.float32)
        return (x, txt)
    x, txt = _rec_inputs()

    def _L0_tok_setup():
        import jax, jax.numpy as jnp
        import numpy as np
        IMG_H = 128
        IMG_W = 128
        C = 3
        PH = 16
        PW = 16
        HID = 256
        NH = IMG_H // PH
        NW = IMG_W // PW
        PD = C * PH * PW
        BATCH = 64

        def sinusoidal_pos_embed(embed_dim, grid_size_x, grid_size_y):
            gh = jnp.arange(grid_size_y)
            gw = jnp.arange(grid_size_x)
            grid = jnp.stack(jnp.meshgrid(gh, gw, indexing='ij'), axis=0)
            h_pos = grid[0].reshape(-1).astype(jnp.float32)
            w_pos = grid[1].reshape(-1).astype(jnp.float32)
            quarter = embed_dim // 4
            factor = 10000.0 ** (jnp.arange(quarter, dtype=jnp.float32) / quarter)
            h = h_pos[:, None] / factor
            w = w_pos[:, None] / factor
            return jnp.concatenate([jnp.sin(h), jnp.cos(h), jnp.sin(w), jnp.cos(w)], axis=-1)
        key = jax.random.key(seed)
        k1, k2 = jax.random.split(key, 2)
        x = jax.random.normal(k1, (BATCH, C, IMG_H, IMG_W), dtype=jnp.float32)
        Wp = jax.random.normal(k2, (HID, PD), dtype=jnp.float32) * (1.0 / np.sqrt(PD))
        b = jnp.zeros((HID,), dtype=jnp.float32)
        return {'x': x, 'Wp': Wp, 'b': b}
    _L0_tok_all = _L0_tok_setup()
    _L0_tok_in = {k: v for k, v in _L0_tok_all.items() if k in ('Wp', 'b')}
    del _L0_tok_all

    def _L0_attn_setup():
        import jax, jax.numpy as jnp
        import numpy as np
        B, S, D = (2, 512, 256)
        H, DH = (16, 64)
        DQL, DKVL = (128, 128)
        DR = 64
        TOPK = 64
        LN_EPS = 1e-05
        ROPE_BASE = 10000.0

        def _rope_tables(seq_len, dim):
            inv_freq = 1.0 / ROPE_BASE ** (np.arange(0, dim, 2, dtype=np.float32) / dim)
            t = np.arange(seq_len, dtype=np.float32)
            freqs = np.outer(t, inv_freq)
            cos = np.concatenate([np.cos(freqs), np.cos(freqs)], -1)[:, ::2]
            sin = np.concatenate([np.sin(freqs), np.sin(freqs)], -1)[:, ::2]
            return (jnp.asarray(cos), jnp.asarray(sin))

        def _apply_rope_subspace(x, d_rope):
            s = x.shape[-2]
            cos, sin = _rope_tables(s, d_rope)
            xr, xp = (x[..., :d_rope], x[..., d_rope:])
            e, o = (xr[..., 0::2], xr[..., 1::2])
            rot = jnp.stack([e * cos - o * sin, e * sin + o * cos], axis=-1).reshape(xr.shape)
            return jnp.concatenate([rot, xp], axis=-1)

        def _reference_tuple_inner(x, w_down_q, w_down_kv, w_up_q, w_up_k, w_up_v, w_out, ln_scale, ln_bias):
            b, s, d = x.shape
            residual = x
            mu = jnp.mean(x, axis=-1, keepdims=True)
            var = jnp.mean((x - mu) ** 2, axis=-1, keepdims=True)
            h = (x - mu) * jax.lax.rsqrt(var + LN_EPS) * ln_scale + ln_bias
            c_q = h @ w_down_q.T
            c_kv = h @ w_down_kv.T
            q = (c_q @ w_up_q.T).reshape(b, s, H, DH).transpose(0, 2, 1, 3)
            k = (c_kv @ w_up_k.T).reshape(b, s, H, DH).transpose(0, 2, 1, 3)
            v = (c_kv @ w_up_v.T).reshape(b, s, H, DH).transpose(0, 2, 1, 3)
            q = _apply_rope_subspace(q, DR)
            k = _apply_rope_subspace(k, DR)
            scale = 1.0 / np.sqrt(DH).astype(np.float32)
            scores = jnp.einsum('bhqd,bhkd->bhqk', q, k) * scale
            _, indices = jax.lax.top_k(scores, min(TOPK, s))
            attn = jax.nn.softmax(scores, axis=-1)
            out = jnp.einsum('bhqk,bhkd->bhqd', attn, v)
            out = out.transpose(0, 2, 1, 3).reshape(b, s, H * DH)
            out = out @ w_out.T + residual
            return (out, indices.astype(jnp.int64))
        key = jax.random.key(seed)
        ks = jax.random.split(key, 7)
        init = lambda k, shape: jax.random.normal(k, shape, jnp.float32) * 0.02
        return {'x': jax.random.normal(ks[0], (B, S, D), jnp.float32), 'w_down_q': init(ks[1], (DQL, D)), 'w_down_kv': init(ks[2], (DKVL, D)), 'w_up_q': init(ks[3], (H * DH, DQL)), 'w_up_k': init(ks[4], (H * DH, DKVL)), 'w_up_v': init(ks[5], (H * DH, DKVL)), 'w_out': init(ks[6], (D, H * DH)), 'ln_scale': jnp.ones((D,), jnp.float32), 'ln_bias': jnp.zeros((D,), jnp.float32)}
    _L0_attn_all = _L0_attn_setup()
    _L0_attn_in = {k: v for k, v in _L0_attn_all.items() if k in ('w_down_q', 'w_down_kv', 'w_up_q', 'w_up_k', 'w_up_v', 'w_out', 'ln_scale', 'ln_bias')}
    del _L0_attn_all

    def _L0_ffn_setup():
        import jax, jax.numpy as jnp
        import numpy as np
        N_HEAD = 16
        NUM_EXPERTS = 8
        TOP_K = 2
        LN_EPS = 1e-05

        def _layernorm(x, g, b):
            mu = jnp.mean(x, axis=-1, keepdims=True)
            var = jnp.mean(jnp.square(x - mu), axis=-1, keepdims=True)
            return (x - mu) * jax.lax.rsqrt(var + LN_EPS) * g + b

        def _attention(h, Wq, bq, Wk, bk, Wv, bv, Wp, bp):
            B, T, D = h.shape
            hd = D // N_HEAD

            def split(z):
                return z.reshape(B, T, N_HEAD, hd).transpose(0, 2, 1, 3)
            q = split(h @ Wq + bq)
            k = split(h @ Wk + bk)
            v = split(h @ Wv + bv)
            att = jnp.einsum('bhqd,bhkd->bhqk', q, k) / jnp.sqrt(jnp.float32(hd))
            causal = jnp.tril(jnp.ones((T, T), bool))
            att = jnp.where(causal, att, -jnp.inf)
            att = jax.nn.softmax(att, axis=-1)
            y = jnp.einsum('bhqk,bhkd->bhqd', att, v)
            y = y.transpose(0, 2, 1, 3).reshape(B, T, D)
            return y @ Wp + bp

        def _token_moe(h, gate_W, gate_b, exp_W1, exp_b1, exp_W2, exp_b2):
            B, T, D = h.shape
            flat = h.reshape(-1, D)
            N = flat.shape[0]
            logits = flat @ gate_W + gate_b
            top_v, top_i = jax.lax.top_k(logits, TOP_K)
            w = jax.nn.softmax(top_v, axis=-1)
            w_full = jnp.zeros((N, NUM_EXPERTS), flat.dtype)
            w_full = w_full.at[jnp.arange(N)[:, None], top_i].add(w)
            out = jnp.zeros_like(flat)
            for e in range(NUM_EXPERTS):
                mid = jax.nn.gelu(flat @ exp_W1[e] + exp_b1[e], approximate=False)
                y_e = mid @ exp_W2[e] + exp_b2[e]
                out = out + w_full[:, e:e + 1] * y_e
            return out.reshape(B, T, D)
        key = jax.random.key(seed)
        B, T, D = (8, 256, 256)
        H = 4 * D
        E = NUM_EXPERTS
        ks = jax.random.split(key, 24)
        s = 0.02
        inp = {'x': jax.random.normal(ks[0], (B, T, D), jnp.float32), 'ln1_g': jnp.ones((D,), jnp.float32), 'ln1_b': jnp.zeros((D,), jnp.float32), 'ln2_g': jnp.ones((D,), jnp.float32), 'ln2_b': jnp.zeros((D,), jnp.float32), 'Wq': jax.random.normal(ks[1], (D, D), jnp.float32) * s, 'bq': jnp.zeros((D,), jnp.float32), 'Wk': jax.random.normal(ks[2], (D, D), jnp.float32) * s, 'bk': jnp.zeros((D,), jnp.float32), 'Wv': jax.random.normal(ks[3], (D, D), jnp.float32) * s, 'bv': jnp.zeros((D,), jnp.float32), 'Wp': jax.random.normal(ks[4], (D, D), jnp.float32) * s, 'bp': jnp.zeros((D,), jnp.float32), 'gate_W': jax.random.normal(ks[5], (D, E), jnp.float32) * s, 'gate_b': jnp.zeros((E,), jnp.float32), 'exp_W1': jax.random.normal(ks[6], (E, D, H), jnp.float32) * s, 'exp_b1': jnp.zeros((E, H), jnp.float32), 'exp_W2': jax.random.normal(ks[7], (E, H, D), jnp.float32) * s, 'exp_b2': jnp.zeros((E, D), jnp.float32)}
        return inp
    _L0_ffn_all = _L0_ffn_setup()
    _L0_ffn_in = {k: v for k, v in _L0_ffn_all.items() if k in ('ln1_g', 'ln1_b', 'ln2_g', 'ln2_b', 'Wq', 'bq', 'Wk', 'bk', 'Wv', 'bv', 'Wp', 'bp', 'gate_W', 'gate_b', 'exp_W1', 'exp_b1', 'exp_W2', 'exp_b2')}
    del _L0_ffn_all

    def _L1_attn_setup():
        import jax, jax.numpy as jnp
        import numpy as np
        import math
        B, N, D, H, G = (4, 512, 256, 16, 512)
        HD = D // H
        MAX_SEQ = 512
        STRIDE = (G - 1) / max(MAX_SEQ - 1, 1)

        def _forward(x, Wqkvg, bqkvg, wave_frequency, wave_damping, wave_phase, field_coupling, Wout, bout):
            b, n, d = x.shape
            qkvg = x @ Wqkvg.T + bqkvg
            q, k, v, gate_raw = jnp.split(qkvg, 4, axis=-1)
            to_heads = lambda t: t.reshape(b, n, H, HD).transpose(0, 2, 1, 3)
            q, k, v = (to_heads(q), to_heads(k), to_heads(v))
            seq_pos = jnp.arange(n, dtype=jnp.float32)
            field_pos = jnp.clip(seq_pos * STRIDE, 0.0, G - 2)
            idx_lo = jnp.clip(field_pos.astype(jnp.int32), 0, G - 2)
            idx_hi = idx_lo + 1
            frac = jnp.clip(field_pos - idx_lo.astype(jnp.float32), 0.0, 1.0)
            w_lo = (1.0 - frac)[None, None, :, None]
            w_hi = frac[None, None, :, None]
            q_feat = jax.nn.elu(q) + 1.0
            k_feat = jax.nn.elu(k) + 1.0
            deposit = k_feat * v
            field = jnp.zeros((b, H, G, HD), deposit.dtype)
            field = field.at[:, :, idx_lo, :].add(deposit * w_lo)
            field = field.at[:, :, idx_hi, :].add(deposit * w_hi)
            t = jnp.arange(G, dtype=jnp.float32)
            alpha = jax.nn.softplus(wave_damping)[:, None]
            omega = wave_frequency[:, None]
            phi = wave_phase[:, None]
            kernels = jnp.exp(-alpha * t[None, :]) * jnp.cos(omega * t[None, :] + phi)
            kernels = kernels / jnp.clip(jnp.sum(jnp.abs(kernels), axis=1, keepdims=True), 1e-08)
            kernel_fft = jnp.fft.rfft(kernels, n=2 * G, axis=-1)
            field_fft = jnp.fft.rfft(field, n=2 * G, axis=2)
            convolved = jnp.fft.irfft(field_fft * kernel_fft[None, :, :, None], n=2 * G, axis=2)[:, :, :G, :]
            coupling = jax.nn.softmax(field_coupling, axis=-1)
            field_c = jnp.einsum('ij,bjgd->bigd', coupling, convolved)
            gathered = field_c[:, :, idx_lo, :] * w_lo + field_c[:, :, idx_hi, :] * w_hi
            wave_output = q_feat * gathered
            gate = jax.nn.sigmoid(gate_raw).reshape(b, n, H, HD).transpose(0, 2, 1, 3)
            output = (wave_output * gate).transpose(0, 2, 1, 3).reshape(b, n, d)
            return output @ Wout.T + bout
        key = jax.random.key(seed)
        ks = jax.random.split(key, 5)
        x = jax.random.normal(ks[0], (B, N, D), jnp.float32)
        Wqkvg = jax.random.normal(ks[1], (4 * D, D), jnp.float32) * 0.02
        Wqkvg = Wqkvg.at[3 * D:].set(0.0)
        bqkvg = jnp.concatenate([jnp.zeros(3 * D, jnp.float32), jnp.full((D,), 2.0, jnp.float32)])
        wave_frequency = jnp.linspace(0.3, 4.0, H, dtype=jnp.float32)
        wave_damping = jnp.linspace(-3.0, 0.5, H, dtype=jnp.float32)
        wave_phase = jnp.linspace(0.0, math.pi, H, dtype=jnp.float32)
        field_coupling = jnp.eye(H, dtype=jnp.float32) + jax.random.normal(ks[2], (H, H), jnp.float32) * 0.01
        Wout = jax.random.normal(ks[3], (D, D), jnp.float32) * 0.02
        bout = jnp.zeros(D, jnp.float32)
        return dict(x=x, Wqkvg=Wqkvg, bqkvg=bqkvg, wave_frequency=wave_frequency, wave_damping=wave_damping, wave_phase=wave_phase, field_coupling=field_coupling, Wout=Wout, bout=bout)
    _L1_attn_all = _L1_attn_setup()
    _L1_attn_in = {k: v for k, v in _L1_attn_all.items() if k in ('Wqkvg', 'bqkvg', 'wave_frequency', 'wave_damping', 'wave_phase', 'field_coupling', 'Wout', 'bout')}
    del _L1_attn_all

    def _L1_ffn_setup():
        import jax, jax.numpy as jnp
        import numpy as np
        DIM = 256
        HIDDEN = 768
        SCALE = 1.0 / 127.0

        def _dequant(w_int, dtype):
            return w_int.astype(dtype) * jnp.asarray(SCALE, dtype)
        key = jax.random.key(seed)
        k_x, k_g, k_u, k_d = jax.random.split(key, 4)
        x = jax.random.normal(k_x, (4, 512, DIM), dtype=jnp.float32)
        w_gate = jax.random.randint(k_g, (HIDDEN, DIM), -127, 128, dtype=jnp.int32)
        w_up = jax.random.randint(k_u, (HIDDEN, DIM), -127, 128, dtype=jnp.int32)
        w_down = jax.random.randint(k_d, (DIM, HIDDEN), -127, 128, dtype=jnp.int32)
        return {'x': x, 'w_gate': w_gate, 'w_up': w_up, 'w_down': w_down}
    _L1_ffn_all = _L1_ffn_setup()
    _L1_ffn_in = {k: v for k, v in _L1_ffn_all.items() if k in ('w_gate', 'w_up', 'w_down')}
    del _L1_ffn_all
    return {'x': x, 'txt': txt, 'L0_tok_Wp': _L0_tok_in['Wp'], 'L0_tok_b': _L0_tok_in['b'], 'L0_attn_w_down_q': _L0_attn_in['w_down_q'], 'L0_attn_w_down_kv': _L0_attn_in['w_down_kv'], 'L0_attn_w_up_q': _L0_attn_in['w_up_q'], 'L0_attn_w_up_k': _L0_attn_in['w_up_k'], 'L0_attn_w_up_v': _L0_attn_in['w_up_v'], 'L0_attn_w_out': _L0_attn_in['w_out'], 'L0_attn_ln_scale': _L0_attn_in['ln_scale'], 'L0_attn_ln_bias': _L0_attn_in['ln_bias'], 'L0_ffn_ln1_g': _L0_ffn_in['ln1_g'], 'L0_ffn_ln1_b': _L0_ffn_in['ln1_b'], 'L0_ffn_ln2_g': _L0_ffn_in['ln2_g'], 'L0_ffn_ln2_b': _L0_ffn_in['ln2_b'], 'L0_ffn_Wq': _L0_ffn_in['Wq'], 'L0_ffn_bq': _L0_ffn_in['bq'], 'L0_ffn_Wk': _L0_ffn_in['Wk'], 'L0_ffn_bk': _L0_ffn_in['bk'], 'L0_ffn_Wv': _L0_ffn_in['Wv'], 'L0_ffn_bv': _L0_ffn_in['bv'], 'L0_ffn_Wp': _L0_ffn_in['Wp'], 'L0_ffn_bp': _L0_ffn_in['bp'], 'L0_ffn_gate_W': _L0_ffn_in['gate_W'], 'L0_ffn_gate_b': _L0_ffn_in['gate_b'], 'L0_ffn_exp_W1': _L0_ffn_in['exp_W1'], 'L0_ffn_exp_b1': _L0_ffn_in['exp_b1'], 'L0_ffn_exp_W2': _L0_ffn_in['exp_W2'], 'L0_ffn_exp_b2': _L0_ffn_in['exp_b2'], 'L1_attn_Wqkvg': _L1_attn_in['Wqkvg'], 'L1_attn_bqkvg': _L1_attn_in['bqkvg'], 'L1_attn_wave_frequency': _L1_attn_in['wave_frequency'], 'L1_attn_wave_damping': _L1_attn_in['wave_damping'], 'L1_attn_wave_phase': _L1_attn_in['wave_phase'], 'L1_attn_field_coupling': _L1_attn_in['field_coupling'], 'L1_attn_Wout': _L1_attn_in['Wout'], 'L1_attn_bout': _L1_attn_in['bout'], 'L1_ffn_w_gate': _L1_ffn_in['w_gate'], 'L1_ffn_w_up': _L1_ffn_in['w_up'], 'L1_ffn_w_down': _L1_ffn_in['w_down']}

def reference(x, txt, L0_tok_Wp, L0_tok_b, L0_attn_w_down_q, L0_attn_w_down_kv, L0_attn_w_up_q, L0_attn_w_up_k, L0_attn_w_up_v, L0_attn_w_out, L0_attn_ln_scale, L0_attn_ln_bias, L0_ffn_ln1_g, L0_ffn_ln1_b, L0_ffn_ln2_g, L0_ffn_ln2_b, L0_ffn_Wq, L0_ffn_bq, L0_ffn_Wk, L0_ffn_bk, L0_ffn_Wv, L0_ffn_bv, L0_ffn_Wp, L0_ffn_bp, L0_ffn_gate_W, L0_ffn_gate_b, L0_ffn_exp_W1, L0_ffn_exp_b1, L0_ffn_exp_W2, L0_ffn_exp_b2, L1_attn_Wqkvg, L1_attn_bqkvg, L1_attn_wave_frequency, L1_attn_wave_damping, L1_attn_wave_phase, L1_attn_field_coupling, L1_attn_Wout, L1_attn_bout, L1_ffn_w_gate, L1_ffn_w_up, L1_ffn_w_down):
    import jax
    import jax.numpy as jnp

    def _L0_tok_ref(x, Wp, b):
        import jax, jax.numpy as jnp
        import numpy as np
        IMG_H = 128
        IMG_W = 128
        C = 3
        PH = 16
        PW = 16
        HID = 256
        NH = IMG_H // PH
        NW = IMG_W // PW
        PD = C * PH * PW
        BATCH = 64

        def sinusoidal_pos_embed(embed_dim, grid_size_x, grid_size_y):
            gh = jnp.arange(grid_size_y)
            gw = jnp.arange(grid_size_x)
            grid = jnp.stack(jnp.meshgrid(gh, gw, indexing='ij'), axis=0)
            h_pos = grid[0].reshape(-1).astype(jnp.float32)
            w_pos = grid[1].reshape(-1).astype(jnp.float32)
            quarter = embed_dim // 4
            factor = 10000.0 ** (jnp.arange(quarter, dtype=jnp.float32) / quarter)
            h = h_pos[:, None] / factor
            w = w_pos[:, None] / factor
            return jnp.concatenate([jnp.sin(h), jnp.cos(h), jnp.sin(w), jnp.cos(w)], axis=-1)
        B = x.shape[0]
        p = x.reshape(B, C, NH, PH, NW, PW)
        p = p.transpose(0, 2, 4, 3, 5, 1)
        p = p.reshape(B, NH * NW, PH * PW * C)
        out = jnp.einsum('bnd,hd->bnh', p, Wp) + b
        pos = sinusoidal_pos_embed(HID, NW, NH)
        return out + pos

    def _L0_attn_ref(x, w_down_q, w_down_kv, w_up_q, w_up_k, w_up_v, w_out, ln_scale, ln_bias):
        import jax, jax.numpy as jnp
        import numpy as np
        B, S, D = (2, 512, 256)
        H, DH = (16, 64)
        DQL, DKVL = (128, 128)
        DR = 64
        TOPK = 64
        LN_EPS = 1e-05
        ROPE_BASE = 10000.0

        def _rope_tables(seq_len, dim):
            inv_freq = 1.0 / ROPE_BASE ** (np.arange(0, dim, 2, dtype=np.float32) / dim)
            t = np.arange(seq_len, dtype=np.float32)
            freqs = np.outer(t, inv_freq)
            cos = np.concatenate([np.cos(freqs), np.cos(freqs)], -1)[:, ::2]
            sin = np.concatenate([np.sin(freqs), np.sin(freqs)], -1)[:, ::2]
            return (jnp.asarray(cos), jnp.asarray(sin))

        def _apply_rope_subspace(x, d_rope):
            s = x.shape[-2]
            cos, sin = _rope_tables(s, d_rope)
            xr, xp = (x[..., :d_rope], x[..., d_rope:])
            e, o = (xr[..., 0::2], xr[..., 1::2])
            rot = jnp.stack([e * cos - o * sin, e * sin + o * cos], axis=-1).reshape(xr.shape)
            return jnp.concatenate([rot, xp], axis=-1)

        def _reference_tuple_inner(x, w_down_q, w_down_kv, w_up_q, w_up_k, w_up_v, w_out, ln_scale, ln_bias):
            b, s, d = x.shape
            residual = x
            mu = jnp.mean(x, axis=-1, keepdims=True)
            var = jnp.mean((x - mu) ** 2, axis=-1, keepdims=True)
            h = (x - mu) * jax.lax.rsqrt(var + LN_EPS) * ln_scale + ln_bias
            c_q = h @ w_down_q.T
            c_kv = h @ w_down_kv.T
            q = (c_q @ w_up_q.T).reshape(b, s, H, DH).transpose(0, 2, 1, 3)
            k = (c_kv @ w_up_k.T).reshape(b, s, H, DH).transpose(0, 2, 1, 3)
            v = (c_kv @ w_up_v.T).reshape(b, s, H, DH).transpose(0, 2, 1, 3)
            q = _apply_rope_subspace(q, DR)
            k = _apply_rope_subspace(k, DR)
            scale = 1.0 / np.sqrt(DH).astype(np.float32)
            scores = jnp.einsum('bhqd,bhkd->bhqk', q, k) * scale
            _, indices = jax.lax.top_k(scores, min(TOPK, s))
            attn = jax.nn.softmax(scores, axis=-1)
            out = jnp.einsum('bhqk,bhkd->bhqd', attn, v)
            out = out.transpose(0, 2, 1, 3).reshape(b, s, H * DH)
            out = out @ w_out.T + residual
            return (out, indices.astype(jnp.int64))
        return _reference_tuple_inner(x, w_down_q, w_down_kv, w_up_q, w_up_k, w_up_v, w_out, ln_scale, ln_bias)[0]

    def _L0_ffn_ref(x, ln1_g, ln1_b, ln2_g, ln2_b, Wq, bq, Wk, bk, Wv, bv, Wp, bp, gate_W, gate_b, exp_W1, exp_b1, exp_W2, exp_b2):
        import jax, jax.numpy as jnp
        import numpy as np
        N_HEAD = 16
        NUM_EXPERTS = 8
        TOP_K = 2
        LN_EPS = 1e-05

        def _layernorm(x, g, b):
            mu = jnp.mean(x, axis=-1, keepdims=True)
            var = jnp.mean(jnp.square(x - mu), axis=-1, keepdims=True)
            return (x - mu) * jax.lax.rsqrt(var + LN_EPS) * g + b

        def _attention(h, Wq, bq, Wk, bk, Wv, bv, Wp, bp):
            B, T, D = h.shape
            hd = D // N_HEAD

            def split(z):
                return z.reshape(B, T, N_HEAD, hd).transpose(0, 2, 1, 3)
            q = split(h @ Wq + bq)
            k = split(h @ Wk + bk)
            v = split(h @ Wv + bv)
            att = jnp.einsum('bhqd,bhkd->bhqk', q, k) / jnp.sqrt(jnp.float32(hd))
            causal = jnp.tril(jnp.ones((T, T), bool))
            att = jnp.where(causal, att, -jnp.inf)
            att = jax.nn.softmax(att, axis=-1)
            y = jnp.einsum('bhqk,bhkd->bhqd', att, v)
            y = y.transpose(0, 2, 1, 3).reshape(B, T, D)
            return y @ Wp + bp

        def _token_moe(h, gate_W, gate_b, exp_W1, exp_b1, exp_W2, exp_b2):
            B, T, D = h.shape
            flat = h.reshape(-1, D)
            N = flat.shape[0]
            logits = flat @ gate_W + gate_b
            top_v, top_i = jax.lax.top_k(logits, TOP_K)
            w = jax.nn.softmax(top_v, axis=-1)
            w_full = jnp.zeros((N, NUM_EXPERTS), flat.dtype)
            w_full = w_full.at[jnp.arange(N)[:, None], top_i].add(w)
            out = jnp.zeros_like(flat)
            for e in range(NUM_EXPERTS):
                mid = jax.nn.gelu(flat @ exp_W1[e] + exp_b1[e], approximate=False)
                y_e = mid @ exp_W2[e] + exp_b2[e]
                out = out + w_full[:, e:e + 1] * y_e
            return out.reshape(B, T, D)
        x = x + _attention(_layernorm(x, ln1_g, ln1_b), Wq, bq, Wk, bk, Wv, bv, Wp, bp)
        x = x + _token_moe(_layernorm(x, ln2_g, ln2_b), gate_W, gate_b, exp_W1, exp_b1, exp_W2, exp_b2)
        return x

    def _L1_attn_ref(x, Wqkvg, bqkvg, wave_frequency, wave_damping, wave_phase, field_coupling, Wout, bout):
        import jax, jax.numpy as jnp
        import numpy as np
        import math
        B, N, D, H, G = (4, 512, 256, 16, 512)
        HD = D // H
        MAX_SEQ = 512
        STRIDE = (G - 1) / max(MAX_SEQ - 1, 1)

        def _forward(x, Wqkvg, bqkvg, wave_frequency, wave_damping, wave_phase, field_coupling, Wout, bout):
            b, n, d = x.shape
            qkvg = x @ Wqkvg.T + bqkvg
            q, k, v, gate_raw = jnp.split(qkvg, 4, axis=-1)
            to_heads = lambda t: t.reshape(b, n, H, HD).transpose(0, 2, 1, 3)
            q, k, v = (to_heads(q), to_heads(k), to_heads(v))
            seq_pos = jnp.arange(n, dtype=jnp.float32)
            field_pos = jnp.clip(seq_pos * STRIDE, 0.0, G - 2)
            idx_lo = jnp.clip(field_pos.astype(jnp.int32), 0, G - 2)
            idx_hi = idx_lo + 1
            frac = jnp.clip(field_pos - idx_lo.astype(jnp.float32), 0.0, 1.0)
            w_lo = (1.0 - frac)[None, None, :, None]
            w_hi = frac[None, None, :, None]
            q_feat = jax.nn.elu(q) + 1.0
            k_feat = jax.nn.elu(k) + 1.0
            deposit = k_feat * v
            field = jnp.zeros((b, H, G, HD), deposit.dtype)
            field = field.at[:, :, idx_lo, :].add(deposit * w_lo)
            field = field.at[:, :, idx_hi, :].add(deposit * w_hi)
            t = jnp.arange(G, dtype=jnp.float32)
            alpha = jax.nn.softplus(wave_damping)[:, None]
            omega = wave_frequency[:, None]
            phi = wave_phase[:, None]
            kernels = jnp.exp(-alpha * t[None, :]) * jnp.cos(omega * t[None, :] + phi)
            kernels = kernels / jnp.clip(jnp.sum(jnp.abs(kernels), axis=1, keepdims=True), 1e-08)
            kernel_fft = jnp.fft.rfft(kernels, n=2 * G, axis=-1)
            field_fft = jnp.fft.rfft(field, n=2 * G, axis=2)
            convolved = jnp.fft.irfft(field_fft * kernel_fft[None, :, :, None], n=2 * G, axis=2)[:, :, :G, :]
            coupling = jax.nn.softmax(field_coupling, axis=-1)
            field_c = jnp.einsum('ij,bjgd->bigd', coupling, convolved)
            gathered = field_c[:, :, idx_lo, :] * w_lo + field_c[:, :, idx_hi, :] * w_hi
            wave_output = q_feat * gathered
            gate = jax.nn.sigmoid(gate_raw).reshape(b, n, H, HD).transpose(0, 2, 1, 3)
            output = (wave_output * gate).transpose(0, 2, 1, 3).reshape(b, n, d)
            return output @ Wout.T + bout
        return _forward(x, Wqkvg, bqkvg, wave_frequency, wave_damping, wave_phase, field_coupling, Wout, bout)

    def _L1_ffn_ref(x, w_gate, w_up, w_down):
        import jax, jax.numpy as jnp
        import numpy as np
        DIM = 256
        HIDDEN = 768
        SCALE = 1.0 / 127.0

        def _dequant(w_int, dtype):
            return w_int.astype(dtype) * jnp.asarray(SCALE, dtype)
        wg = _dequant(w_gate, x.dtype)
        wu = _dequant(w_up, x.dtype)
        wd = _dequant(w_down, x.dtype)
        gate = jnp.einsum('bsd,hd->bsh', x, wg)
        up = jnp.einsum('bsd,hd->bsh', x, wu)
        h = jax.nn.silu(gate) * up
        return jnp.einsum('bsh,dh->bsd', h, wd)
    h = _L0_tok_ref(x, L0_tok_Wp, L0_tok_b)
    h = jnp.concatenate([h, txt], axis=1)
    h = h + _L0_attn_ref(_layernorm(h, axis=-1), L0_attn_w_down_q, L0_attn_w_down_kv, L0_attn_w_up_q, L0_attn_w_up_k, L0_attn_w_up_v, L0_attn_w_out, L0_attn_ln_scale, L0_attn_ln_bias)
    h = h + _L0_ffn_ref(_layernorm(h, axis=-1), L0_ffn_ln1_g, L0_ffn_ln1_b, L0_ffn_ln2_g, L0_ffn_ln2_b, L0_ffn_Wq, L0_ffn_bq, L0_ffn_Wk, L0_ffn_bk, L0_ffn_Wv, L0_ffn_bv, L0_ffn_Wp, L0_ffn_bp, L0_ffn_gate_W, L0_ffn_gate_b, L0_ffn_exp_W1, L0_ffn_exp_b1, L0_ffn_exp_W2, L0_ffn_exp_b2)
    h = h + _L1_attn_ref(_layernorm(h, axis=-1), L1_attn_Wqkvg, L1_attn_bqkvg, L1_attn_wave_frequency, L1_attn_wave_damping, L1_attn_wave_phase, L1_attn_field_coupling, L1_attn_Wout, L1_attn_bout)
    h = h + _L1_ffn_ref(_layernorm(h, axis=-1), L1_ffn_w_gate, L1_ffn_w_up, L1_ffn_w_down)
    return h

_drawn_inputs = setup_inputs


def setup_inputs(seed=0):
    import zlib

    import numpy as np

    out = dict(_drawn_inputs(seed))
    spreads = {'L0_tok_b': (0.0, 0.1),
     'L0_attn_ln_scale': (1.0, 0.6),
     'L0_attn_ln_bias': (0.0, 0.8),
     'L0_ffn_ln1_g': (1.0, 0.6),
     'L0_ffn_ln1_b': (0.0, 2.0),
     'L0_ffn_ln2_g': (1.0, 0.6),
     'L0_ffn_ln2_b': (0.0, 2.0),
     'L0_ffn_bq': (0.0, 2.0),
     'L0_ffn_bk': (0.0, 2.0),
     'L0_ffn_bv': (0.0, 1.663),
     'L0_ffn_bp': (0.0, 0.485),
     'L0_ffn_gate_b': (0.0, 0.538),
     'L0_ffn_exp_b1': (0.0, 1.908),
     'L0_ffn_exp_b2': (0.0, 0.671),
     'L1_attn_bout': (0.0, 0.8)}
    factors = {'L0_attn_w_down_q': 8.0,
     'L0_attn_w_down_kv': 5.253,
     'L0_attn_w_up_q': 8.0,
     'L0_attn_w_up_k': 8.0,
     'L0_attn_w_up_v': 5.553,
     'L0_attn_w_out': 5.509,
     'L0_ffn_Wq': 26.472,
     'L0_ffn_Wk': 26.089,
     'L1_attn_Wqkvg': 8.0,
     'L1_attn_bqkvg': 8.0,
     'L1_attn_wave_frequency': 8.0,
     'L1_attn_wave_damping': 8.0,
     'L1_attn_wave_phase': 8.0,
     'L1_attn_field_coupling': 8.0,
     'L1_attn_Wout': 8.0,
     'L0_ffn_exp_W1': 3.045}
    for name, (base, spread) in spreads.items():
        noise = np.random.default_rng([zlib.crc32(name.encode()), seed]).standard_normal(out[name].shape)
        drawn = base * np.exp(spread * noise) if base else spread * noise
        out[name] = jnp.asarray(drawn.astype(out[name].dtype))
    for name, factor in factors.items():
        out[name] = (out[name] * factor).astype(out[name].dtype)
    return out
```

```python
from contextlib import ExitStack

import numpy as np
import concourse.bass as bass
from concourse import mybir

F32 = mybir.dt.float32
BF16 = mybir.dt.bfloat16
I32 = mybir.dt.int32
U32 = mybir.dt.uint32
ALU = mybir.AluOpType
ACT = mybir.ActivationFunctionType
AX_X = mybir.AxisListType.X

P = 128
B = 32
T = 96
IMG = 64
TXT = 32
D = 256
KD = D // P
GB = 4
G = B // GB
GT = GB * T
PATCH = 768
KP = PATCH // P
NH = 16
DH = 64
NCH = NH // 2
DM = 16
HC = P // DM
E = 8
HID = 1024
KH = HID // P
EPS = 1e-5
TOPK = 2
CAP = B * T
TILES = B * T * TOPK // P + E
LIST = (E * CAP + TILES * P + P - 1) // P * P
FFN = 768
KF = FFN // P
FIELD = 512
NEG = -1e30
RING = 4


BIG = 2 * B * D + KD * B * T
PERM = 2700
ARENA = 53200


class Space:

    def __init__(self, arena, at, end):
        self.arena, self.at, self.end = arena, at, end

    def take(self, shape, dt=F32):
        words = int(np.prod(shape[1:]))
        if dt == BF16:
            assert words % 2 == 0
            words //= 2
        v = self.arena[0:shape[0], self.at:self.at + words]
        self.at += words
        assert self.at <= self.end, (self.at, self.end)
        if dt != F32:
            v = v.bitcast(dt)
        if len(shape) > 2:
            names = "abcd"[:len(shape) - 1]
            v = v.rearrange(f"p ({' '.join(names)}) -> p {' '.join(names)}",
                            **{n: k for n, k in zip(names, shape[1:])})
        return v


class Ring:

    def __init__(self, banks, filled, drained, base, per_group, gap=None, late=2, groups=G):
        self.groups = groups
        self.banks, self.filled, self.drained, self.base = banks, filled, drained, base
        self.n, self.per_group, self.gap, self.late = len(banks), per_group, gap, late
        assert per_group % self.n == 0 and late % self.n == 0 or gap is None
        assert gap is None or gap % self.n == 0

    def before(self, g, m, at_end=False):
        late = self.gap is not None and not (isinstance(g, int) and g == 0 and m < self.gap)
        count = self.base[m % self.n] + (self.per_group // self.n) * g + m // self.n - (self.late // self.n if late else 0)
        return count - (self.gap // self.n if at_end else 0)

    def bank(self, m):
        return self.banks[m % self.n]

    def wait_free(self, eng, g, m, at_end=False):
        eng.wait_ge(self.drained[m % self.n], self.before(g, m, at_end))

    def wait_filled(self, eng, g, m, at_end=False):
        if m < 0 and isinstance(g, int) and g == 0:
            return
        eng.wait_ge(self.filled[m % self.n], self.before(g, m, at_end) + 1)

    def fill(self, ins, m):
        ins.then_inc(self.filled[m % self.n], 1)

    def drain(self, ins, m):
        ins.then_inc(self.drained[m % self.n], 1)

    def end(self):
        return [x + (self.per_group // self.n) * self.groups for x in self.base]


def program(nc, a, out, upto=9):
    top = ExitStack()
    with top:
        arena = top.enter_context(nc.sbuf_tensor("arena", [P, ARENA], F32))

        def sem(name):
            return top.enter_context(nc.semaphore(name))

        banks = [top.enter_context(nc.psum_tensor(f"bank{i}", [P, 512], F32)) for i in range(8)]
        filled = [sem(f"filled{i}") for i in range(8)]
        drained = [sem(f"drained{i}") for i in range(8)]
        count = [0] * 8

        def ring(first, n, per_group, gap=None, late=2, groups=G):
            ids = range(first, first + n)
            r = Ring([banks[i] for i in ids], [filled[i] for i in ids], [drained[i] for i in ids],
                     [count[i] for i in ids], per_group, gap, late, groups)
            for i, c in zip(ids, r.end()):
                count[i] = c
            return r

        big = Space(arena, 0, BIG)
        perm = Space(arena, BIG, BIG + PERM)
        h = big.take([T, G, GB, D])
        xres = big.take([T, G, GB, D])
        hnT = big.take([P, KD, G, GT])
        ident = perm.take([P, P])
        pows = perm.take([T, 3, GB])
        lnT = perm.take([P, KD, GT])
        zz = perm.take([T, GB, D])
        stats = perm.take([T, GB, 6])
        mv = perm.take([T, GB, 2])
        lnw = perm.take([T, 7, GB])
        gb = perm.take([P, 3, 2, KD])

        ln_stat, ln_mean, ln_chain, ln_row, ln_added = (
            sem(n) for n in ("ln_stat", "ln_mean", "ln_chain", "ln_row", "ln_added"))
        ln_out, ln_stored = sem("ln_out"), sem("ln_stored")
        ln_turn, dma_turn, load_turn = (sem(n) for n in ("ln_turn", "dma_turn", "load_turn"))
        const_ready = sem("const_ready")
        made = sem("made")
        out_stored = sem("out_stored")

        ACTS = {"first": (0, True, h), "second": (1, True, h), "third": (2, False, xres)}

        CH = 7

        def ln_vector_stats(src, g, l):
            nc.vector.sem_inc(ln_turn, 1)
            for b in range(GB):
                last = nc.vector.bn_stats(stats[:, b, :], src[:, g, b, :])
            last.then_inc(ln_stat, 1)

        def ln_vector_mean(v, l):
            v.wait_ge(ln_stat, l + 1)
            if not (isinstance(l, int) and l == 0):
                v.wait_ge(ln_chain, CH * l)
            v.sem_inc(ln_turn, 1)
            for b in range(GB):
                last = nc.vector.bn_aggr(mv[:, b, :], stats[:, b, :])
            last.then_inc(ln_mean, 1)

        def ln_pool_rstd(pool, l):
            gp = nc.gpsimd
            var = mv[:, :, 1]
            pool.wait_ge(ln_mean, l + 1)
            pool.wait_ge(ln_row, l)
            w = lnw

            def step(k, ins):
                ins.then_inc(ln_chain, 1)
                pool.wait_ge(ln_chain, CH * l + k)
            step(1, gp.tensor_tensor(w[:, 0, :], var, pows[:, 2, :], ALU.add))
            step(2, gp.tensor_tensor(w[:, 1, :], w[:, 0, :], pows[:, 0, :], ALU.pow))
            step(3, gp.tensor_tensor(w[:, 2, :], w[:, 0, :], pows[:, 1, :], ALU.pow))
            step(4, gp.tensor_tensor(w[:, 3, :], var, w[:, 2, :], ALU.mult))
            step(5, gp.tensor_tensor(w[:, 4, :], w[:, 3, :], pows[:, 2, :], ALU.add))
            step(6, gp.tensor_tensor(w[:, 5, :], w[:, 4, :], pows[:, 0, :], ALU.pow))
            gp.tensor_tensor(w[:, 6, :], w[:, 1, :], w[:, 5, :], ALU.mult).then_inc(ln_chain, 1)

        def ln_vector_rows(v, src, twice, g, l, t_ring, m, at_end=False):
            v.wait_ge(ln_chain, CH * l + CH)
            if not (isinstance(l, int) and l == 0):
                v.wait_ge(ln_out, 2 * l)
            v.wait_ge(ln_added, l)
            for b in range(GB):
                if twice:
                    nc.vector.tensor_scalar(xres[:, g, b, :], src[:, g, b, :], mv[:, b, 0:1], lnw[:, 1, b:b + 1],
                                            ALU.subtract, ALU.mult)
                r = lnw[:, 6 if twice else 1, b:b + 1]
                last = nc.vector.tensor_scalar(zz[:, b, :], src[:, g, b, :], mv[:, b, 0:1], r,
                                               ALU.subtract, ALU.mult)
            last.then_inc(ln_row, 1)

        def ln_pool_add(pool, add, g, l):
            pool.wait_ge(ln_row, l + 1)
            if add:
                nc.gpsimd.tensor_tensor(h[:, g, :, :], h[:, g, :, :], xres[:, g, :, :], ALU.add).then_inc(ln_added, 1)
            else:
                pool.sem_inc(ln_added, 1)

        def ln_tensor(pe, r, g, l, m, at_end=False):
            pe.wait_ge(ln_row, l + 1)
            for k in range(KD):
                r.wait_free(pe, g, m + k, at_end)
                for b in range(GB):
                    last = nc.tensor.transpose(r.bank(m + k)[:, b * T:(b + 1) * T], zz[:, b, k * P:(k + 1) * P],
                                               ident[0:T, 0:T])
                r.fill(last, m + k)

        def ln_scalar(act, r, g, l, m, which, dst_g, at_end=False):
            if not (isinstance(l, int) and l == 0):
                act.wait_ge(ln_stored, 16 * l)
            for k in range(KD):
                r.wait_filled(act, g, m + k, at_end)
                if which is None:
                    ins = nc.scalar.activation(lnT[:, k, :], r.bank(m + k)[:, 0:GT], ACT.Identity)
                else:
                    ins = nc.scalar.activation(lnT[:, k, :], r.bank(m + k)[:, 0:GT], ACT.Identity,
                                               bias=gb[:, which, 1, k:k + 1], scale=gb[:, which, 0, k:k + 1])
                r.drain(ins, m + k)
                act.wait_ge(r.drained[(m + k) % r.n], r.before(g, m + k, at_end) + 1)
                act.sem_inc(ln_out, 1)
            act.dma_start(hnT[:, :, dst_g, :], lnT[:]).then_inc(ln_stored, 16)

        with ExitStack() as ph:
            work = Space(arena, BIG + PERM, ARENA)
            wpT = work.take([P, KP, D])
            posb = work.take([P, D])
            tokb = work.take([P, D])
            patches = work.take([P, 2, KP, GB * IMG])
            x_loaded = [sem(f"x_loaded{i}") for i in range(2)]
            tok_rows = sem("tok_rows")
            r = ring(0, 4, 4)
            block = nc.Block()
            with block:
                @block.sync
                def _(sp):
                    for n, (dst, src) in enumerate([
                            (wpT, "wpT"), (posb, "pos2"), (tokb, "tokb"), (ident, "ident"), (gb, "gb")]):
                        src = a[src]
                        sp.dma_start(dst[:], src).then_inc(const_ready, 16)
                    sp.dma_start(h[IMG:T].rearrange("p g b d -> p (g b) d"), a["txt"]).then_inc(const_ready, 16)
                    with sp.Fori(0, G // 2) as i:
                        for s in range(2):
                            sp.wait_ge(filled[1], 2 * i)
                            sp.dma_start(patches[:, s], a["patches"][2 * i + s]).then_inc(x_loaded[s], 16)

                @block.tensor
                def _(pe):
                    pe.wait_ge(const_ready, 96)
                    with pe.Fori(0, G // 2) as i:
                        for s in range(2):
                            g = 2 * i + s
                            pe.wait_ge(x_loaded[s], 16 * i + 16)
                            for p in range(2):
                                r.wait_free(pe, g, p)
                                for k in range(KP):
                                    last = nc.tensor.matmul(r.bank(p)[:, 0:D], patches[:, s, k, p * P:(p + 1) * P],
                                                            wpT[:, k, :], start=(k == 0), stop=(k == KP - 1))
                                r.fill(last, p)
                        for s in range(2):
                            g = 2 * i + s
                            ln_tensor(pe, r, g, g, 2)

                @block.vector
                def _(v):
                    v.wait_ge(const_ready, 96)
                    nc.vector.memset(pows[:, 0, :], -0.5)
                    nc.vector.memset(pows[:, 2, :], EPS)
                    nc.vector.memset(pows[:, 1, :], -1.0).then_inc(made, 1)
                    nc.vector.tensor_tensor(posb[:], posb[:], tokb[:], ALU.add).then_inc(made, 1)
                    v.wait_ge(made, 2)
                    with v.Fori(0, G // 2) as i:
                        for s in range(2):
                            g = 2 * i + s
                            for p in range(2):
                                r.wait_filled(v, g, p)
                                for j in range(2):
                                    rows = slice(j * IMG, (j + 1) * IMG)
                                    last = nc.vector.tensor_tensor(h[0:IMG, g, 2 * p + j, :], r.bank(p)[rows, 0:D],
                                                                   posb[rows, :], ALU.add)
                                r.drain(last, p)
                            v.wait_ge(r.drained[1], r.before(g, 1) + 1)
                            ln_vector_stats(h, g, g)
                            ln_vector_mean(v, g)
                            ln_vector_rows(v, h, True, g, g, r, 2)

                @block.gpsimd
                def _(pool):
                    pool.wait_ge(made, 1)
                    with pool.Fori(0, G) as g:
                        ln_pool_rstd(pool, g)
                        ln_pool_add(pool, True, g, g)

                @block.scalar
                def _(act):
                    act.wait_ge(const_ready, 96)
                    with act.Fori(0, G) as g:
                        ln_scalar(act, r, g, g, 2, 0, g)
                    act.wait_ge(ln_stored, 16 * G)

        att_max, att_shift, att_exp, att_sum, att_inv, att_norm, att_T = (
            sem(n) for n in ("att_max", "att_shift", "att_exp", "att_sum", "att_inv", "att_norm", "att_T"))
        both = Space(arena, BIG + PERM, ARENA)
        prob = both.take([T, RING, GB, T])
        probT = both.take([T, RING, GT])
        mx = both.take([T, RING, GB])
        sm = both.take([T, RING, GB])
        inv = both.take([T, RING, GB])

        def attention_vector_shift(v, rs, rt, seq, g, n, t_item):
            s = n % RING
            rs.wait_filled(v, g, n)
            sc = rs.bank(n)[0:T, 0:GT].rearrange("p (b k) -> p b k", b=GB)
            nc.vector.tensor_reduce(mx[:, s, :], sc, AX_X, ALU.max).then_inc(att_max, 1)
            v.wait_ge(att_max, seq(g, n) + 1)
            rt.wait_filled(v, g, t_item(n - RING))
            rs.drain(nc.vector.tensor_tensor(prob[:, s], sc, mx[:, s, :].unsqueeze(2).broadcast_to([T, GB, T]),
                                             ALU.subtract), n)

        def attention_vector_sum(v, seq, g, n):
            s = n % RING
            v.wait_ge(att_exp, seq(g, n) + 1)
            nc.vector.tensor_reduce(sm[:, s, :], prob[:, s], AX_X, ALU.add).then_inc(att_sum, 1)
            v.wait_ge(att_sum, seq(g, n) + 1)
            nc.vector.reciprocal(inv[:, s, :], sm[:, s, :]).then_inc(att_inv, 1)

        def attention_scalar_exp(act, rs, g, n, seq, scale):
            s = n % RING
            act.wait_ge(rs.drained[n % rs.n], rs.before(g, n) + 1)
            nc.scalar.activation(prob[:, s], prob[:, s], ACT.Exp, scale=scale).then_inc(att_exp, 1)

        def attention_pool_norm(pool, seq, g, n):
            s = n % RING
            pool.wait_ge(att_inv, seq(g, n) + 1)
            nc.gpsimd.tensor_tensor(prob[:, s], prob[:, s], inv[:, s, :].unsqueeze(2).broadcast_to([T, GB, T]),
                                    ALU.mult).then_inc(att_norm, 1)

        def attention_tensor_T(pe, rt, seq, g, n, m):
            s = n % RING
            pe.wait_ge(att_norm, seq(g, n) + 1)
            rt.wait_free(pe, g, m)
            for b in range(GB):
                last = nc.tensor.transpose(rt.bank(m)[0:T, b * T:(b + 1) * T], prob[:, s, b, :], ident[0:T, 0:T])
            rt.fill(last, m)

        rows_d = nc.dram_tensor("norm_rows", (B * T, D), F32, kind="Internal").ap()
        h_d = nc.dram_tensor("stream_rows", (G, T, GB * D), F32, kind="Internal").ap()
        list_d = nc.dram_tensor("token_list", (LIST, 1), I32, kind="Internal").ap()
        y_d = nc.dram_tensor("expert_rows", (TILES * P, D), F32, kind="Internal").ap()

        if upto < 1:
            final(nc, sem, h, out)
            return

        wB = {n: both.take([P, KD, D]) for n in ("wq2", "wk2", "wv2", "wp2")}
        bB = both.take([P, 3, KD])
        wB_loaded = sem("wB_loaded")
        with ExitStack() as ph:
            work = Space(arena, both.at, ARENA)
            w = {n: work.take(s) for n, s in (
                ("wdq", [P, KD, P]), ("wdkv", [P, KD, P]), ("wuq", [P, HID]), ("wuqs", [P, HID]),
                ("wuk", [P, HID]), ("wuks", [P, HID]), ("wuv", [P, HID]), ("woT", [P, NCH, D]),
                ("ropeC", [P, T]), ("ropeS", [P, T]))}
            cq = work.take([P, GT])
            ckv = work.take([P, GT])
            V = work.take([T, GB, HID])
            qprod = work.take([P, 2, GT])
            kprod = work.take([P, 2, GT])
            qrot = work.take([P, 2, GT])
            krot = work.take([P, 2, 2, GT])
            oT = work.take([P, NCH, GT])
            w1_loaded, down, v_rows, q_prod, q_rot, k_prod, k_rot, o_cols, h_rows, z_made = (
                sem(n) for n in ("w1_loaded", "down", "v_rows", "q_prod", "q_rot", "k_prod", "k_rot", "o_cols",
                                 "h_rows", "z_made"))
            STEPS = NH
            LT, LAV = 2, 3
            LN_STEP = 8
            LN_M = 2 + 8 + 4 + 2 * LN_STEP
            N1 = LN_M + 2 + 4 * NCH - 4 - 2 * LN_STEP + 2
            rp = ring(0, 2, N1, LN_M)
            rs = ring(2, 2, NH)
            rt = ring(4, 2, NH)
            rv = ring(6, 2, NCH)

            def proj_m(c, i):
                m = 10 + 4 * c + i
                return m if m < LN_M else m + 2

            def seq(g, n):
                return NH * g + n

            def item(n):
                return n

            block = nc.Block()
            with block:
                @block.sync
                def _(sp):
                    for n in w:
                        sp.dma_start(w[n][:], a[n]).then_inc(w1_loaded, 16)
                    for n in wB:
                        sp.dma_start(wB[n][:], a[n]).then_inc(wB_loaded, 16)
                    sp.dma_start(bB[:], a["bB"]).then_inc(wB_loaded, 16)
                    sp.wait_ge(w1_loaded, 16 * len(w))
                    sp.wait_ge(wB_loaded, 16 * len(wB) + 16)

                @block.tensor
                def _(pe):
                    def proj(g, c, i):
                        m = proj_m(c, i)
                        rp.wait_free(pe, g, m)
                        lhsT = w[("wuq", "wuqs", "wuk", "wuks")[i]][:, c * P:(c + 1) * P]
                        rp.fill(nc.tensor.matmul(rp.bank(m)[:, 0:GT], lhsT, (cq, cq, ckv, ckv)[i][:],
                                                 start=True, stop=True), m)

                    def scores(g, n):
                        c, hh = n // 2, n % 2
                        if hh == 0:
                            pe.wait_ge(q_rot, NCH * g + c + 1)
                            pe.wait_ge(k_rot, NCH * g + c + 1)
                        rs.wait_free(pe, g, n)
                        for b in range(GB):
                            cols = slice(b * T, (b + 1) * T)
                            last = nc.tensor.matmul(rs.bank(n)[0:T, cols], qrot[:, c % 2, cols],
                                                    krot[:, c % 2, hh, cols], start=True, stop=True)
                        rs.fill(last, n)

                    def values(g, c):
                        rv.wait_free(pe, g, c)
                        pe.wait_ge(att_T, seq(g, 2 * c + 1) + 1)
                        for hh in range(2):
                            n = 2 * c + hh
                            for b in range(GB):
                                last = nc.tensor.matmul(
                                    rv.bank(c)[hh * DH:(hh + 1) * DH, b * T:(b + 1) * T],
                                    V[:, b, n * DH:(n + 1) * DH], probT[:, n % RING, b * T:(b + 1) * T],
                                    start=True, stop=True)
                        rv.fill(last, c)

                    def body(g, norm):
                        for m, name in enumerate(("wdq", "wdkv")):
                            rp.wait_free(pe, g, m)
                            for k in range(KD):
                                last = nc.tensor.matmul(rp.bank(m)[:, 0:GT], w[name][:, k, :], hnT[:, k, g, :],
                                                        start=(k == 0), stop=(k == KD - 1))
                            rp.fill(last, m)
                        pe.wait_ge(down, 2 * g + 2)
                        for i in range(4):
                            if i < 4:
                                pass
                        for b in range(GB):
                            for f in range(2):
                                m = 2 + 2 * b + f
                                rp.wait_free(pe, g, m)
                                rp.fill(nc.tensor.matmul(rp.bank(m)[0:T, 0:512], ckv[:, b * T:(b + 1) * T],
                                                         w["wuv"][:, f * 512:(f + 1) * 512], start=True, stop=True), m)
                        for i in range(4):
                            proj(g, 0, i)
                        for n in range(NH + LAV + 1):
                            if n == LN_STEP and norm:
                                ln_tensor(pe, rp, g, G + g - 1, LN_M)
                            if n // 2 + 1 < NCH:
                                for i in range(2):
                                    proj(g, n // 2 + 1, 2 * (n % 2) + i)
                            if n < NH:
                                scores(g, n)
                            if 0 <= n - LT < NH:
                                attention_tensor_T(pe, rt, seq, g, n - LT, n - LT)
                            if 0 <= n - LAV < NH and (n - LAV) % 2 == 1:
                                values(g, (n - LAV) // 2)
                        pe.wait_ge(o_cols, NCH * g + NCH)
                        for j in range(2):
                            m = N1 - 2 + j
                            rp.wait_free(pe, g, m)
                            for bb in range(2):
                                b = 2 * j + bb
                                for c in range(NCH):
                                    last = nc.tensor.matmul(rp.bank(m)[0:T, bb * D:(bb + 1) * D],
                                                            oT[:, c, b * T:(b + 1) * T], w["woT"][:, c, :],
                                                            start=(c == 0), stop=(c == NCH - 1))
                            rp.fill(last, m)

                    pe.wait_ge(w1_loaded, 16 * len(w))
                    pe.wait_ge(z_made, 1)
                    body(0, False)
                    with pe.Fori(1, G) as g:
                        body(g, True)
                    ln_tensor(pe, rp, G, 2 * G - 1, LN_M, at_end=True)

                @block.vector
                def _(v):
                    def rope(g, c, i):
                        prod = (qprod, kprod)[i]
                        if i == 0:
                            if not (isinstance(g, int) and g == 0 and c == 0):
                                v.wait_ge(q_rot, NCH * g + c)
                        else:
                            if not (isinstance(g, int) and g == 0 and c == 0):
                                v.wait_ge(k_rot, NCH * g + c)
                        for j, table in enumerate(("ropeC", "ropeS")):
                            m = proj_m(c, 2 * i + j)
                            rp.wait_filled(v, g, m)
                            ins = nc.vector.tensor_tensor(
                                prod[:, j, :].rearrange("p (b t) -> p b t", b=GB),
                                rp.bank(m)[:, 0:GT].rearrange("p (b t) -> p b t", b=GB),
                                w[table][:].unsqueeze(1).broadcast_to([P, GB, T]), ALU.mult)
                            rp.drain(ins, m)
                        m = proj_m(c, 2 * i + 1)
                        if i == 1:
                            for j in range(2):
                                m = proj_m(c, 2 * i + j)
                                v.wait_ge(rp.drained[m % 2], rp.before(g, m) + 1)
                            rs.wait_filled(v, g, 2 * (c - 2) + 1)
                            for hh in range(2):
                                rows = slice(hh * DH, (hh + 1) * DH)
                                last = nc.vector.tensor_tensor(krot[rows, c % 2, hh, :], kprod[rows, 0, :],
                                                               kprod[rows, 1, :], ALU.add)
                            last.then_inc(k_rot, 1)

                    def body(g, norm):
                        rope(g, 0, 0)
                        rope(g, 0, 1)
                        for n in range(NH + 1):
                            if norm and n == 1:
                                ln_vector_stats(h, g - 1, G + g - 1)
                            if norm and n == 2:
                                ln_vector_mean(v, G + g - 1)
                            if norm and n == 5:
                                ln_vector_rows(v, h, True, g - 1, G + g - 1, rp, LN_M)
                            if n < NH:
                                attention_vector_shift(v, rs, rt, seq, g, n, item)
                            if n // 2 + 1 < NCH:
                                rope(g, n // 2 + 1, n % 2)
                            if n >= 1:
                                attention_vector_sum(v, seq, g, n - 1)
                        for j in range(2):
                            m = N1 - 2 + j
                            rp.wait_filled(v, g, m)
                            rows = h[:, g, 2 * j:2 * j + 2, :]
                            rp.drain(nc.vector.tensor_tensor(
                                rows, rows, rp.bank(m)[0:T, :].rearrange("p (b d) -> p b d", b=2), ALU.add), m)
                        for j in range(2):
                            m = N1 - 2 + j
                            v.wait_ge(rp.drained[j], rp.before(g, m) + 1)

                    nc.vector.memset(krot[:], 0.0).then_inc(z_made, 1)
                    v.wait_ge(z_made, 1)
                    v.wait_ge(w1_loaded, 16 * len(w))
                    v.wait_ge(ln_added, G)
                    body(0, False)
                    with v.Fori(1, G) as g:
                        body(g, True)
                    l = 2 * G - 1
                    ln_vector_stats(h, G - 1, l)
                    ln_vector_mean(v, l)
                    ln_vector_rows(v, h, True, G - 1, l, rp, LN_M)

                @block.gpsimd
                def _(pool):
                    def add_q(g, c):
                        for j in range(2):
                            m = proj_m(c, j)
                            pool.wait_ge(rp.drained[m % 2], rp.before(g, m) + 1)
                        rs.wait_filled(pool, g, 2 * (c - 2) + 1)
                        nc.gpsimd.tensor_tensor(qrot[:, c % 2, :], qprod[:, 0, :], qprod[:, 1, :],
                                                ALU.add).then_inc(q_rot, 1)

                    def body(g, norm):
                        add_q(g, 0)
                        for n in range(NH + 1):
                            if norm and n == 3:
                                ln_pool_rstd(pool, G + g - 1)
                            if norm and n == 7:
                                ln_pool_add(pool, False, g - 1, G + g - 1)
                            if n % 2 == 0 and n // 2 + 1 < NCH:
                                add_q(g, n // 2 + 1)
                            if n >= 1:
                                attention_pool_norm(pool, seq, g, n - 1)

                    body(0, False)
                    with pool.Fori(1, G) as g:
                        body(g, True)
                    ln_pool_rstd(pool, 2 * G - 1)
                    ln_pool_add(pool, False, G - 1, 2 * G - 1)

                @block.scalar
                def _(act):
                    def probT_out(g, n):
                        rt.wait_filled(act, g, n)
                        if n >= RING:
                            rv.wait_filled(act, g, (n - RING) // 2)
                        else:
                            rv.wait_filled(act, g, (n - RING) // 2)
                        nc.scalar.activation(probT[:, n % RING, :], rt.bank(n)[0:T, 0:GT], ACT.Copy).then_inc(att_T, 1)
                        act.wait_ge(att_T, seq(g, n) + 1)
                        act.sem_inc(rt.drained[n % 2], 1)

                    def body(g, norm):
                        if not (isinstance(g, int) and g == 0):
                            rp.wait_filled(act, g - 1, N1 - 1)
                        for m, dst in enumerate((cq, ckv)):
                            rp.wait_filled(act, g, m)
                            rp.drain(nc.scalar.activation(dst[:], rp.bank(m)[:, 0:GT], ACT.Copy), m)
                            act.wait_ge(rp.drained[m], rp.before(g, m) + 1)
                            act.sem_inc(down, 1)
                        for b in range(GB):
                            for f in range(2):
                                m = 2 + 2 * b + f
                                rp.wait_filled(act, g, m)
                                rp.drain(nc.scalar.activation(V[:, b, f * 512:(f + 1) * 512],
                                                              rp.bank(m)[0:T, 0:512], ACT.Copy), m)
                        for n in range(NH + LAV + 1):
                            if norm and n == LN_STEP:
                                ln_scalar(act, rp, g, G + g - 1, LN_M, 1, g - 1)
                            if n < NH:
                                attention_scalar_exp(act, rs, g, n, seq, 1.0 / np.sqrt(DH))
                            if 0 <= n - LT < NH:
                                probT_out(g, n - LT)
                            if 0 <= n - LAV < NH and (n - LAV) % 2 == 1:
                                c = (n - LAV) // 2
                                rv.wait_filled(act, g, c)
                                rv.drain(nc.scalar.activation(oT[:, c, :], rv.bank(c)[:, 0:GT], ACT.Copy), c)
                                act.wait_ge(rv.drained[c % 2], rv.before(g, c) + 1)
                                act.sem_inc(o_cols, 1)

                    body(0, False)
                    with act.Fori(1, G) as g:
                        body(g, True)
                    ln_scalar(act, rp, G, 2 * G - 1, LN_M, 1, G - 1, at_end=True)
                    act.wait_ge(ln_stored, 16 * 2 * G)

        if upto < 2:
            final(nc, sem, h, out)
            return

        rank = perm.take([T, G, GB, TOPK])
        expert = perm.take([T, G, GB, TOPK])
        weight = perm.take([T, G, GB, TOPK])
        total = perm.take([T, E])
        iota8 = perm.take([T, E])
        place_i = perm.take([T, G, GB, TOPK], I32)
        tile_e = perm.take([T, TILES], I32)
        tile_at = perm.take([T, TILES], I32)
        iota_t = perm.take([T, TILES])
        with ExitStack() as ph:
            work = Space(arena, both.at, ARENA)
            slab = work.take([P, KD, GT])
            qT = work.take([P, KD, GT])
            kT = work.take([P, KD, GT])
            kmask = work.take([P, 2, GT])
            V2 = work.take([T, GB, NCH, 2, 2 * DM])
            yT = work.take([P, KD, GT])
            c2 = {n: work.take(sh) for n, sh in (
                ("hmask", [P, HC]), ("bkm", [P, 1]), ("causal", [T, T]), ("bpb", [T, D]),
                ("gateW", [P, KD, E]), ("gateb", [T, E]), ("tri", [T, T]))}
            ones = work.take([T, T])
            ids = work.take([T, G, GB], I32)
            ids_g = work.take([T, GB], I32)
            identb = work.take([T, T], BF16)
            causalb = work.take([T, GB, T], BF16)
            lg = work.take([T, GB, E])
            best = work.take([T, GB, 8])
            topi = work.take([T, GB, 8], U32)
            gap = work.take([T, GB])
            ew = work.take([T, GB])
            den = work.take([T, GB])
            oh = work.take([T, TOPK, GB, E])
            ohs = work.take([T, GB, E])
            tot = work.take([T, GB, E])
            base = work.take([T, GB, E])
            rk = work.take([T, GB, E])
            picked = work.take([T, TOPK, GB, E])
            pos = work.take([T, GB, TOPK], I32)
            zeros_i = work.take([P, LIST // P])
            (w2_loaded, slab_loaded, q_ready, k_ready, kmasked, v2_rows, y_cols, bp_added, zz_stored, h_stored,
             gate_lg, gate_chain, gate_gap, gate_exp, gate_oh, pos_ready, scattered, list_zero, projected, t2) = (
                sem(n) for n in (
                    "w2_loaded", "slab_loaded", "q_ready", "k_ready", "kmasked", "v2_rows", "y_cols", "bp_added",
                    "zz_stored", "h_stored", "gate_lg", "gate_chain", "gate_gap", "gate_exp", "gate_oh",
                    "pos_ready", "scattered", "list_zero", "projected", "t2"))
            GATE_M = 8
            LN2_STEP, GATE1_STEP, GATE2_STEP = 5, 8, 12
            rp = ring(0, 2, 12, 6, 4)
            rs = ring(2, 2, NH)
            rt = ring(4, 2, NH)
            rv = ring(6, 2, NCH)
            n_pairs = NCH // KD

            def pair_item(j):
                return 2 * (j % n_pairs) + j // n_pairs

            GC = 15

            def seq2(g, n):
                return NH * (G + g) + n

            def norm_index(g):
                return 2 * G + g

            block = nc.Block()
            with block:
                @block.sync
                def _(sp):
                    n_small = len(c2) + 3
                    for n in c2:
                        sp.dma_start(c2[n], a[n]).then_inc(w2_loaded, 16)
                    sp.dma_start(ids, a["ids"]).then_inc(w2_loaded, 16)
                    sp.dma_start(iota8, a["iota8"]).then_inc(w2_loaded, 16)
                    sp.dma_start(iota_t, a["iota_t"]).then_inc(w2_loaded, 16)
                    sp.wait_ge(t2, 1)
                    sp.dma_start(list_d.rearrange("(p n) o -> p (n o)", p=P), zeros_i.bitcast(I32)).then_inc(
                        list_zero, 16)

                    def after(g):
                        sp.wait_ge(ln_row, norm_index(g) + 1)
                        sp.dma_start(rows_d.rearrange("(g b p) d -> g p b d", b=GB, p=T)[g], zz[:]).then_inc(zz_stored, 16)
                        sp.wait_ge(ln_added, norm_index(g) + 1)
                        sp.dma_start(h_d[g], h[:, g].rearrange("p b d -> p (b d)")).then_inc(h_stored, 16)

                    sp.dma_start(slab, hnT[:, :, 0, :]).then_inc(slab_loaded, 16)
                    with sp.Fori(1, G) as g:
                        sp.wait_ge(projected, g)
                        sp.dma_start(slab, hnT[:, :, g, :]).then_inc(slab_loaded, 16)
                        after(g - 1)
                    after(G - 1)
                    sp.wait_ge(zz_stored, 16 * G)
                    sp.wait_ge(h_stored, 16 * G)

                @block.tensor
                def _(pe):
                    def scores(g, n):
                        pe.wait_ge(kmasked, NH * g + n + 1)
                        rs.wait_free(pe, g, n)
                        nc.tensor.matmul(rs.bank(n)[0:T, 0:GT], identb, causalb.rearrange("p b k -> p (b k)"),
                                         start=True, stop=False)
                        for b in range(GB):
                            cols = slice(b * T, (b + 1) * T)
                            last = nc.tensor.matmul(rs.bank(n)[0:T, cols], qT[:, n // HC, cols],
                                                    kmask[:, n % 2, cols], start=False, stop=(b == GB - 1))
                        rs.fill(last, n)

                    def values(g, j):
                        m = 2 * j // HC
                        if 2 * j % HC == 0:
                            rv.wait_free(pe, g, pair_item(j))
                        pe.wait_ge(att_T, seq2(g, 2 * j + 1) + 1)
                        quad = (j % (HC // 2)) * 2 * DM
                        for b in range(GB):
                            for hh in range(2):
                                n = 2 * j + hh
                                last = nc.tensor.matmul(
                                    rv.banks[m][quad:quad + 2 * DM, b * T:(b + 1) * T], V2[:, b, j, hh, :],
                                    probT[:, n % RING, b * T:(b + 1) * T], start=(hh == 0), stop=(hh == 1))
                        rv.fill(last, pair_item(j))

                    def gate(g, at_end=False):
                        pe.wait_ge(ln_out, 2 * norm_index(g) + 2)
                        gg = g + 1
                        rp.wait_free(pe, gg, GATE_M, at_end)
                        for b in range(GB):
                            for k in range(KD):
                                last = nc.tensor.matmul(rp.bank(GATE_M)[0:T, b * E:(b + 1) * E],
                                                        lnT[:, k, b * T:(b + 1) * T], c2["gateW"][:, k, :],
                                                        start=(k == 0), stop=(k == KD - 1))
                        rp.fill(last, GATE_M)

                    def prefix(g, at_end=False):
                        pe.wait_ge(gate_oh, g + 1)
                        m = GATE_M + 1
                        rp.wait_free(pe, g + 1, m, at_end)
                        cols = ohs.rearrange("p b e -> p (b e)")
                        nc.tensor.matmul(rp.bank(m)[0:T, 0:GB * E], c2["tri"], cols, start=True, stop=True)
                        rp.fill(nc.tensor.matmul(rp.bank(m)[0:T, GB * E:2 * GB * E], ones, cols, start=True, stop=True), m)

                    def body(g, norm):
                        pe.wait_ge(slab_loaded, 16 * g + 16)
                        for m in range(4):
                            rp.wait_free(pe, g, m)
                            for k in range(KD):
                                last = nc.tensor.matmul(rp.bank(m)[:, 0:GT],
                                                        wB[("wq2", "wk2")[m // 2]][:, k, (m % 2) * P:(m % 2 + 1) * P],
                                                        slab[:, k, :], start=(k == 0), stop=(k == KD - 1))
                            rp.fill(last, m)
                        for j in range(2):
                            rp.wait_free(pe, g, 4 + j)
                            for bb in range(2):
                                b = 2 * j + bb
                                for k in range(KD):
                                    last = nc.tensor.matmul(rp.bank(4 + j)[0:T, bb * D:(bb + 1) * D],
                                                            slab[:, k, b * T:(b + 1) * T], wB["wv2"][:, k, :],
                                                            start=(k == 0), stop=(k == KD - 1))
                            rp.fill(last, 4 + j)
                        rp.wait_filled(pe, g, 5)
                        pe.sem_inc(projected, 1)
                        pe.wait_ge(q_ready, KD * g + KD)
                        for n in range(NH + LAV + 1):
                            if norm and n == LN2_STEP:
                                ln_tensor(pe, rp, g, norm_index(g - 1), 6)
                            if norm and n == GATE1_STEP:
                                gate(g - 1)
                            if norm and n == GATE2_STEP:
                                prefix(g - 1)
                            if n < NH:
                                scores(g, n)
                            if 0 <= n - LT < NH:
                                attention_tensor_T(pe, rt, seq2, g, n - LT, n - LT)
                            if 0 <= n - LAV < NH and (n - LAV) % 2 == 1:
                                values(g, (n - LAV) // 2)
                        pe.wait_ge(y_cols, KD * g + KD)
                        for j in range(2):
                            m = 10 + j
                            rp.wait_free(pe, g, m)
                            for bb in range(2):
                                b = 2 * j + bb
                                for k in range(KD):
                                    last = nc.tensor.matmul(rp.bank(m)[0:T, bb * D:(bb + 1) * D],
                                                            yT[:, k, b * T:(b + 1) * T], wB["wp2"][:, k, :],
                                                            start=(k == 0), stop=(k == KD - 1))
                            rp.fill(last, m)

                    pe.wait_ge(w2_loaded, 16 * (len(c2) + 3))
                    pe.wait_ge(t2, 4)
                    body(0, False)
                    with pe.Fori(1, G) as g:
                        body(g, True)
                    ln_tensor(pe, rp, G, norm_index(G - 1), 6, at_end=True)
                    gate(G - 1, at_end=True)
                    prefix(G - 1, at_end=True)

                @block.vector
                def _(v):
                    def mask_keys(g, n):
                        if n % HC == 0:
                            v.wait_ge(k_ready, KD * g + n // HC + 1)
                        rs.wait_filled(v, g, n - 2)
                        nc.vector.tensor_scalar(kmask[:, n % 2, :], kT[:, n // HC, :], c2["hmask"][:, n % HC:n % HC + 1],
                                                None, ALU.mult).then_inc(kmasked, 1)

                    def gate_top(g, at_end=False):
                        rp.wait_filled(v, g + 1, GATE_M, at_end)
                        rp.drain(nc.vector.tensor_tensor(
                            lg, rp.bank(GATE_M)[0:T, 0:GB * E].rearrange("p (b e) -> p b e", b=GB),
                            c2["gateb"].unsqueeze(1).broadcast_to([T, GB, E]), ALU.add), GATE_M)
                        v.wait_ge(rp.drained[0], rp.before(g + 1, GATE_M, at_end) + 1)
                        v.sem_inc(ln_turn, 1)
                        for b in range(GB):
                            last = nc.vector.max(best[:, b, :], lg[:, b, :])
                        last.then_inc(gate_lg, 1)
                        v.wait_ge(gate_lg, 2 * g + 1)
                        v.sem_inc(ln_turn, 1)
                        for b in range(GB):
                            last = nc.vector.max_index(topi[:, b, :], best[:, b, :], lg[:, b, :])
                        last.then_inc(gate_lg, 1)
                        nc.vector.tensor_tensor(gap, best[:, :, 1], best[:, :, 0], ALU.subtract).then_inc(gate_gap, 1)
                        v.wait_ge(gate_lg, 2 * g + 2)
                        ex = expert[:, g]
                        chain(v, g, 1, nc.vector.tensor_copy(ex, topi[:, :, 0:TOPK]))
                        for k in range(TOPK):
                            last = nc.vector.tensor_tensor(
                                oh[:, k], iota8.unsqueeze(1).broadcast_to([T, GB, E]),
                                expert[:, g, :, k].unsqueeze(2).broadcast_to([T, GB, E]), ALU.is_equal)
                        chain(v, g, 2, last)
                        nc.vector.tensor_tensor(ohs, oh[:, 0], oh[:, 1], ALU.add).then_inc(gate_oh, 1)

                    def chain(v, g, k, ins):
                        ins.then_inc(gate_chain, 1)
                        v.wait_ge(gate_chain, GC * g + k)

                    def gate_place(g, at_end=False):
                        v.wait_ge(gate_exp, g + 1)
                        chain(v, g, 3, nc.vector.tensor_scalar(den, ew, 1.0, None, ALU.add))
                        chain(v, g, 4, nc.vector.reciprocal(weight[:, g, :, 0], den))
                        chain(v, g, 5, nc.vector.tensor_tensor(weight[:, g, :, 1], weight[:, g, :, 0], ew, ALU.mult))
                        m = GATE_M + 1
                        rp.wait_filled(v, g + 1, m, at_end)
                        chain(v, g, 6, nc.vector.tensor_copy(
                            tot, rp.bank(m)[0:T, GB * E:2 * GB * E].rearrange("p (b e) -> p b e", b=GB)))
                        chain(v, g, 7, nc.vector.tensor_copy(base[:, 0], total))
                        for b in range(1, GB):
                            chain(v, g, 7 + b, nc.vector.tensor_tensor(base[:, b], base[:, b - 1], tot[:, b - 1], ALU.add))
                        chain(v, g, 11, nc.vector.tensor_tensor(total, base[:, GB - 1], tot[:, GB - 1], ALU.add))
                        rp.drain(nc.vector.tensor_tensor(
                            rk, rp.bank(m)[0:T, 0:GB * E].rearrange("p (b e) -> p b e", b=GB), base, ALU.add), m)
                        v.wait_ge(rp.drained[1], rp.before(g + 1, m, at_end) + 1)
                        for k in range(TOPK):
                            last = nc.vector.tensor_tensor(picked[:, k], oh[:, k], rk, ALU.mult)
                        chain(v, g, 12, last)
                        for k in range(TOPK):
                            last = nc.vector.tensor_reduce(rank[:, g, :, k], picked[:, k], AX_X, ALU.add)
                        chain(v, g, 13, last)
                        v.wait_ge(scattered, 16 * TOPK * GB * g)
                        chain(v, g, 14, nc.vector.scalar_tensor_tensor(
                            pos, expert[:, g], float(CAP), rank[:, g], ALU.mult, ALU.add))
                        chain(v, g, 15, nc.vector.tensor_copy(ids_g, ids[:, g]))
                        v.sem_inc(pos_ready, 1)

                    def body(g, norm):
                        mask_keys(g, 0)
                        for n in range(NH + 1):
                            if norm and n == 1:
                                ln_vector_stats(xres, g - 1, norm_index(g - 1))
                            if norm and n == 2:
                                ln_vector_mean(v, norm_index(g - 1))
                            if norm and n == 4:
                                v.wait_ge(zz_stored, 16 * (g - 1))
                                ln_vector_rows(v, xres, False, g - 1, norm_index(g - 1), rp, 6)
                            if n < NH:
                                attention_vector_shift(v, rs, rt, seq2, g, n, lambda n: n)
                            if n + 1 < NH:
                                mask_keys(g, n + 1)
                            if n >= 1:
                                attention_vector_sum(v, seq2, g, n - 1)
                            if norm and n == GATE1_STEP:
                                gate_top(g - 1)
                            if norm and n == GATE2_STEP:
                                gate_place(g - 1)
                        v.wait_ge(bp_added, g + 1)
                        for j in range(2):
                            m = 10 + j
                            rp.wait_filled(v, g, m)
                            rows = xres[:, g, 2 * j:2 * j + 2, :]
                            rp.drain(nc.vector.tensor_tensor(
                                rows, rows, rp.bank(m)[0:T, :].rearrange("p (b d) -> p b d", b=2), ALU.add), m)
                        for j in range(2):
                            v.wait_ge(rp.drained[j], rp.before(g, 10 + j) + 1)

                    nc.vector.memset(zeros_i, 0.0).then_inc(t2, 1)
                    nc.vector.memset(V2, 0.0)
                    nc.vector.memset(total, 0.0)
                    nc.vector.memset(ones, 1.0).then_inc(t2, 1)
                    v.wait_ge(w2_loaded, 16 * (len(c2) + 3))
                    nc.vector.tensor_copy(identb, ident[0:T, 0:T]).then_inc(t2, 1)
                    nc.vector.tensor_copy(causalb, c2["causal"].unsqueeze(1).broadcast_to([T, GB, T])).then_inc(t2, 1)
                    v.wait_ge(t2, 4)
                    body(0, False)
                    with v.Fori(1, G) as g:
                        body(g, True)
                    l = norm_index(G - 1)
                    ln_vector_stats(xres, G - 1, l)
                    ln_vector_mean(v, l)
                    v.wait_ge(zz_stored, 16 * (G - 1))
                    ln_vector_rows(v, xres, False, G - 1, l, rp, 6)
                    gate_top(G - 1, at_end=True)
                    gate_place(G - 1, at_end=True)

                @block.gpsimd
                def _(pool):
                    def scatter(g):
                        pool.wait_ge(pos_ready, g + 1)
                        pool.sem_inc(dma_turn, 1)
                        for b in range(GB):
                            for k in range(TOPK):
                                nc.gpsimd.indirect_dma_start(
                                    list_d, bass.IndirectOffsetOnAxis(ap=pos[:, b, k:k + 1], axis=0),
                                    ids_g[:, b:b + 1], None).then_inc(scattered, 16)

                    def body(g, norm):
                        nc.gpsimd.tensor_tensor(xres[:, g], xres[:, g], c2["bpb"].unsqueeze(1).broadcast_to([T, GB, D]),
                                                ALU.add).then_inc(bp_added, 1)
                        for n in range(NH + 1):
                            if norm and n == 3:
                                ln_pool_rstd(pool, norm_index(g - 1))
                            if n >= 1:
                                attention_pool_norm(pool, seq2, g, n - 1)
                            if norm and n == 7:
                                ln_pool_add(pool, True, g - 1, norm_index(g - 1))
                        if norm:
                            scatter(g - 1)

                    pool.wait_ge(w2_loaded, 16 * (len(c2) + 3))
                    pool.wait_ge(list_zero, 16)
                    body(0, False)
                    with pool.Fori(1, G) as g:
                        body(g, True)
                    ln_pool_rstd(pool, norm_index(G - 1))
                    ln_pool_add(pool, True, G - 1, norm_index(G - 1))
                    scatter(G - 1)
                    pool.wait_ge(scattered, 16 * TOPK * GB * G)

                @block.scalar
                def _(act):
                    def probT_out(g, n):
                        rt.wait_filled(act, g, n)
                        if n >= RING:
                            rv.wait_filled(act, g, pair_item((n - RING) // 2))
                        elif not (isinstance(g, int) and g == 0):
                            rv.wait_filled(act, g - 1, pair_item((n - RING) // 2 + NCH))
                        nc.scalar.activation(probT[:, n % RING, :], rt.bank(n)[0:T, 0:GT], ACT.Copy).then_inc(att_T, 1)
                        act.wait_ge(att_T, seq2(g, n) + 1)
                        act.sem_inc(rt.drained[n % 2], 1)

                    def body(g, norm):
                        for m in range(4):
                            dst, done, bias = (qT, q_ready, bB[:, 0, m % 2:m % 2 + 1]) if m < 2 else (
                                kT, k_ready, bB[:, 1, m % 2:m % 2 + 1])
                            rp.wait_filled(act, g, m)
                            rp.drain(nc.scalar.activation(dst[:, m % 2, :], rp.bank(m)[:, 0:GT], ACT.Identity, bias=bias), m)
                            act.wait_ge(rp.drained[m % 2], rp.before(g, m) + 1)
                            act.sem_inc(done, 1)
                        for j in range(2):
                            rp.wait_filled(act, g, 4 + j)
                            src = rp.bank(4 + j)[0:T, :].rearrange("p (b n h d) -> p b n h d", b=2, n=NCH, h=2)
                            for bb in range(2):
                                for hh in range(2):
                                    last = nc.scalar.activation(
                                        V2[:, 2 * j + bb, :, hh, hh * DM:(hh + 1) * DM], src[:, bb, :, hh, :], ACT.Copy)
                            rp.drain(last, 4 + j)
                        for n in range(NH + LAV + 1):
                            if norm and n == LN2_STEP:
                                ln_scalar(act, rp, g, norm_index(g - 1), 6, 2, g - 1)
                            if norm and n == GATE1_STEP + 1:
                                act.wait_ge(gate_gap, g)
                                nc.scalar.activation(ew, gap, ACT.Exp).then_inc(gate_exp, 1)
                            if n < NH:
                                attention_scalar_exp(act, rs, g, n, seq2, 1.0 / np.sqrt(DM))
                            if 0 <= n - LT < NH:
                                probT_out(g, n - LT)
                            if 0 <= n - LAV < NH and (n - LAV) % HC == HC - 1:
                                m = (n - LAV) // HC
                                rv.wait_filled(act, g, pair_item(n_pairs * m + n_pairs - 1))
                                nc.scalar.activation(yT[:, m, :], rv.banks[m][:, 0:GT], ACT.Identity,
                                                     bias=bB[:, 2, m:m + 1]).then_inc(rv.drained[m], n_pairs)
                                act.wait_ge(rv.drained[m], rv.before(g, m) + n_pairs)
                                act.sem_inc(y_cols, 1)

                    act.wait_ge(w2_loaded, 16 * (len(c2) + 3))
                    act.wait_ge(t2, 2)
                    body(0, False)
                    with act.Fori(1, G) as g:
                        body(g, True)
                    l = norm_index(G - 1)
                    ln_scalar(act, rp, G, l, 6, 2, G - 1, at_end=True)
                    act.wait_ge(gate_gap, G)
                    nc.scalar.activation(ew, gap, ACT.Exp).then_inc(gate_exp, 1)
                    act.wait_ge(ln_stored, 16 * (l + 1))

        PAIRS = TILES // 2
        low = Space(arena, 0, BIG)
        high = Space(arena, BIG + PERM, ARENA)
        W2 = low.take([P, E, KH, D])
        b2 = low.take([P, E, D])
        W1 = high.take([P, E, KD, HID])
        b1 = high.take([P, E, HID])
        route = Space(arena, low.at, BIG)
        X = high.take([P, 2, D])
        xT = high.take([P, 2, KD, P])
        yt = high.take([P, 2, D])
        mid = low.take([P, 2, HID])
        midT = low.take([P, 2, KH, P])
        idx = high.take([P, 2], I32)
        n1 = route.take([T, E])
        n1i = route.take([T, E], I32)
        n2i = route.take([T, E], I32)
        n2 = route.take([T, E])
        ends = route.take([T, E + 1])
        start = route.take([T, E])
        NTOK = G * GB * TOPK
        sel = route.take([T, NTOK, E])
        selv = route.take([T, NTOK, E])
        stok = route.take([T, NTOK])
        past = route.take([T, TILES, E])
        pastv = route.take([T, TILES, E])
        te = route.take([T, TILES])
        tef = route.take([T, TILES])
        tst = route.take([T, TILES])
        toff = route.take([T, TILES])
        toff2 = route.take([T, TILES])
        (w3_loaded, routed, gathered0, gathered1, idx_loaded0, idx_loaded1, xT_ready, mid_ready, gelu_done,
         midT_ready, y_ready, y_stored0, y_stored1) = (sem(n) for n in (
            "w3_loaded", "routed", "gathered0", "gathered1", "idx_loaded0", "idx_loaded1", "xT_ready", "mid_ready",
            "gelu_done", "midT_ready", "y_ready", "y_stored0", "y_stored1"))
        gathered, idx_loaded, y_stored = (gathered0, gathered1), (idx_loaded0, idx_loaded1), (y_stored0, y_stored1)
        ROUTE = 17 + E
        rx = ring(0, 2, 2, groups=PAIRS)
        r1 = ring(2, 2, 4, groups=PAIRS)
        rm = ring(4, 2, 4, groups=PAIRS)
        r2 = ring(6, 2, 2, groups=PAIRS)

        def tiles_loop(eng, step, ahead):
            pass

        block = nc.Block()
        with block:
            @block.sync
            def _(sp):
                for e in range(E):
                    sp.dma_start(W1[:, e], a["W1"][:, e]).then_inc(w3_loaded, 16)
                    sp.dma_start(W2[:, e], a["W2"][:, e]).then_inc(w3_loaded, 16)
                sp.dma_start(b1, a["b1"]).then_inc(w3_loaded, 16)
                sp.dma_start(b2, a["b2"]).then_inc(w3_loaded, 16)
                sp.wait_ge(routed, ROUTE)

                def load_idx(i, s):
                    t = 2 * i + s
                    if not (isinstance(i, int) and t < 2):
                        sp.wait_ge(gathered[s % 2], 16 * (i + s // 2))
                    at = sp.value_load(tile_at[0:1, bass.ds(t, 1)], min_val=0, max_val=LIST - P)
                    sp.dma_start(idx[:, s % 2:s % 2 + 1], list_d[bass.ds(at, P), :]).then_inc(idx_loaded[s % 2], 16)

                def store(i, s):
                    t = 2 * i + s
                    sp.wait_ge(y_ready, t + 1)
                    sp.dma_start(y_d[bass.ds(t * P, P), :], yt[:, s, :]).then_inc(y_stored[s], 16)

                load_idx(0, 0)
                load_idx(0, 1)
                with sp.Fori(0, PAIRS - 1) as i:
                    for s in range(2):
                        load_idx(i, s + 2)
                        store(i, s)
                for s in range(2):
                    store(PAIRS - 1, s)
                for s in range(2):
                    sp.wait_ge(y_stored[s], 16 * PAIRS)

            @block.gpsimd
            def _(pool):
                def gather(i, s):
                    pool.wait_ge(idx_loaded[s], 16 * i + 16)
                    if not (isinstance(i, int) and i == 0):
                        rx.wait_filled(pool, i, s - 2)
                    pool.sem_inc(dma_turn, 1)
                    nc.gpsimd.indirect_dma_start(X[:, s, :], None, rows_d,
                                                 bass.IndirectOffsetOnAxis(ap=idx[:, s:s + 1], axis=0)
                                                 ).then_inc(gathered[s], 16)

                for s in range(2):
                    gather(0, s)
                with pool.Fori(1, PAIRS) as i:
                    for s in range(2):
                        gather(i, s)

            @block.tensor
            def _(pe):
                def rows(i, s):
                    pe.wait_ge(gathered[s % 2], 16 * (i + s // 2) + 16)
                    rx.wait_free(pe, i, s)
                    for k in range(KD):
                        last = nc.tensor.transpose(rx.bank(s)[:, k * P:(k + 1) * P], X[:, s % 2, k * P:(k + 1) * P], ident[:])
                    rx.fill(last, s)

                def hidden(i, s):
                    pe.wait_ge(xT_ready, 2 * i + s + 1)
                    pe.sem_inc(load_turn, 1)
                    e = pe.value_load(tile_e[0:1, bass.ds(2 * i + s, 1)], min_val=0, max_val=E - 1)
                    for f in range(2):
                        m = 2 * s + f
                        r1.wait_free(pe, i, m)
                        for k in range(KD):
                            last = nc.tensor.matmul(r1.bank(m)[:, 0:512], xT[:, s % 2, k, :],
                                                    W1[:, bass.ds(e, 1), k, f * 512:(f + 1) * 512],
                                                    start=(k == 0), stop=(k == KD - 1))
                        r1.fill(last, m)

                def turn(i, s):
                    pe.wait_ge(gelu_done, 2 * i + s + 1)
                    for f in range(2):
                        m = 2 * s + f
                        rm.wait_free(pe, i, m)
                        for j in range(4):
                            last = nc.tensor.transpose(rm.bank(m)[:, j * P:(j + 1) * P],
                                                       mid[:, s, (4 * f + j) * P:(4 * f + j + 1) * P], ident[:])
                        rm.fill(last, m)

                def result(i, s):
                    for f in range(2):
                        m = 2 * s + f
                        pe.wait_ge(rm.drained[f], rm.before(i, m) + 1)
                    pe.sem_inc(load_turn, 1)
                    e = pe.value_load(tile_e[0:1, bass.ds(2 * i + s, 1)], min_val=0, max_val=E - 1)
                    r2.wait_free(pe, i, s)
                    for k in range(KH):
                        last = nc.tensor.matmul(r2.bank(s)[:, 0:D], midT[:, s, k, :], W2[:, bass.ds(e, 1), k, :],
                                                start=(k == 0), stop=(k == KH - 1))
                    r2.fill(last, s)

                pe.wait_ge(routed, ROUTE)
                rows(0, 0)
                rows(0, 1)
                pe.wait_ge(w3_loaded, 16 * (2 * E + 2))
                hidden(0, 0)
                with pe.Fori(0, PAIRS - 1) as i:
                    for s in range(2):
                        rows(i, s + 2)
                        turn(i, s)
                        hidden(i, s + 1)
                        result(i, s)
                i = PAIRS - 1
                turn(i, 0)
                hidden(i, 1)
                result(i, 0)
                turn(i, 1)
                result(i, 1)

            @block.vector
            def _(v):
                vec = nc.vector
                done = [0]

                def chain(ins):
                    done[0] += 1
                    ins.then_inc(routed, 1)
                    v.wait_ge(routed, done[0])

                chain(vec.tensor_scalar(n1, total, float(P - 1), None, ALU.add))
                chain(vec.tensor_copy(n1i, n1))
                chain(vec.tensor_scalar(n2i, n1i, 7, None, ALU.arith_shift_right))
                chain(vec.tensor_copy(n2, n2i))
                chain(vec.memset(ends, 0.0))
                for e in range(E):
                    chain(vec.tensor_tensor(ends[:, e + 1:e + 2], ends[:, e:e + 1], n2[:, e:e + 1], ALU.add))
                chain(vec.tensor_scalar(start, ends[:, 0:E], float(P), None, ALU.mult))
                flat = expert.rearrange("p g b k -> p (g b k)")
                chain(vec.tensor_tensor(sel, iota8.unsqueeze(1).broadcast_to([T, NTOK, E]),
                                        flat.unsqueeze(2).broadcast_to([T, NTOK, E]), ALU.is_equal))
                chain(vec.tensor_tensor(selv, sel, start.unsqueeze(1).broadcast_to([T, NTOK, E]), ALU.mult))
                chain(vec.tensor_reduce(stok, selv, AX_X, ALU.add))
                vec.tensor_tensor(place_i.rearrange("p g b k -> p (g b k)"), stok,
                                  rank.rearrange("p g b k -> p (g b k)"), ALU.add)
                last_end = ends[:, 1:E + 1].unsqueeze(1).broadcast_to([T, TILES, E])
                chain(vec.tensor_tensor(past, iota_t.unsqueeze(2).broadcast_to([T, TILES, E]), last_end, ALU.is_ge))
                chain(vec.tensor_tensor(pastv, past, last_end, ALU.mult))
                vec.tensor_reduce(te, past, AX_X, ALU.add)
                chain(vec.tensor_reduce(tst, pastv, AX_X, ALU.max))
                chain(vec.tensor_scalar(tef, te, float(E - 1), None, ALU.min))
                vec.tensor_copy(tile_e, tef)
                chain(vec.tensor_tensor(toff, iota_t, tst, ALU.subtract))
                chain(vec.tensor_scalar(toff2, toff, float(P), None, ALU.mult))
                chain(vec.scalar_tensor_tensor(tile_at, tef, float(CAP), toff2, ALU.mult, ALU.add))
                assert done[0] == ROUTE - 1, done
                vec.memset(idx.bitcast(F32), 0.0).then_inc(routed, 1)
                v.wait_ge(routed, ROUTE)
                v.wait_ge(w3_loaded, 16 * (2 * E + 2))

                def add_b1(i, s):
                    e = v.value_load(tile_e[0:1, bass.ds(2 * i + s, 1)], min_val=0, max_val=E - 1)
                    if not (isinstance(i, int) and 2 * i + s < 2):
                        for f in range(2):
                            rm.wait_filled(v, i, 2 * (s - 2) + f)
                    for f in range(2):
                        m = 2 * s + f
                        r1.wait_filled(v, i, m)
                        r1.drain(vec.tensor_tensor(mid[:, s % 2, f * 512:(f + 1) * 512], r1.bank(m)[:, 0:512],
                                                   b1[:, bass.ds(e, 1), f * 512:(f + 1) * 512], ALU.add), m)

                def midT_out(i, s):
                    m = 2 * s + 1
                    rm.wait_filled(v, i, m)
                    if not (isinstance(i, int) and 2 * i + s < 2):
                        r2.wait_filled(v, i, s - 2)
                    rm.drain(vec.tensor_copy(midT[:, s, 4:8, :].rearrange("p k t -> p (k t)"), rm.bank(m)[:, 0:512]), m)

                def add_b2(i, s):
                    e = v.value_load(tile_e[0:1, bass.ds(2 * i + s, 1)], min_val=0, max_val=E - 1)
                    if not (isinstance(i, int) and i == 0):
                        v.wait_ge(y_stored[s], 16 * i)
                    r2.wait_filled(v, i, s)
                    r2.drain(vec.tensor_tensor(yt[:, s, :], r2.bank(s)[:, 0:D], b2[:, bass.ds(e, 1), :], ALU.add), s)
                    v.wait_ge(r2.drained[s], r2.before(i, s) + 1)
                    v.sem_inc(y_ready, 1)

                def step(i, s, more):
                    midT_out(i, s)
                    if more:
                        add_b1(i, s + 1)
                    add_b2(i, s)

                add_b1(0, 0)
                step(0, 0, True)
                step(0, 1, True)
                with v.Fori(1, PAIRS - 1) as i:
                    step(i, 0, True)
                    step(i, 1, True)
                step(PAIRS - 1, 0, True)
                step(PAIRS - 1, 1, False)

            @block.scalar
            def _(act):
                def rows_out(i, s):
                    rx.wait_filled(act, i, s)
                    if not (isinstance(i, int) and 2 * i + s < 2):
                        r1.wait_filled(act, i, 2 * (s - 2) + 1)
                    for k in range(KD):
                        last = nc.scalar.activation(xT[:, s % 2, k, :], rx.bank(s)[:, k * P:(k + 1) * P], ACT.Identity,
                                                    bias=gb[:, 2, 1, k:k + 1], scale=gb[:, 2, 0, k:k + 1])
                    rx.drain(last, s)
                    act.wait_ge(rx.drained[s % 2], rx.before(i, s) + 1)
                    act.sem_inc(xT_ready, 1)

                def gelu(i, s):
                    for f in range(2):
                        m = 2 * s + f
                        act.wait_ge(r1.drained[f], r1.before(i, m) + 1)
                    nc.scalar.activation(mid[:, s % 2, :], mid[:, s % 2, :], ACT.Gelu).then_inc(gelu_done, 1)

                def midT_out(i, s):
                    m = 2 * s
                    rm.wait_filled(act, i, m)
                    if not (isinstance(i, int) and 2 * i + s < 2):
                        r2.wait_filled(act, i, s - 2)
                    rm.drain(nc.scalar.activation(midT[:, s, 0:4, :].rearrange("p k t -> p (k t)"),
                                                  rm.bank(m)[:, 0:512], ACT.Copy), m)

                def step(i, s, rows, more):
                    if rows:
                        rows_out(i, s + 2)
                    midT_out(i, s)
                    if more:
                        gelu(i, s + 1)

                rows_out(0, 0)
                rows_out(0, 1)
                gelu(0, 0)
                step(0, 0, True, True)
                step(0, 1, True, True)
                with act.Fori(1, PAIRS - 1) as i:
                    step(i, 0, True, True)
                    step(i, 1, True, True)
                step(PAIRS - 1, 0, False, True)
                step(PAIRS - 1, 1, False, False)

        YG = Space(arena, BIG + PERM, ARENA)
        yg = YG.take([T, 2, GB, TOPK, D])
        pg = YG.take([T, 2, GB, TOPK], I32)
        h_back, pg_ready, y_in0, y_in1, mixed = (sem(n) for n in ("h_back", "pg_ready", "y_in0", "y_in1", "mixed"))
        y_in = (y_in0, y_in1)
        r = ring(0, 2, 2)
        block = nc.Block()
        with block:
            @block.sync
            def _(sp):
                for g in range(G):
                    sp.dma_start(h[:, g].rearrange("p b d -> p (b d)"), h_d[g]).then_inc(h_back, 16)

            @block.gpsimd
            def _(pool):
                with pool.Fori(0, G // 2) as i:
                    for s in range(2):
                        g = 2 * i + s
                        pool.wait_ge(pg_ready, g + 1)
                        pool.sem_inc(dma_turn, 1)
                        for b in range(GB):
                            for k in range(TOPK):
                                nc.gpsimd.indirect_dma_start(
                                    yg[:, s, b, k, :], None, y_d,
                                    bass.IndirectOffsetOnAxis(ap=pg[:, s, b, k:k + 1], axis=0)).then_inc(y_in[s], 16)
                    for s in range(2):
                        ln_pool_rstd(pool, 3 * G + 2 * i + s)
                        ln_pool_add(pool, False, 2 * i + s, 3 * G + 2 * i + s)

            @block.vector
            def _(v):
                v.wait_ge(h_back, 16 * G)
                with v.Fori(0, G // 2) as i:
                    for s in range(2):
                        g = 2 * i + s
                        v.wait_ge(mixed, 2 * TOPK * i)
                        nc.vector.tensor_copy(pg[:, s], place_i[:, g]).then_inc(pg_ready, 1)
                        for s2 in ([] if s == 0 else [0, 1]):
                            g2 = 2 * i + s2
                            v.wait_ge(y_in[s2], 16 * GB * TOPK * (i + 1))
                            for k in range(TOPK):
                                for b in range(GB):
                                    last = nc.vector.scalar_tensor_tensor(
                                        h[:, g2, b, :], yg[:, s2, b, k, :], weight[:, g2, b, k:k + 1], h[:, g2, b, :],
                                        ALU.mult, ALU.add)
                                last.then_inc(mixed, 1)
                                v.wait_ge(mixed, 2 * g2 + k + 1)
                            ln_vector_stats(h, g2, 3 * G + g2)
                            ln_vector_mean(v, 3 * G + g2)
                            ln_vector_rows(v, h, False, g2, 3 * G + g2, r, 0)

            @block.tensor
            def _(pe):
                with pe.Fori(0, G) as g:
                    ln_tensor(pe, r, g, 3 * G + g, 0)

            @block.scalar
            def _(act):
                with act.Fori(0, G) as g:
                    ln_scalar(act, r, g, 3 * G + g, 0, None, g)
                act.wait_ge(ln_stored, 16 * 4 * G)

        if upto < 4:
            final(nc, sem, h, out)
            return

        late = Space(arena, BIG + PERM, ARENA)
        wg = late.take([P, KD, FFN])
        wu = late.take([P, KD, FFN])
        wd = late.take([P, KF, D])
        wave = Space(arena, late.at, ARENA)
        wqk = wave.take([P, KD, 4 * D])
        wout = wave.take([P, KD, D])
        bias4 = wave.take([T, 4 * D])
        bout = wave.take([T, D])
        toep = wave.take([T, NH, T])
        mixT = wave.take([P, KD, D])
        setup = Space(arena, wave.at, ARENA)
        TT = T + FIELD // P
        lag = setup.take([P, TT])
        keep = setup.take([T, T])
        pw = setup.take([P, 3, NH])
        fc = setup.take([NH, NH])
        dmask = setup.take([P, DM])
        sp_ = setup.take([P, 8, NH])
        arg = setup.take([P, NH, TT])
        turns = setup.take([P, NH, TT])
        env = setup.take([P, NH, TT])
        env2 = setup.take([P, NH, TT])
        ab = setup.take([P, NH])
        nrm = setup.take([T, 2, NH])
        ones4 = setup.take([P, T])
        cst = setup.take([NH, 4])
        cx = setup.take([NH, 2, NH])
        cb = setup.take([NH, NH, DM])
        w4_loaded, built, act_in, act_built, pe_built = (
            sem(n) for n in ("w4_loaded", "built", "act_in", "act_built", "pe_built"))
        ENV_AT, ARG_AT, SUM_AT, CX_AT, CB_AT = 10, 20, 25, 31, 34
        PI2 = 2 * np.pi
        C1 = 6.28125
        C2 = float(np.float32(np.floor((PI2 - C1) * 2 ** 21) / 2 ** 21))
        C3 = float(np.float32(PI2 - C1 - C2))
        ROUND = 12582912.0

        block = nc.Block()
        with block:
            loads = [(wqk, "wqk"), (wout, "wout4"), (bias4, "bias4"), (bout, "bout"), (lag, "lag"), (keep, "keep"),
                     (pw, "pw"), (fc, "fc"), (dmask, "dmask")]

            @block.sync
            def _(sp):
                for dst, n in loads:
                    sp.dma_start(dst, a[n]).then_inc(w4_loaded, 16)
                sp.wait_ge(w4_loaded, 16 * len(loads))

            @block.vector
            def _(v):
                vec = nc.vector
                n = [0]

                def chain(ins):
                    n[0] += 1
                    ins.then_inc(built, 1)
                    v.wait_ge(built, n[0])

                def heads(x):
                    return x.unsqueeze(2).broadcast_to([P, NH, TT])

                v.wait_ge(w4_loaded, 16 * len(loads))
                damp = pw[:, 1, :]
                chain(vec.tensor_scalar(sp_[:, 0], damp, -1.0, None, ALU.mult))
                chain(vec.tensor_tensor(sp_[:, 1], sp_[:, 0], damp, ALU.min))
                v.wait_ge(act_built, 1)
                chain(vec.tensor_scalar(sp_[:, 4], sp_[:, 2], 1.0, -1.0, ALU.add, ALU.add))
                chain(vec.tensor_scalar(sp_[:, 5], sp_[:, 4], 0.0, None, ALU.is_equal))
                vec.tensor_tensor(sp_[:, 4], sp_[:, 4], sp_[:, 5], ALU.add)
                chain(vec.tensor_tensor(sp_[:, 3], sp_[:, 3], sp_[:, 5], ALU.add))
                chain(vec.reciprocal(sp_[:, 6], sp_[:, 4]))
                chain(vec.tensor_tensor(sp_[:, 3], sp_[:, 3], sp_[:, 6], ALU.mult))
                chain(vec.tensor_tensor(sp_[:, 3], sp_[:, 3], sp_[:, 2], ALU.mult))
                chain(vec.scalar_tensor_tensor(sp_[:, 7], damp, 0.0, sp_[:, 3], ALU.max, ALU.add))
                lags = lag.unsqueeze(1).broadcast_to([P, NH, TT])
                chain(vec.tensor_tensor(env, lags, heads(sp_[:, 7]), ALU.mult))
                assert n[0] == ENV_AT
                chain(vec.tensor_tensor(arg, lags, heads(pw[:, 0, :]), ALU.mult))
                chain(vec.tensor_tensor(arg, arg, heads(pw[:, 2, :]), ALU.add))
                chain(vec.tensor_scalar(turns, arg, float(1 / PI2), ROUND, ALU.mult, ALU.add))
                chain(vec.tensor_scalar(turns, turns, -ROUND, None, ALU.add))
                for c in (C1, C2, C3):
                    chain(vec.scalar_tensor_tensor(arg, turns, -c, arg, ALU.mult, ALU.add))
                chain(vec.tensor_scalar(turns, arg, -1.0, None, ALU.mult))
                chain(vec.tensor_tensor(arg, arg, turns, ALU.min))
                chain(vec.tensor_scalar(arg, arg, float(np.pi / 2), float(-np.pi / 2), ALU.add, ALU.max))
                assert n[0] == ARG_AT
                v.wait_ge(act_built, 3)
                chain(vec.tensor_tensor(arg, env2, turns, ALU.mult))
                chain(vec.tensor_scalar(turns, arg, -1.0, None, ALU.mult))
                chain(vec.tensor_tensor(env, arg, turns, ALU.max))
                chain(vec.tensor_reduce(ab, env[:, :, T:TT], AX_X, ALU.add))
                chain(vec.memset(ones4, 1.0))
                assert n[0] == SUM_AT
                v.wait_ge(pe_built, 1)
                chain(vec.tensor_scalar(nrm[:, 0], banks[0][0:T, 0:NH], 1e-8, None, ALU.max))
                chain(vec.reciprocal(nrm[:, 1], nrm[:, 0]))
                chain(vec.tensor_tensor(toep, arg[0:T, :, 0:T], nrm[:, 1].unsqueeze(2).broadcast_to([T, NH, T]), ALU.mult))
                chain(vec.tensor_tensor(toep, toep, keep.unsqueeze(1).broadcast_to([T, NH, T]), ALU.mult))
                chain(vec.tensor_reduce(cst[:, 0:1], fc, AX_X, ALU.max))
                chain(vec.tensor_scalar(cx[:, 0], fc, cst[:, 0:1], None, ALU.subtract))
                assert n[0] == CX_AT
                v.wait_ge(act_built, 4)
                chain(vec.tensor_reduce(cst[:, 1:2], cx[:, 1], AX_X, ALU.add))
                chain(vec.reciprocal(cst[:, 2:3], cst[:, 1:2]))
                chain(vec.tensor_scalar(cb, cx[:, 1].unsqueeze(2).broadcast_to([NH, NH, DM]), cst[:, 2:3], None, ALU.mult))
                assert n[0] == CB_AT
                v.wait_ge(pe_built, 2)
                for k in range(KD):
                    last = vec.tensor_tensor(mixT[:, k, :].rearrange("p (i d) -> p i d", d=DM),
                                             banks[1][:, k * NH:(k + 1) * NH].unsqueeze(2).broadcast_to([P, NH, DM]),
                                             dmask.unsqueeze(1).broadcast_to([P, NH, DM]), ALU.mult)
                chain(last)

            @block.scalar
            def _(act):
                act.wait_ge(built, 2)
                nc.scalar.activation(sp_[:, 2], sp_[:, 1], ACT.Exp).then_inc(act_in, 1)
                act.wait_ge(act_in, 1)
                nc.scalar.activation(sp_[:, 3], sp_[:, 2], ACT.Ln, bias=1.0).then_inc(act_built, 1)
                act.wait_ge(built, ENV_AT)
                nc.scalar.activation(env2, env, ACT.Exp, scale=-1.0).then_inc(act_built, 1)
                act.wait_ge(built, ARG_AT)
                nc.scalar.activation(turns, arg, ACT.Sin).then_inc(act_built, 1)
                act.wait_ge(built, CX_AT)
                nc.scalar.activation(cx[:, 1], cx[:, 0], ACT.Exp).then_inc(act_built, 1)

            @block.tensor
            def _(pe):
                pe.wait_ge(built, SUM_AT)
                nc.tensor.matmul(banks[0][0:T, 0:NH], ones4, ab, start=True, stop=True).then_inc(pe_built, 1)
                pe.wait_ge(built, CB_AT)
                for k in range(KD):
                    last = nc.tensor.transpose(banks[1][:, k * NH:(k + 1) * NH],
                                               cb.rearrange("p j d -> p (j d)")[:, k * P:(k + 1) * P], ident[0:NH, 0:NH])
                last.then_inc(pe_built, 1)

        tile4 = Space(arena, wave.at, ARENA)
        slab = tile4.take([P, KD, GT])
        qk = tile4.take([T, GB, 2 * D])
        vg = tile4.take([T, GB, 2 * D])
        ex = tile4.take([T, GB, 2 * D])
        eg = tile4.take([T, GB, D])
        dep = tile4.take([T, GB, D])
        qg = tile4.take([T, GB, D])
        conv = tile4.take([T, GB, D])
        convT = tile4.take([P, KD, GT])
        fT = tile4.take([P, KD, GT])
        (slab4, qkvg_done, v4, a4, p4, fT_ready, convT_ready, conv_ready, raw_loaded, w5_ready, bout_added) = (sem(n) for n in (
            "slab4", "qkvg_done", "v4", "a4", "p4", "fT_ready", "convT_ready", "conv_ready", "raw_loaded", "w5_ready",
            "bout_added"))
        raw = Space(arena, tile4.at, ARENA).take([P, KD, FFN], I32)
        r = ring(0, 4, 20)
        VS = 7

        block = nc.Block()
        with block:
            @block.sync
            def _(sp):
                with sp.Fori(0, G) as g:
                    sp.wait_ge(qkvg_done, g)
                    sp.dma_start(slab, hnT[:, :, g, :]).then_inc(slab4, 16)
                for n, name in enumerate(("wg_i", "wu_i", "wd_i")):
                    sp.wait_ge(w5_ready, n)
                    dst = raw if n < 2 else raw.rearrange("p k f -> p (k f)").rearrange("p (k d) -> p k d", k=KF)
                    sp.dma_start(dst, a[name]).then_inc(raw_loaded, 16)
                sp.wait_ge(raw_loaded, 48)

            @block.tensor
            def _(pe):
                def turn(g, m0, src):
                    for k in range(KD):
                        r.wait_free(pe, g, m0 + k)
                        for b in range(GB):
                            last = nc.tensor.transpose(r.bank(m0 + k)[:, b * T:(b + 1) * T], src[:, b, k * P:(k + 1) * P],
                                                       ident[0:T, 0:T])
                        r.fill(last, m0 + k)

                def contract(g, m0, lhs, rhs):
                    for j in range(2):
                        r.wait_free(pe, g, m0 + j)
                        for bb in range(2):
                            b = 2 * j + bb
                            for k in range(KD):
                                last = nc.tensor.matmul(r.bank(m0 + j)[0:T, bb * D:(bb + 1) * D],
                                                        lhs[:, k, b * T:(b + 1) * T], rhs[:, k, :],
                                                        start=(k == 0), stop=(k == KD - 1))
                        r.fill(last, m0 + j)

                with pe.Fori(0, G) as g:
                    pe.wait_ge(slab4, 16 * g + 16)
                    for b in range(GB):
                        for f in range(2):
                            m = 2 * b + f
                            r.wait_free(pe, g, m)
                            for k in range(KD):
                                last = nc.tensor.matmul(r.bank(m)[0:T, 0:512], slab[:, k, b * T:(b + 1) * T],
                                                        wqk[:, k, f * 512:(f + 1) * 512], start=(k == 0), stop=(k == KD - 1))
                            r.fill(last, m)
                    r.wait_filled(pe, g, 7)
                    pe.sem_inc(qkvg_done, 1)
                    pe.wait_ge(v4, VS * g + 3)
                    for k in range(2):
                        r.wait_free(pe, g, 8 + k)
                        for jj in range(HC):
                            j = HC * k + jj
                            last = nc.tensor.matmul(r.bank(8 + k)[0:T, jj * GB * DM:(jj + 1) * GB * DM], toep[:, j, :],
                                                    dep[:, :, j * DM:(j + 1) * DM], start=True, stop=True)
                        r.fill(last, 8 + k)
                    pe.wait_ge(conv_ready, g + 1)
                    turn(g, 10, conv)
                    pe.wait_ge(convT_ready, g + 1)
                    contract(g, 12, convT, mixT)
                    pe.wait_ge(v4, VS * g + 7)
                    turn(g, 14, conv)
                    pe.wait_ge(fT_ready, g + 1)
                    contract(g, 16, fT, wout)
                    ln_tensor(pe, r, g, 4 * G + g, 18)

            @block.vector
            def _(v):
                vec = nc.vector
                with v.Fori(0, G) as g:
                    def chain(k, ins):
                        ins.then_inc(v4, 1)
                        v.wait_ge(v4, VS * g + k)
                    for b in range(GB):
                        for f in range(2):
                            m = 2 * b + f
                            r.wait_filled(v, g, m)
                            r.drain(vec.tensor_tensor((qk, vg)[f][:, b, :], r.bank(m)[0:T, 0:512],
                                                      bias4[:, f * 512:(f + 1) * 512], ALU.add), m)
                    for m in range(4, 8):
                        v.wait_ge(r.drained[m % 4], r.before(g, m) + 1)
                    chain(1, vec.tensor_scalar(ex, qk, 0.0, None, ALU.min))
                    v.wait_ge(a4, 2 * g + 1)
                    chain(2, vec.scalar_tensor_tensor(qk, qk, 0.0, ex, ALU.max, ALU.add))
                    chain(3, vec.tensor_tensor(dep, qk[:, :, D:2 * D], vg[:, :, 0:D], ALU.mult))
                    v.wait_ge(a4, 2 * g + 2)
                    chain(4, vec.tensor_scalar(eg, eg, 1.0, None, ALU.add))
                    chain(5, vec.reciprocal(vg[:, :, D:2 * D], eg))
                    chain(6, vec.tensor_tensor(qg, qk[:, :, 0:D], vg[:, :, D:2 * D], ALU.mult))
                    r.wait_filled(v, g, 11)
                    for j in range(2):
                        m = 12 + j
                        r.wait_filled(v, g, m)
                        r.drain(vec.tensor_tensor(conv[:, 2 * j:2 * j + 2, :],
                                                  r.bank(m)[0:T, :].rearrange("p (b d) -> p b d", b=2),
                                                  qg[:, 2 * j:2 * j + 2, :], ALU.mult), m)
                    for j in range(2):
                        v.wait_ge(r.drained[j], r.before(g, 12 + j) + 1)
                    v.sem_inc(v4, 1)
                    v.wait_ge(bout_added, g + 1)
                    for j in range(2):
                        m = 16 + j
                        r.wait_filled(v, g, m)
                        rows = h[:, g, 2 * j:2 * j + 2, :]
                        r.drain(vec.tensor_tensor(rows, rows, r.bank(m)[0:T, :].rearrange("p (b d) -> p b d", b=2),
                                                  ALU.add), m)
                    for j in range(2):
                        v.wait_ge(r.drained[j], r.before(g, 16 + j) + 1)
                    ln_vector_stats(h, g, 4 * G + g)
                    ln_vector_mean(v, 4 * G + g)
                    ln_vector_rows(v, h, False, g, 4 * G + g, r, 18)
                SCALE = float(np.float32(1.0 / 127.0))
                for n, dst in enumerate((wg, wu, wd)):
                    v.wait_ge(raw_loaded, 16 * n + 16)
                    src = raw if n < 2 else raw.rearrange("p k f -> p (k f)").rearrange("p (k d) -> p k d", k=KF)
                    vec.tensor_scalar(dst, src, SCALE, None, ALU.mult).then_inc(w5_ready, 1)

            @block.scalar
            def _(act):
                with act.Fori(0, G) as g:
                    act.wait_ge(v4, VS * g + 1)
                    nc.scalar.activation(ex, ex, ACT.Exp).then_inc(a4, 1)
                    nc.scalar.activation(eg, vg[:, :, D:2 * D], ACT.Exp, scale=-1.0).then_inc(a4, 1)
                    for k in range(2):
                        m = 8 + k
                        r.wait_filled(act, g, m)
                        r.drain(nc.scalar.activation(
                            conv.rearrange("p b (j d) -> p b j d", d=DM)[:, :, k * HC:(k + 1) * HC, :],
                            r.bank(m)[0:T, :].rearrange("p (j b d) -> p b j d", j=HC, b=GB), ACT.Copy), m)
                    for k in range(2):
                        act.wait_ge(r.drained[k], r.before(g, 8 + k) + 1)
                    act.sem_inc(conv_ready, 1)
                    for m0, dst, done in ((10, convT, convT_ready), (14, fT, fT_ready)):
                        for k in range(KD):
                            r.wait_filled(act, g, m0 + k)
                            r.drain(nc.scalar.activation(dst[:, k, :], r.bank(m0 + k)[:, 0:GT], ACT.Copy), m0 + k)
                        for k in range(KD):
                            act.wait_ge(r.drained[(m0 + k) % 4], r.before(g, m0 + k) + 1)
                        act.sem_inc(done, 1)
                    ln_scalar(act, r, g, 4 * G + g, 18, None, g)
                act.wait_ge(ln_stored, 16 * 5 * G)

            @block.gpsimd
            def _(pool):
                with pool.Fori(0, G) as g:
                    nc.gpsimd.tensor_tensor(h[:, g], h[:, g], bout.unsqueeze(1).broadcast_to([T, GB, D]),
                                            ALU.add).then_inc(bout_added, 1)
                    ln_pool_rstd(pool, 4 * G + g)
                    ln_pool_add(pool, False, g, 4 * G + g)

        if upto < 5:
            final(nc, sem, h, out)
            return

        fin = Space(arena, late.at, ARENA)
        hid = fin.take([P, 2, KF, GT])
        sg = fin.take([P, 2, GT])
        hid_ready, rows_ready = sem("hid_ready"), sem("rows_ready")
        ru = ring(0, 4, 2 * KF)
        rd = ring(4, 4, 4, groups=G // 2)
        block = nc.Block()
        with block:
            @block.tensor
            def _(pe):
                def up(i, s):
                    g = 2 * i + s
                    for c in range(KF):
                        for j, w_ in enumerate((wg, wu)):
                            m = 2 * c + j
                            ru.wait_free(pe, g, m)
                            for k in range(KD):
                                last = nc.tensor.matmul(ru.bank(m)[:, 0:GT], w_[:, k, c * P:(c + 1) * P], hnT[:, k, g, :],
                                                        start=(k == 0), stop=(k == KD - 1))
                            ru.fill(last, m)

                def down(i, s):
                    g = 2 * i + s
                    pe.wait_ge(hid_ready, KF * g + KF)
                    for j in range(2):
                        m = 2 * (s % 2) + j
                        gg = i + s // 2
                        rd.wait_free(pe, gg, m)
                        for bb in range(2):
                            b = 2 * j + bb
                            for c in range(KF):
                                last = nc.tensor.matmul(rd.bank(m)[0:T, bb * D:(bb + 1) * D],
                                                        hid[:, s % 2, c, b * T:(b + 1) * T], wd[:, c, :],
                                                        start=(c == 0), stop=(c == KF - 1))
                        rd.fill(last, m)

                up(0, 0)
                with pe.Fori(0, G // 2 - 1) as i:
                    for s in range(2):
                        up(i, s + 1)
                        down(i, s)
                up(G // 2 - 1, 1)
                down(G // 2 - 1, 0)
                down(G // 2 - 1, 1)

            @block.scalar
            def _(act):
                with act.Fori(0, G) as g:
                    for c in range(KF):
                        m = 2 * c
                        ru.wait_filled(act, g, m)
                        if c >= 2:
                            act.wait_ge(hid_ready, KF * g + c - 1)
                        else:
                            act.wait_ge(hid_ready, KF * g)
                        ru.drain(nc.scalar.activation(sg[:, c % 2, :], ru.bank(m)[:, 0:GT], ACT.Silu), m)

            @block.vector
            def _(v):
                def mul(i, s):
                    g = 2 * i + s
                    if not (isinstance(i, int) and i == 0 and s < 2):
                        rd.wait_filled(v, i + s // 2 - 1, 2 * (s % 2) + 1)
                    for c in range(KF):
                        m = 2 * c + 1
                        v.wait_ge(ru.drained[(m - 1) % 4], ru.before(g, m - 1) + 1)
                        ru.wait_filled(v, g, m)
                        ru.drain(nc.vector.tensor_tensor(hid[:, s % 2, c, :], sg[:, c % 2, :], ru.bank(m)[:, 0:GT],
                                                         ALU.mult), m)
                        v.wait_ge(ru.drained[m % 4], ru.before(g, m) + 1)
                        v.sem_inc(hid_ready, 1)

                def add(i, s):
                    g = 2 * i + s
                    for j in range(2):
                        m = 2 * s + j
                        rd.wait_filled(v, i, m)
                        rows = h[:, g, 2 * j:2 * j + 2, :]
                        rd.drain(nc.vector.tensor_tensor(rows, rows, rd.bank(m)[0:T, :].rearrange("p (b d) -> p b d", b=2),
                                                         ALU.add), m)
                    for j in range(2):
                        v.wait_ge(rd.drained[2 * s + j], rd.before(i, 2 * s + j) + 1)
                    v.sem_inc(rows_ready, 1)

                mul(0, 0)
                with v.Fori(0, G // 2 - 1) as i:
                    for s in range(2):
                        mul(i, s + 1)
                        add(i, s)
                mul(G // 2 - 1, 1)
                add(G // 2 - 1, 0)
                add(G // 2 - 1, 1)

            @block.sync
            def _(sp):
                with sp.Fori(0, G) as g:
                    sp.wait_ge(rows_ready, g + 1)
                    sp.dma_start(out[:, bass.ds(GB * g, GB), :], h[:, g]).then_inc(out_stored, 16)
                sp.wait_ge(out_stored, 16 * G)


def final(nc, sem, h, out):
    out_stored = sem("dbg_stored")
    with nc.Block() as block:
        @block.sync
        def _(sp):
            for q in range(4):
                sp.dma_start(out[:, 8 * q:8 * q + 8, :], h[:, 2 * q:2 * q + 2].rearrange("p g b d -> p (g b) d")).then_inc(out_stored, 16)
            sp.wait_ge(out_stored, 64)


def layouts(x, txt, i):
    f = np.float32

    def chunks(m):
        k, n = m.shape
        return m.reshape(k // P, P, n).transpose(1, 0, 2)

    def column(v):
        return v.reshape(-1, P).T

    o = {}
    p = x.reshape(G, GB, 3, 8, 16, 8, 16).transpose(0, 4, 6, 2, 1, 3, 5)
    o["patches"] = p.reshape(G, KP, P, GB * IMG).transpose(0, 2, 1, 3)
    o["txt"] = txt.transpose(1, 0, 2)
    o["wpT"] = chunks(i["L0_tok_Wp"].T)
    o["tokb"] = np.broadcast_to(i["L0_tok_b"], (P, D))
    gh, gw = np.meshgrid(np.arange(8), np.arange(8), indexing="ij")
    quarter = D // 4
    factor = f(10000.0) ** (np.arange(quarter, dtype=f) / f(quarter))
    hh = gh.reshape(-1).astype(f)[:, None] / factor
    ww = gw.reshape(-1).astype(f)[:, None] / factor
    pos = np.concatenate([np.sin(hh), np.cos(hh), np.sin(ww), np.cos(ww)], axis=-1).astype(f)
    o["pos2"] = np.concatenate([pos, pos], axis=0)
    o["ident"] = np.eye(P, dtype=f)
    inv_freq = 1.0 / 10000.0 ** (np.arange(0, DH, 2, dtype=f) / DH)
    freqs = np.outer(np.arange(T, dtype=f), inv_freq)
    cos = np.concatenate([np.cos(freqs), np.cos(freqs)], -1)[:, ::2].astype(f).T
    sin = np.concatenate([np.sin(freqs), np.sin(freqs)], -1)[:, ::2].astype(f).T
    o["ropeC"] = np.concatenate([cos] * 4, axis=0)
    o["ropeS"] = np.concatenate([-sin, sin, -sin, sin], axis=0)
    o["gb"] = np.stack([np.stack([column(i[s]), column(i[t])], 1) for s, t in (
        ("L0_attn_ln_scale", "L0_attn_ln_bias"), ("L0_ffn_ln1_g", "L0_ffn_ln1_b"), ("L0_ffn_ln2_g", "L0_ffn_ln2_b"))], 1)
    n = np.arange(HID).reshape(NH, DH)
    straight = np.concatenate([n[:, 0::2], n[:, 1::2]], 1).reshape(-1)
    swapped = np.concatenate([n[:, 1::2], n[:, 0::2]], 1).reshape(-1)
    o["wdq"] = chunks(i["L0_attn_w_down_q"].T)
    o["wdkv"] = chunks(i["L0_attn_w_down_kv"].T)
    o["wuq"] = i["L0_attn_w_up_q"][straight].T
    o["wuqs"] = i["L0_attn_w_up_q"][swapped].T
    o["wuk"] = i["L0_attn_w_up_k"][straight].T
    o["wuks"] = i["L0_attn_w_up_k"][swapped].T
    o["wuv"] = i["L0_attn_w_up_v"].T
    o["woT"] = chunks(i["L0_attn_w_out"].T)
    for k, s in (("wq2", "Wq"), ("wk2", "Wk"), ("wv2", "Wv"), ("wp2", "Wp")):
        o[k] = chunks(i["L0_ffn_" + s])
    o["bB"] = np.stack([column(i["L0_ffn_" + s]) for s in ("bq", "bk", "bv")], 1)
    o["hmask"] = (np.arange(P)[:, None] // DM == np.arange(HC)[None, :]).astype(f)
    o["bkm"] = np.zeros((P, 1), f)
    o["causal"] = np.where(np.arange(T)[None, :] <= np.arange(T)[:, None], f(0), f(NEG))
    o["tri"] = (np.arange(T)[:, None] < np.arange(T)[None, :]).astype(f)
    o["bpb"] = np.broadcast_to(i["L0_ffn_bp"], (T, D))
    o["gateW"] = chunks(i["L0_ffn_gate_W"])
    o["gateb"] = np.broadcast_to(i["L0_ffn_gate_b"], (T, E))
    o["ids"] = (np.arange(T)[:, None, None] + T * np.arange(B).reshape(1, G, GB)).astype(np.int32)
    o["iota8"] = np.broadcast_to(np.arange(E, dtype=f), (T, E))
    o["iota_t"] = np.broadcast_to(np.arange(TILES, dtype=f), (T, TILES))
    o["W1"] = i["L0_ffn_exp_W1"].reshape(E, KD, P, HID).transpose(2, 0, 1, 3)
    o["W2"] = i["L0_ffn_exp_W2"].reshape(E, KH, P, D).transpose(2, 0, 1, 3)
    o["b1"] = np.broadcast_to(i["L0_ffn_exp_b1"], (P, E, HID))
    o["b2"] = np.broadcast_to(i["L0_ffn_exp_b2"], (P, E, D))
    o["wqk"] = chunks(i["L1_attn_Wqkvg"].T)
    o["wout4"] = chunks(i["L1_attn_Wout"].T)
    o["bias4"] = np.broadcast_to(i["L1_attn_bqkvg"], (T, 4 * D))
    o["bout"] = np.broadcast_to(i["L1_attn_bout"], (T, D))
    s_, t_ = np.arange(T)[:, None], np.arange(T)[None, :]
    lag = np.zeros((P, T + FIELD // P), f)
    lag[0:T, 0:T] = np.maximum(t_ - s_, 0)
    lag[:, T:] = np.arange(FIELD).reshape(FIELD // P, P).T
    o["lag"] = lag
    o["keep"] = (t_ >= s_).astype(f)
    o["pw"] = np.broadcast_to(np.stack([i["L1_attn_wave_frequency"], i["L1_attn_wave_damping"], i["L1_attn_wave_phase"]]),
                              (P, 3, NH))
    o["fc"] = i["L1_attn_field_coupling"]
    o["dmask"] = (np.arange(P)[:, None] % DM == np.arange(DM)[None, :]).astype(f)
    o["wg_i"] = chunks(i["L1_ffn_w_gate"].T)
    o["wu_i"] = chunks(i["L1_ffn_w_up"].T)
    o["wd_i"] = chunks(i["L1_ffn_w_down"].T)
    return {k: np.ascontiguousarray(v) for k, v in o.items()}


UPTO = 9


def kernel(x, txt, **inputs):
    import concourse.bacc as _bacc
    from concourse.bass_utils import run_bass_kernel_spmd as _run

    nc = _bacc.Bacc("TRN2", target_bir_lowering=False, num_devices=1)
    arrays = layouts(np.asarray(x), np.asarray(txt), {k: np.asarray(v) for k, v in inputs.items()})
    aps = {k: nc.dram_tensor("in_" + k, v.shape, mybir.dt.from_np(v.dtype), kind="ExternalInput").ap()
           for k, v in arrays.items()}
    out = nc.dram_tensor("out", (T, B, D), F32, kind="ExternalOutput").ap()
    program(nc, aps, out, UPTO)
    r = _run(nc, [{"in_" + k: v for k, v in arrays.items()}], core_ids=[0])
    return np.ascontiguousarray(r.results[0]["out"].transpose(1, 0, 2))
```

```python
from contextlib import ExitStack

import numpy as np
import concourse.bass as bass
from concourse import mybir

F32 = mybir.dt.float32
BF16 = mybir.dt.bfloat16
I32 = mybir.dt.int32
U32 = mybir.dt.uint32
ALU = mybir.AluOpType
ACT = mybir.ActivationFunctionType
AX_X = mybir.AxisListType.X

P = 128
B = 32
T = 96
IMG = 64
TXT = 32
D = 256
KD = D // P
GB = 4
G = B // GB
GT = GB * T
PATCH = 768
KP = PATCH // P
NH = 16
DH = 64
NCH = NH // 2
DM = 16
HC = P // DM
E = 8
HID = 1024
KH = HID // P
EPS = 1e-5
TOPK = 2
CAP = B * T
TILES = B * T * TOPK // P + E
LIST = (E * CAP + TILES * P + P - 1) // P * P
FFN = 768
KF = FFN // P
FIELD = 512
NEG = -1e30
RING = 4


BIG = 2 * B * D + KD * B * T
PERM = 2700
ARENA = 53200


class Space:

    def __init__(self, arena, at, end):
        self.arena, self.at, self.end = arena, at, end

    def take(self, shape, dt=F32):
        words = int(np.prod(shape[1:]))
        if dt == BF16:
            assert words % 2 == 0
            words //= 2
        v = self.arena[0:shape[0], self.at:self.at + words]
        self.at += words
        assert self.at <= self.end, (self.at, self.end)
        if dt != F32:
            v = v.bitcast(dt)
        if len(shape) > 2:
            names = "abcd"[:len(shape) - 1]
            v = v.rearrange(f"p ({' '.join(names)}) -> p {' '.join(names)}",
                            **{n: k for n, k in zip(names, shape[1:])})
        return v


class Ring:

    def __init__(self, banks, filled, drained, base, per_group, gap=None, late=2, groups=G):
        self.groups = groups
        self.banks, self.filled, self.drained, self.base = banks, filled, drained, base
        self.n, self.per_group, self.gap, self.late = len(banks), per_group, gap, late
        assert per_group % self.n == 0 and late % self.n == 0 or gap is None
        assert gap is None or gap % self.n == 0

    def before(self, g, m, at_end=False):
        late = self.gap is not None and not (isinstance(g, int) and g == 0 and m < self.gap)
        count = self.base[m % self.n] + (self.per_group // self.n) * g + m // self.n - (self.late // self.n if late else 0)
        return count - (self.gap // self.n if at_end else 0)

    def bank(self, m):
        return self.banks[m % self.n]

    def wait_free(self, eng, g, m, at_end=False):
        eng.wait_ge(self.drained[m % self.n], self.before(g, m, at_end))

    def wait_drained(self, eng, g, m):
        eng.wait_ge(self.drained[m % self.n], self.before(g, m) + 1)

    def wait_filled(self, eng, g, m, at_end=False):
        if m < 0 and isinstance(g, int) and g == 0:
            return
        eng.wait_ge(self.filled[m % self.n], self.before(g, m, at_end) + 1)

    def fill(self, ins, m):
        ins.then_inc(self.filled[m % self.n], 1)

    def drain(self, ins, m):
        ins.then_inc(self.drained[m % self.n], 1)

    def end(self):
        return [x + (self.per_group // self.n) * self.groups for x in self.base]


def program(nc, a, out, upto=9):
    top = ExitStack()
    with top:
        arena = top.enter_context(nc.sbuf_tensor("arena", [P, ARENA], F32))

        def sem(name):
            return top.enter_context(nc.semaphore(name))

        banks = [top.enter_context(nc.psum_tensor(f"bank{i}", [P, 512], F32)) for i in range(8)]
        filled = [sem(f"filled{i}") for i in range(8)]
        drained = [sem(f"drained{i}") for i in range(8)]
        count = [0] * 8

        def ring(first, n, per_group, gap=None, late=2, groups=G):
            ids = range(first, first + n)
            r = Ring([banks[i] for i in ids], [filled[i] for i in ids], [drained[i] for i in ids],
                     [count[i] for i in ids], per_group, gap, late, groups)
            for i, c in zip(ids, r.end()):
                count[i] = c
            return r

        big = Space(arena, 0, BIG)
        perm = Space(arena, BIG, BIG + PERM)
        h = big.take([T, G, GB, D])
        xres = big.take([T, G, GB, D])
        hnT = big.take([P, KD, G, GT])
        ident = perm.take([P, P])
        pows = perm.take([T, 3, GB])
        lnT = perm.take([P, KD, GT])
        zz = perm.take([T, GB, D])
        stats = perm.take([T, GB, 6])
        mv = perm.take([T, GB, 2])
        lnw = perm.take([T, 7, GB])
        gb = perm.take([P, 3, 2, KD])

        ln_stat, ln_mean, ln_chain, ln_row, ln_added = (
            sem(n) for n in ("ln_stat", "ln_mean", "ln_chain", "ln_row", "ln_added"))
        ln_out, ln_stored = sem("ln_out"), sem("ln_stored")
        ln_turn, dma_turn, load_turn = (sem(n) for n in ("ln_turn", "dma_turn", "load_turn"))
        const_ready = sem("const_ready")
        made = sem("made")
        out_stored = sem("out_stored")

        ACTS = {"first": (0, True, h), "second": (1, True, h), "third": (2, False, xres)}

        CH = 7

        def ln_vector_stats(src, g, l):
            nc.vector.sem_inc(ln_turn, 1)
            for b in range(GB):
                last = nc.vector.bn_stats(stats[:, b, :], src[:, g, b, :])
            last.then_inc(ln_stat, 1)

        def ln_vector_mean(v, l):
            v.wait_ge(ln_stat, l + 1)
            if not (isinstance(l, int) and l == 0):
                v.wait_ge(ln_chain, CH * l)
            v.sem_inc(ln_turn, 1)
            for b in range(GB):
                last = nc.vector.bn_aggr(mv[:, b, :], stats[:, b, :])
            last.then_inc(ln_mean, 1)

        def ln_pool_rstd(pool, l):
            gp = nc.gpsimd
            var = mv[:, :, 1]
            pool.wait_ge(ln_mean, l + 1)
            pool.wait_ge(ln_row, l)
            w = lnw

            def step(k, ins):
                ins.then_inc(ln_chain, 1)
                pool.wait_ge(ln_chain, CH * l + k)
            step(1, gp.tensor_tensor(w[:, 0, :], var, pows[:, 2, :], ALU.add))
            step(2, gp.tensor_tensor(w[:, 1, :], w[:, 0, :], pows[:, 0, :], ALU.pow))
            step(3, gp.tensor_tensor(w[:, 2, :], w[:, 0, :], pows[:, 1, :], ALU.pow))
            step(4, gp.tensor_tensor(w[:, 3, :], var, w[:, 2, :], ALU.mult))
            step(5, gp.tensor_tensor(w[:, 4, :], w[:, 3, :], pows[:, 2, :], ALU.add))
            step(6, gp.tensor_tensor(w[:, 5, :], w[:, 4, :], pows[:, 0, :], ALU.pow))
            gp.tensor_tensor(w[:, 6, :], w[:, 1, :], w[:, 5, :], ALU.mult).then_inc(ln_chain, 1)

        def ln_vector_rows(v, src, twice, g, l, t_ring, m, at_end=False):
            v.wait_ge(ln_chain, CH * l + CH)
            if not (isinstance(l, int) and l == 0):
                v.wait_ge(ln_out, 2 * l)
            v.wait_ge(ln_added, l)
            for b in range(GB):
                if twice:
                    nc.vector.tensor_scalar(xres[:, g, b, :], src[:, g, b, :], mv[:, b, 0:1], lnw[:, 1, b:b + 1],
                                            ALU.subtract, ALU.mult)
                r = lnw[:, 6 if twice else 1, b:b + 1]
                last = nc.vector.tensor_scalar(zz[:, b, :], src[:, g, b, :], mv[:, b, 0:1], r,
                                               ALU.subtract, ALU.mult)
            last.then_inc(ln_row, 1)

        def ln_pool_add(pool, add, g, l):
            pool.wait_ge(ln_row, l + 1)
            if add:
                nc.gpsimd.tensor_tensor(h[:, g, :, :], h[:, g, :, :], xres[:, g, :, :], ALU.add).then_inc(ln_added, 1)
            else:
                pool.sem_inc(ln_added, 1)

        def ln_tensor(pe, r, g, l, m, at_end=False):
            pe.wait_ge(ln_row, l + 1)
            for k in range(KD):
                r.wait_free(pe, g, m + k, at_end)
                for b in range(GB):
                    last = nc.tensor.transpose(r.bank(m + k)[:, b * T:(b + 1) * T], zz[:, b, k * P:(k + 1) * P],
                                               ident[0:T, 0:T])
                r.fill(last, m + k)

        def ln_scalar(act, r, g, l, m, which, dst_g, at_end=False):
            if not (isinstance(l, int) and l == 0):
                act.wait_ge(ln_stored, 16 * l)
            for k in range(KD):
                r.wait_filled(act, g, m + k, at_end)
                if which is None:
                    ins = nc.scalar.activation(lnT[:, k, :], r.bank(m + k)[:, 0:GT], ACT.Identity)
                else:
                    ins = nc.scalar.activation(lnT[:, k, :], r.bank(m + k)[:, 0:GT], ACT.Identity,
                                               bias=gb[:, which, 1, k:k + 1], scale=gb[:, which, 0, k:k + 1])
                r.drain(ins, m + k)
                act.wait_ge(r.drained[(m + k) % r.n], r.before(g, m + k, at_end) + 1)
                act.sem_inc(ln_out, 1)
            act.dma_start(hnT[:, :, dst_g, :], lnT[:]).then_inc(ln_stored, 16)

        with ExitStack() as ph:
            work = Space(arena, BIG + PERM, ARENA)
            wpT = work.take([P, KP, D])
            posb = work.take([P, D])
            tokb = work.take([P, D])
            patches = work.take([P, 2, KP, GB * IMG])
            x_loaded = [sem(f"x_loaded{i}") for i in range(2)]
            tok_rows = sem("tok_rows")
            r = ring(0, 4, 4)
            block = nc.Block()
            with block:
                @block.sync
                def _(sp):
                    for n, (dst, src) in enumerate([
                            (wpT, "wpT"), (posb, "pos2"), (tokb, "tokb"), (ident, "ident"), (gb, "gb")]):
                        src = a[src]
                        sp.dma_start(dst[:], src).then_inc(const_ready, 16)
                    sp.dma_start(h[IMG:T].rearrange("p g b d -> p (g b) d"), a["txt"]).then_inc(const_ready, 16)
                    with sp.Fori(0, G // 2) as i:
                        for s in range(2):
                            sp.wait_ge(filled[1], 2 * i)
                            sp.dma_start(patches[:, s], a["patches"][2 * i + s]).then_inc(x_loaded[s], 16)

                @block.tensor
                def _(pe):
                    pe.wait_ge(const_ready, 96)
                    with pe.Fori(0, G // 2) as i:
                        for s in range(2):
                            g = 2 * i + s
                            pe.wait_ge(x_loaded[s], 16 * i + 16)
                            for p in range(2):
                                r.wait_free(pe, g, p)
                                for k in range(KP):
                                    last = nc.tensor.matmul(r.bank(p)[:, 0:D], patches[:, s, k, p * P:(p + 1) * P],
                                                            wpT[:, k, :], start=(k == 0), stop=(k == KP - 1))
                                r.fill(last, p)
                        for s in range(2):
                            g = 2 * i + s
                            ln_tensor(pe, r, g, g, 2)

                @block.vector
                def _(v):
                    v.wait_ge(const_ready, 96)
                    nc.vector.memset(pows[:, 0, :], -0.5)
                    nc.vector.memset(pows[:, 2, :], EPS)
                    nc.vector.memset(pows[:, 1, :], -1.0).then_inc(made, 1)
                    nc.vector.tensor_tensor(posb[:], posb[:], tokb[:], ALU.add).then_inc(made, 1)
                    v.wait_ge(made, 2)
                    with v.Fori(0, G // 2) as i:
                        for s in range(2):
                            g = 2 * i + s
                            for p in range(2):
                                r.wait_filled(v, g, p)
                                for j in range(2):
                                    rows = slice(j * IMG, (j + 1) * IMG)
                                    last = nc.vector.tensor_tensor(h[0:IMG, g, 2 * p + j, :], r.bank(p)[rows, 0:D],
                                                                   posb[rows, :], ALU.add)
                                r.drain(last, p)
                            v.wait_ge(r.drained[1], r.before(g, 1) + 1)
                            ln_vector_stats(h, g, g)
                            ln_vector_mean(v, g)
                            ln_vector_rows(v, h, True, g, g, r, 2)

                @block.gpsimd
                def _(pool):
                    pool.wait_ge(made, 1)
                    with pool.Fori(0, G) as g:
                        ln_pool_rstd(pool, g)
                        ln_pool_add(pool, True, g, g)

                @block.scalar
                def _(act):
                    act.wait_ge(const_ready, 96)
                    with act.Fori(0, G) as g:
                        ln_scalar(act, r, g, g, 2, 0, g)
                    act.wait_ge(ln_stored, 16 * G)

        att_max, att_sum, att_inv, att_norm, att_T = (
            sem(n) for n in ("att_max", "att_sum", "att_inv", "att_norm", "att_T"))
        both = Space(arena, BIG + PERM, ARENA)
        prob = both.take([T, RING, GB, T])
        probT = both.take([T, RING, GT])
        mx = both.take([T, RING, GB])
        sm = both.take([T, RING, GB])
        inv = both.take([T, RING, GB])

        def attention_vector_max(v, rs, seq, g, n):
            rs.wait_filled(v, g, n)
            sc = rs.bank(n)[0:T, 0:GT].rearrange("p (b k) -> p b k", b=GB)
            nc.vector.tensor_reduce(mx[:, n % RING, :], sc, AX_X, ALU.max, negate=True).then_inc(att_max, 1)

        def attention_scalar_exp(act, rs, rt, seq, g, n):
            s = n % RING
            act.wait_ge(att_max, seq(g, n) + 1)
            rt.wait_filled(act, g, n - RING)
            for b in range(GB):
                last = nc.scalar.activation(prob[:, s, b, :], rs.bank(n)[0:T, b * T:(b + 1) * T], ACT.Exp,
                                            bias=mx[:, s, b:b + 1])
            rs.drain(last, n)

        def attention_vector_sum(v, rs, seq, g, n):
            s = n % RING
            rs.wait_drained(v, g, n)
            nc.vector.tensor_reduce(sm[:, s, :], prob[:, s], AX_X, ALU.add).then_inc(att_sum, 1)
            v.wait_ge(att_sum, seq(g, n) + 1)
            nc.vector.reciprocal(inv[:, s, :], sm[:, s, :]).then_inc(att_inv, 1)

        def attention_pool_norm(pool, seq, g, n):
            s = n % RING
            pool.wait_ge(att_inv, seq(g, n) + 1)
            nc.gpsimd.tensor_tensor(prob[:, s], prob[:, s], inv[:, s, :].unsqueeze(2).broadcast_to([T, GB, T]),
                                    ALU.mult).then_inc(att_norm, 1)

        def attention_tensor_T(pe, rt, seq, g, n):
            s = n % RING
            pe.wait_ge(att_norm, seq(g, n) + 1)
            rt.wait_free(pe, g, n)
            for b in range(GB):
                last = nc.tensor.transpose(rt.bank(n)[0:T, b * T:(b + 1) * T], prob[:, s, b, :], ident[0:T, 0:T])
            rt.fill(last, n)

        def attention_scalar_T(act, rt, seq, g, n, pair):
            rt.wait_filled(act, g, n)
            pair((n - RING) // 2)
            nc.scalar.activation(probT[:, n % RING, :], rt.bank(n)[0:T, 0:GT], ACT.Copy).then_inc(att_T, 1)
            act.wait_ge(att_T, seq(g, n) + 1)
            act.sem_inc(rt.drained[n % rt.n], 1)

        rows_d = nc.dram_tensor("norm_rows", (B * T, D), F32, kind="Internal").ap()
        h_d = nc.dram_tensor("stream_rows", (G, T, GB * D), F32, kind="Internal").ap()
        list_d = nc.dram_tensor("token_list", (LIST, 1), I32, kind="Internal").ap()
        y_d = nc.dram_tensor("expert_rows", (TILES * P, D), F32, kind="Internal").ap()

        if upto < 1:
            final(nc, sem, h, out)
            return

        wB = {n: both.take([P, KD, D]) for n in ("wq2", "wk2", "wv2", "wp2")}
        bB = both.take([P, 3, KD])
        wB_loaded = sem("wB_loaded")
        with ExitStack() as ph:
            work = Space(arena, both.at, ARENA)
            w = {n: work.take(s) for n, s in (
                ("wdq", [P, KD, P]), ("wdkv", [P, KD, P]), ("wuq", [P, HID]), ("wuqs", [P, HID]),
                ("wuk", [P, HID]), ("wuks", [P, HID]), ("wuv", [P, HID]), ("woT", [P, NCH, D]),
                ("ropeC", [P, T]), ("ropeS", [P, T]), ("ropeCq", [P, T]), ("ropeSq", [P, T]))}
            cq = work.take([P, GT])
            ckv = work.take([P, GT])
            V = work.take([T, GB, HID])
            qprod = work.take([P, 2, GT])
            kprod = work.take([P, 2, GT])
            qrot = work.take([P, 2, GT])
            krot = work.take([P, 2, 2, GT])
            oT = work.take([P, NCH, GT])
            w1_loaded, down, q_rot, k_rot, o_cols, z_made = (
                sem(n) for n in ("w1_loaded", "down", "q_rot", "k_rot", "o_cols", "z_made"))
            LT, LAV = 3, 4
            LN_STEP = 8
            LN_M = 2 * LN_STEP
            START_M = 4 * (NCH - 2) + 2
            N_START = 2 + 8 + 2 * GB
            ra = ring(0, 2, N_START, groups=1)
            rp = ring(0, 2, START_M + N_START + 2, LN_M)
            for bank in range(2):
                count[bank] -= N_START // 2
            rs = ring(2, 2, NH)
            rt = ring(4, 2, NH)
            rv = ring(6, 2, NCH)
            OUT_M, OUT_LAST = START_M + N_START, START_M

            def start_items(g, first):
                return (ra, 0, 0) if first else (rp, g - 1, START_M)

            def proj_item(g, c, i, first):
                if c < 2:
                    r_, gg, m0 = start_items(g, first)
                    return r_, gg, m0 + 2 + 4 * c + i
                m = 4 * (c - 2) + i
                return rp, g, m if m < LN_M else m + 2

            def seq(g, n):
                return NH * g + n

            block = nc.Block()
            with block:
                @block.sync
                def _(sp):
                    for n in w:
                        sp.dma_start(w[n][:], a[n]).then_inc(w1_loaded, 16)
                    for n in wB:
                        sp.dma_start(wB[n][:], a[n]).then_inc(wB_loaded, 16)
                    sp.dma_start(bB[:], a["bB"]).then_inc(wB_loaded, 16)
                    sp.wait_ge(w1_loaded, 16 * len(w))
                    sp.wait_ge(wB_loaded, 16 * len(wB) + 16)

                @block.tensor
                def _(pe):
                    def proj(g, c, i, first):
                        r_, gg, m = proj_item(g, c, i, first)
                        r_.wait_free(pe, gg, m)
                        lhsT = w[("wuq", "wuqs", "wuk", "wuks")[i]][:, c * P:(c + 1) * P]
                        r_.fill(nc.tensor.matmul(r_.bank(m)[:, 0:GT], lhsT, (cq, cq, ckv, ckv)[i][:],
                                                 start=True, stop=True), m)

                    def scores(g, n):
                        c, hh = n // 2, n % 2
                        if hh == 0:
                            pe.wait_ge(q_rot, NCH * g + c + 1)
                            pe.wait_ge(k_rot, NCH * g + c + 1)
                        rs.wait_free(pe, g, n)
                        for b in range(GB):
                            cols = slice(b * T, (b + 1) * T)
                            last = nc.tensor.matmul(rs.bank(n)[0:T, cols], qrot[:, c % 2, cols],
                                                    krot[:, c % 2, hh, cols], start=True, stop=True)
                        rs.fill(last, n)

                    def values(g, c):
                        rv.wait_free(pe, g, c)
                        pe.wait_ge(att_T, seq(g, 2 * c + 1) + 1)
                        for hh in range(2):
                            n = 2 * c + hh
                            for b in range(GB):
                                last = nc.tensor.matmul(
                                    rv.bank(c)[hh * DH:(hh + 1) * DH, b * T:(b + 1) * T],
                                    V[:, b, n * DH:(n + 1) * DH], probT[:, n % RING, b * T:(b + 1) * T],
                                    start=True, stop=True)
                        rv.fill(last, c)

                    def start(g, first, between):
                        r_, gg, m0 = start_items(g, first)
                        for j, name in enumerate(("wdq", "wdkv")):
                            r_.wait_free(pe, gg, m0 + j)
                            for k in range(KD):
                                last = nc.tensor.matmul(r_.bank(m0 + j)[:, 0:GT], w[name][:, k, :], hnT[:, k, g, :],
                                                        start=(k == 0), stop=(k == KD - 1))
                            r_.fill(last, m0 + j)
                        between(0)
                        pe.wait_ge(down, 2 * g + 2)
                        for c in range(2):
                            for i in range(4):
                                proj(g, c, i, first)
                            between(1 + c)
                        between(3)
                        for b in range(GB):
                            for f in range(2):
                                m = m0 + 10 + 2 * b + f
                                r_.wait_free(pe, gg, m)
                                r_.fill(nc.tensor.matmul(r_.bank(m)[0:T, 0:512], ckv[:, b * T:(b + 1) * T],
                                                         w["wuv"][:, f * 512:(f + 1) * 512], start=True, stop=True), m)
                        scores(g, 0)

                    def lagging(g, n):
                        if 0 <= n - LT < NH:
                            attention_tensor_T(pe, rt, seq, g, n - LT)
                        if 0 <= n - LAV < NH and (n - LAV) % 2 == 1:
                            values(g, (n - LAV) // 2)

                    def body(g, norm, more):
                        for n in range(NH):
                            if n == LN_STEP and norm:
                                ln_tensor(pe, rp, g, G + g - 1, LN_M)
                            if n + 1 < NH:
                                scores(g, n + 1)
                            if n // 2 + 2 < NCH:
                                for i in range(2):
                                    proj(g, n // 2 + 2, 2 * (n % 2) + i, False)
                            lagging(g, n)

                        if more:
                            start(g + 1, False, lambda k: lagging(g, NH + k))
                        else:
                            for k in range(4):
                                lagging(g, NH + k)
                        pe.wait_ge(o_cols, NCH * g + NCH)
                        m0 = OUT_M if more else OUT_LAST
                        for j in range(2):
                            m = m0 + j
                            rp.wait_free(pe, g, m)
                            for bb in range(2):
                                b = 2 * j + bb
                                for c in range(NCH):
                                    last = nc.tensor.matmul(rp.bank(m)[0:T, bb * D:(bb + 1) * D],
                                                            oT[:, c, b * T:(b + 1) * T], w["woT"][:, c, :],
                                                            start=(c == 0), stop=(c == NCH - 1))
                            rp.fill(last, m)

                    pe.wait_ge(w1_loaded, 16 * len(w))
                    pe.wait_ge(z_made, 1)
                    start(0, True, lambda k: None)
                    body(0, False, True)
                    with pe.Fori(1, G - 1) as g:
                        body(g, True, True)
                    body(G - 1, True, False)
                    ln_tensor(pe, rp, G - 1, 2 * G - 1, OUT_LAST + 2)

                @block.vector
                def _(v):
                    def rope(g, c, i, first):
                        prod = (qprod, kprod)[i]
                        if not (first and c == 0):
                            v.wait_ge((q_rot, k_rot)[i], NCH * g + c)
                        for j, table in enumerate((("ropeCq", "ropeSq"), ("ropeC", "ropeS"))[i]):
                            r_, gg, m = proj_item(g, c, 2 * i + j, first)
                            r_.wait_filled(v, gg, m)
                            ins = nc.vector.tensor_tensor(
                                prod[:, j, :].rearrange("p (b t) -> p b t", b=GB),
                                r_.bank(m)[:, 0:GT].rearrange("p (b t) -> p b t", b=GB),
                                w[table][:].unsqueeze(1).broadcast_to([P, GB, T]), ALU.mult)
                            r_.drain(ins, m)
                        if i == 1:
                            for j in range(2):
                                r_, gg, m = proj_item(g, c, 2 * i + j, first)
                                r_.wait_drained(v, gg, m)
                            if not (first and c < 2):
                                rs.wait_filled(v, g, 2 * (c - 2) + 1)
                            for hh in range(2):
                                rows = slice(hh * DH, (hh + 1) * DH)
                                last = nc.vector.tensor_tensor(krot[rows, c % 2, hh, :], kprod[rows, 0, :],
                                                               kprod[rows, 1, :], ALU.add)
                            last.then_inc(k_rot, 1)

                    def start(g, first):
                        for c in range(2):
                            for i in range(2):
                                rope(g, c, i, first)
                        attention_vector_max(v, rs, seq, g, 0)

                    def body(g, norm, more):
                        for n in range(NH):
                            if norm and n == 1:
                                ln_vector_stats(h, g - 1, G + g - 1)
                            if norm and n == 2:
                                ln_vector_mean(v, G + g - 1)
                            if norm and n == 5:
                                ln_vector_rows(v, h, True, g - 1, G + g - 1, rp, LN_M)
                            if n + 1 < NH:
                                attention_vector_max(v, rs, seq, g, n + 1)
                            if n // 2 + 2 < NCH:
                                rope(g, n // 2 + 2, n % 2, False)
                            attention_vector_sum(v, rs, seq, g, n)
                        if more:
                            start(g + 1, False)
                        m0 = OUT_M if more else OUT_LAST
                        for j in range(2):
                            m = m0 + j
                            rp.wait_filled(v, g, m)
                            rows = h[:, g, 2 * j:2 * j + 2, :]
                            rp.drain(nc.vector.tensor_tensor(
                                rows, rows, rp.bank(m)[0:T, :].rearrange("p (b d) -> p b d", b=2), ALU.add), m)
                        for j in range(2):
                            rp.wait_drained(v, g, m0 + j)

                    nc.vector.memset(krot[:], 0.0).then_inc(z_made, 1)
                    v.wait_ge(z_made, 1)
                    v.wait_ge(w1_loaded, 16 * len(w))
                    v.wait_ge(ln_added, G)
                    start(0, True)
                    body(0, False, True)
                    with v.Fori(1, G - 1) as g:
                        body(g, True, True)
                    body(G - 1, True, False)
                    l = 2 * G - 1
                    ln_vector_stats(h, G - 1, l)
                    ln_vector_mean(v, l)
                    ln_vector_rows(v, h, True, G - 1, l, rp, LN_M)

                @block.gpsimd
                def _(pool):
                    def add_q(g, c, first):
                        for j in range(2):
                            r_, gg, m = proj_item(g, c, j, first)
                            r_.wait_drained(pool, gg, m)
                        if not (first and c < 2):
                            rs.wait_filled(pool, g, 2 * (c - 2) + 1)
                        nc.gpsimd.tensor_tensor(qrot[:, c % 2, :], qprod[:, 0, :], qprod[:, 1, :],
                                                ALU.add).then_inc(q_rot, 1)

                    def start(g, first):
                        add_q(g, 0, first)
                        add_q(g, 1, first)

                    def body(g, norm, more):
                        for n in range(NH):
                            if n % 2 == 0 and n // 2 + 2 < NCH:
                                add_q(g, n // 2 + 2, False)
                            if norm and n == 3:
                                ln_pool_rstd(pool, G + g - 1)
                            if norm and n == 7:
                                ln_pool_add(pool, False, g - 1, G + g - 1)
                            attention_pool_norm(pool, seq, g, n)
                        if more:
                            start(g + 1, False)

                    start(0, True)
                    body(0, False, True)
                    with pool.Fori(1, G - 1) as g:
                        body(g, True, True)
                    body(G - 1, True, False)
                    ln_pool_rstd(pool, 2 * G - 1)
                    ln_pool_add(pool, False, G - 1, 2 * G - 1)

                @block.scalar
                def _(act):
                    def lagging(g, n):
                        if 0 <= n - LT < NH:
                            attention_scalar_T(act, rt, seq, g, n - LT, lambda c: rv.wait_filled(act, g, c))
                        if 0 <= n - LAV < NH and (n - LAV) % 2 == 1:
                            c = (n - LAV) // 2
                            rv.wait_filled(act, g, c)
                            rv.drain(nc.scalar.activation(oT[:, c, :], rv.bank(c)[:, 0:GT], ACT.Copy), c)
                            rv.wait_drained(act, g, c)
                            act.sem_inc(o_cols, 1)

                    def start(g, first, between):
                        r_, gg, m0 = start_items(g, first)
                        for j, dst in enumerate((cq, ckv)):
                            r_.wait_filled(act, gg, m0 + j)
                            r_.drain(nc.scalar.activation(dst[:], r_.bank(m0 + j)[:, 0:GT], ACT.Copy), m0 + j)
                            r_.wait_drained(act, gg, m0 + j)
                            act.sem_inc(down, 1)
                        for k in range(4):
                            between(k)
                        for b in range(GB):
                            for f in range(2):
                                m = m0 + 10 + 2 * b + f
                                r_.wait_filled(act, gg, m)
                                r_.drain(nc.scalar.activation(V[:, b, f * 512:(f + 1) * 512],
                                                              r_.bank(m)[0:T, 0:512], ACT.Copy), m)
                        attention_scalar_exp(act, rs, rt, seq, g, 0)

                    def body(g, norm, more):
                        for n in range(NH):
                            if norm and n == LN_STEP:
                                ln_scalar(act, rp, g, G + g - 1, LN_M, 1, g - 1)
                            if norm and n == LAV + 1:
                                rp.wait_filled(act, g - 1, OUT_M + 1)
                            if n + 1 < NH:
                                attention_scalar_exp(act, rs, rt, seq, g, n + 1)
                            lagging(g, n)
                        if more:
                            start(g + 1, False, lambda k: lagging(g, NH + k))
                        else:
                            for k in range(4):
                                lagging(g, NH + k)

                    act.wait_ge(w1_loaded, 16 * len(w))
                    start(0, True, lambda k: None)
                    body(0, False, True)
                    with act.Fori(1, G - 1) as g:
                        body(g, True, True)
                    body(G - 1, True, False)
                    ln_scalar(act, rp, G - 1, 2 * G - 1, OUT_LAST + 2, 1, G - 1)
                    act.wait_ge(ln_stored, 16 * 2 * G)

        if upto < 2:
            final(nc, sem, h, out)
            return

        rank = perm.take([T, G, GB, TOPK])
        expert = perm.take([T, G, GB, TOPK])
        weight = perm.take([T, G, GB, TOPK])
        total = perm.take([T, E])
        iota8 = perm.take([T, E])
        place_i = perm.take([T, G, GB, TOPK], I32)
        tile_e = perm.take([T, TILES], I32)
        tile_at = perm.take([T, TILES], I32)
        iota_t = perm.take([T, TILES])
        with ExitStack() as ph:
            work = Space(arena, both.at, ARENA)
            slab = work.take([P, KD, GT])
            qT = work.take([P, KD, GT])
            kT = work.take([P, KD, GT])
            kmask = work.take([P, 2, GT])
            V2 = work.take([T, GB, NCH, 2, 2 * DM])
            yT = work.take([P, KD, GT])
            c2 = {n: work.take(sh) for n, sh in (
                ("hmask", [P, HC]), ("causal", [T, T]), ("bpb", [T, D]),
                ("gateW", [P, KD, E]), ("gateb", [T, E]), ("tri", [T, T]))}
            ones = work.take([T, T])
            ids = work.take([T, G, GB], I32)
            ids_g = work.take([T, GB], I32)
            identb = work.take([T, T], BF16)
            causalb = work.take([T, GB, T], BF16)
            lg = work.take([T, GB, E])
            best = work.take([T, GB, 8])
            topi = work.take([T, GB, 8], U32)
            gap = work.take([T, GB])
            ew = work.take([T, GB])
            den = work.take([T, GB])
            oh = work.take([T, TOPK, GB, E])
            ohs = work.take([T, GB, E])
            tot = work.take([T, GB, E])
            base = work.take([T, GB, E])
            rk = work.take([T, GB, E])
            picked = work.take([T, TOPK, GB, E])
            pos = work.take([T, GB, TOPK], I32)
            zeros_i = work.take([P, LIST // P])
            (w2_loaded, slab_loaded, q_ready, k_ready, kmasked, y_cols, bp_added, zz_stored, h_stored,
             gate_lg, gate_chain, gate_gap, gate_exp, gate_oh, pos_ready, scattered, list_zero, projected, t2) = (
                sem(n) for n in (
                    "w2_loaded", "slab_loaded", "q_ready", "k_ready", "kmasked", "y_cols", "bp_added",
                    "zz_stored", "h_stored", "gate_lg", "gate_chain", "gate_gap", "gate_exp", "gate_oh",
                    "pos_ready", "scattered", "list_zero", "projected", "t2"))
            places_free = sem("places_free")
            LN_M, GATE_M, START_M, N_START = 0, 2, 4, 6
            LN2_STEP, GATE1_STEP, GATE2_STEP = 5, 8, 12
            OUT_M, OUT_LAST = START_M + N_START, START_M
            ra = ring(0, 2, N_START, groups=1)
            rp = ring(0, 2, START_M + N_START + 2, 0, 4)
            for bank in range(2):
                count[bank] += (4 - 4 - N_START) // 2
            rs = ring(2, 2, NH)
            rt = ring(4, 2, NH)
            rv = ring(6, 2, NCH)

            def start_items(g, first):
                return (ra, 0, 0) if first else (rp, g - 1, START_M)

            def norm_items(g, last):
                return (rp, g, OUT_LAST + 2) if last else (rp, g + 1, 0)

            n_pairs = NCH // KD

            def pair_item(j):
                return 2 * (j % n_pairs) + j // n_pairs

            GC = 15

            def seq2(g, n):
                return NH * (G + g) + n

            def norm_index(g):
                return 2 * G + g

            block = nc.Block()
            with block:
                @block.sync
                def _(sp):
                    n_small = len(c2) + 3
                    for n in c2:
                        sp.dma_start(c2[n], a[n]).then_inc(w2_loaded, 16)
                    sp.dma_start(ids, a["ids"]).then_inc(w2_loaded, 16)
                    sp.dma_start(iota8, a["iota8"]).then_inc(w2_loaded, 16)
                    sp.dma_start(iota_t, a["iota_t"]).then_inc(w2_loaded, 16)
                    sp.wait_ge(t2, 1)
                    sp.dma_start(list_d.rearrange("(p n) o -> p (n o)", p=P), zeros_i.bitcast(I32)).then_inc(
                        list_zero, 16)

                    def after(g):
                        sp.wait_ge(ln_row, norm_index(g) + 1)
                        sp.dma_start(rows_d.rearrange("(g b p) d -> g p b d", b=GB, p=T)[g], zz[:]).then_inc(zz_stored, 16)
                        sp.wait_ge(ln_added, norm_index(g) + 1)
                        sp.dma_start(h_d[g], h[:, g].rearrange("p b d -> p (b d)")).then_inc(h_stored, 16)

                    sp.sem_inc(zz_stored, 1)
                    sp.dma_start(slab, hnT[:, :, 0, :]).then_inc(slab_loaded, 16)
                    sp.wait_ge(projected, 1)
                    sp.dma_start(slab, hnT[:, :, 1, :]).then_inc(slab_loaded, 16)
                    with sp.Fori(1, G - 1) as g:
                        after(g - 1)
                        sp.wait_ge(projected, g + 1)
                        sp.dma_start(slab, hnT[:, :, g + 1, :]).then_inc(slab_loaded, 16)
                    after(G - 2)
                    after(G - 1)
                    sp.wait_ge(zz_stored, 16 * G + 1)
                    sp.wait_ge(h_stored, 16 * G)

                @block.tensor
                def _(pe):
                    def scores(g, n):
                        pe.wait_ge(kmasked, NH * g + n + 1)
                        rs.wait_free(pe, g, n)
                        nc.tensor.matmul(rs.bank(n)[0:T, 0:GT], identb, causalb.rearrange("p b k -> p (b k)"),
                                         start=True, stop=False)
                        for b in range(GB):
                            cols = slice(b * T, (b + 1) * T)
                            last = nc.tensor.matmul(rs.bank(n)[0:T, cols], qT[:, n // HC, cols],
                                                    kmask[:, n % 2, cols], start=False, stop=(b == GB - 1))
                        rs.fill(last, n)

                    def values(g, j):
                        m = 2 * j // HC
                        if 2 * j % HC == 0:
                            rv.wait_free(pe, g, pair_item(j))
                        pe.wait_ge(att_T, seq2(g, 2 * j + 1) + 1)
                        quad = (j % (HC // 2)) * 2 * DM
                        for b in range(GB):
                            for hh in range(2):
                                n = 2 * j + hh
                                last = nc.tensor.matmul(
                                    rv.banks[m][quad:quad + 2 * DM, b * T:(b + 1) * T], V2[:, b, j, hh, :],
                                    probT[:, n % RING, b * T:(b + 1) * T], start=(hh == 0), stop=(hh == 1))
                        rv.fill(last, pair_item(j))

                    def gate(g, last_):
                        pe.wait_ge(ln_out, 2 * norm_index(g) + 2)
                        _, gg, m0 = norm_items(g, last_)
                        m = m0 + 2
                        rp.wait_free(pe, gg, m)
                        for b in range(GB):
                            for k in range(KD):
                                last = nc.tensor.matmul(rp.bank(m)[0:T, b * E:(b + 1) * E],
                                                        lnT[:, k, b * T:(b + 1) * T], c2["gateW"][:, k, :],
                                                        start=(k == 0), stop=(k == KD - 1))
                        rp.fill(last, m)

                    def prefix(g, last_):
                        pe.wait_ge(gate_oh, g + 1)
                        _, gg, m0 = norm_items(g, last_)
                        m = m0 + 3
                        rp.wait_free(pe, gg, m)
                        cols = ohs.rearrange("p b e -> p (b e)")
                        nc.tensor.matmul(rp.bank(m)[0:T, 0:GB * E], c2["tri"], cols, start=True, stop=True)
                        rp.fill(nc.tensor.matmul(rp.bank(m)[0:T, GB * E:2 * GB * E], ones, cols, start=True, stop=True), m)

                    def lagging(g, n):
                        if 0 <= n - LT < NH:
                            attention_tensor_T(pe, rt, seq2, g, n - LT)
                        if 0 <= n - LAV < NH and (n - LAV) % 2 == 1:
                            values(g, (n - LAV) // 2)

                    def start(g, first, between):
                        r_, gg, m0 = start_items(g, first)
                        pe.wait_ge(slab_loaded, 16 * g + 16)
                        for m in range(4):
                            r_.wait_free(pe, gg, m0 + m)
                            for k in range(KD):
                                last = nc.tensor.matmul(r_.bank(m)[:, 0:GT],
                                                        wB[("wq2", "wk2")[m // 2]][:, k, (m % 2) * P:(m % 2 + 1) * P],
                                                        slab[:, k, :], start=(k == 0), stop=(k == KD - 1))
                            r_.fill(last, m0 + m)
                            between(m)
                        for j in range(2):
                            r_.wait_free(pe, gg, m0 + 4 + j)
                            for bb in range(2):
                                b = 2 * j + bb
                                for k in range(KD):
                                    last = nc.tensor.matmul(r_.bank(4 + j)[0:T, bb * D:(bb + 1) * D],
                                                            slab[:, k, b * T:(b + 1) * T], wB["wv2"][:, k, :],
                                                            start=(k == 0), stop=(k == KD - 1))
                            r_.fill(last, m0 + 4 + j)
                        r_.wait_filled(pe, gg, m0 + 5)
                        pe.sem_inc(projected, 1)
                        pe.wait_ge(q_ready, KD * g + KD)
                        scores(g, 0)

                    def body(g, norm, more):
                        for n in range(NH):
                            if norm and n == LN2_STEP:
                                ln_tensor(pe, rp, g, norm_index(g - 1), LN_M)
                            if norm and n == GATE1_STEP:
                                gate(g - 1, False)
                            if norm and n == GATE2_STEP:
                                prefix(g - 1, False)
                            if n + 1 < NH:
                                scores(g, n + 1)
                            lagging(g, n)
                        if more:
                            start(g + 1, False, lambda k: lagging(g, NH + k))
                        else:
                            for k in range(4):
                                lagging(g, NH + k)
                        pe.wait_ge(y_cols, KD * g + KD)
                        m0 = OUT_M if more else OUT_LAST
                        for j in range(2):
                            m = m0 + j
                            rp.wait_free(pe, g, m)
                            for bb in range(2):
                                b = 2 * j + bb
                                for k in range(KD):
                                    last = nc.tensor.matmul(rp.bank(m)[0:T, bb * D:(bb + 1) * D],
                                                            yT[:, k, b * T:(b + 1) * T], wB["wp2"][:, k, :],
                                                            start=(k == 0), stop=(k == KD - 1))
                            rp.fill(last, m)

                    pe.wait_ge(w2_loaded, 16 * (len(c2) + 3))
                    pe.wait_ge(t2, 4)
                    start(0, True, lambda k: None)
                    body(0, False, True)
                    with pe.Fori(1, G - 1) as g:
                        body(g, True, True)
                    body(G - 1, True, False)
                    ln_tensor(pe, rp, G - 1, norm_index(G - 1), OUT_LAST + 2)
                    gate(G - 1, True)
                    prefix(G - 1, True)

                @block.vector
                def _(v):
                    def mask_keys(g, n):
                        if n % HC == 0:
                            v.wait_ge(k_ready, KD * g + n // HC + 1)
                        if not (n < 2 and isinstance(g, int) and g == 0):
                            rs.wait_filled(v, g, n - 2)
                        nc.vector.tensor_scalar(kmask[:, n % 2, :], kT[:, n // HC, :], c2["hmask"][:, n % HC:n % HC + 1],
                                                None, ALU.mult).then_inc(kmasked, 1)

                    def gate_top(g, last_):
                        _, gg, m0 = norm_items(g, last_)
                        m = m0 + 2
                        rp.wait_filled(v, gg, m)
                        rp.drain(nc.vector.tensor_tensor(
                            lg, rp.bank(m)[0:T, 0:GB * E].rearrange("p (b e) -> p b e", b=GB),
                            c2["gateb"].unsqueeze(1).broadcast_to([T, GB, E]), ALU.add), m)
                        rp.wait_drained(v, gg, m)
                        v.sem_inc(ln_turn, 1)
                        for b in range(GB):
                            last = nc.vector.max(best[:, b, :], lg[:, b, :])
                        last.then_inc(gate_lg, 1)
                        v.wait_ge(gate_lg, 2 * g + 1)
                        v.sem_inc(ln_turn, 1)
                        for b in range(GB):
                            last = nc.vector.max_index(topi[:, b, :], best[:, b, :], lg[:, b, :])
                        last.then_inc(gate_lg, 1)
                        nc.vector.tensor_tensor(gap, best[:, :, 1], best[:, :, 0], ALU.subtract).then_inc(gate_gap, 1)
                        v.wait_ge(gate_lg, 2 * g + 2)
                        ex = expert[:, g]
                        chain(v, g, 1, nc.vector.tensor_copy(ex, topi[:, :, 0:TOPK]))
                        for k in range(TOPK):
                            last = nc.vector.tensor_tensor(
                                oh[:, k], iota8.unsqueeze(1).broadcast_to([T, GB, E]),
                                expert[:, g, :, k].unsqueeze(2).broadcast_to([T, GB, E]), ALU.is_equal)
                        chain(v, g, 2, last)
                        nc.vector.tensor_tensor(ohs, oh[:, 0], oh[:, 1], ALU.add).then_inc(gate_oh, 1)

                    def chain(v, g, k, ins):
                        ins.then_inc(gate_chain, 1)
                        v.wait_ge(gate_chain, GC * g + k)

                    def gate_place(g, last_):
                        v.wait_ge(gate_exp, g + 1)
                        chain(v, g, 3, nc.vector.tensor_scalar(den, ew, 1.0, None, ALU.add))
                        chain(v, g, 4, nc.vector.reciprocal(weight[:, g, :, 0], den))
                        chain(v, g, 5, nc.vector.tensor_tensor(weight[:, g, :, 1], weight[:, g, :, 0], ew, ALU.mult))
                        _, gg, m0 = norm_items(g, last_)
                        m = m0 + 3
                        rp.wait_filled(v, gg, m)
                        chain(v, g, 6, nc.vector.tensor_copy(
                            tot, rp.bank(m)[0:T, GB * E:2 * GB * E].rearrange("p (b e) -> p b e", b=GB)))
                        chain(v, g, 7, nc.vector.tensor_copy(base[:, 0], total))
                        for b in range(1, GB):
                            chain(v, g, 7 + b, nc.vector.tensor_tensor(base[:, b], base[:, b - 1], tot[:, b - 1], ALU.add))
                        chain(v, g, 11, nc.vector.tensor_tensor(total, base[:, GB - 1], tot[:, GB - 1], ALU.add))
                        rp.drain(nc.vector.tensor_tensor(
                            rk, rp.bank(m)[0:T, 0:GB * E].rearrange("p (b e) -> p b e", b=GB), base, ALU.add), m)
                        rp.wait_drained(v, gg, m)
                        for k in range(TOPK):
                            last = nc.vector.tensor_tensor(picked[:, k], oh[:, k], rk, ALU.mult)
                        chain(v, g, 12, last)
                        for k in range(TOPK):
                            last = nc.vector.tensor_reduce(rank[:, g, :, k], picked[:, k], AX_X, ALU.add)
                        chain(v, g, 13, last)
                        v.wait_ge(places_free, g + 1)
                        chain(v, g, 14, nc.vector.scalar_tensor_tensor(
                            pos, expert[:, g], float(CAP), rank[:, g], ALU.mult, ALU.add))
                        chain(v, g, 15, nc.vector.tensor_copy(ids_g, ids[:, g]))
                        v.sem_inc(pos_ready, 1)

                    def start(g):
                        mask_keys(g, 0)
                        mask_keys(g, 1)
                        attention_vector_max(v, rs, seq2, g, 0)

                    def body(g, norm, more):
                        for n in range(NH):
                            if norm and n == 1:
                                ln_vector_stats(xres, g - 1, norm_index(g - 1))
                            if norm and n == 2:
                                ln_vector_mean(v, norm_index(g - 1))
                            if norm and n == 4:
                                v.wait_ge(zz_stored, 16 * (g - 1) + 1)
                                ln_vector_rows(v, xres, False, g - 1, norm_index(g - 1), rp, LN_M)
                            if n + 1 < NH:
                                attention_vector_max(v, rs, seq2, g, n + 1)
                            if n + 2 < NH:
                                mask_keys(g, n + 2)
                            attention_vector_sum(v, rs, seq2, g, n)
                            if norm and n == GATE1_STEP:
                                gate_top(g - 1, False)
                            if norm and n == GATE2_STEP:
                                gate_place(g - 1, False)
                        if more:
                            start(g + 1)
                        v.wait_ge(bp_added, g + 1)
                        m0 = OUT_M if more else OUT_LAST
                        for j in range(2):
                            m = m0 + j
                            rp.wait_filled(v, g, m)
                            rows = xres[:, g, 2 * j:2 * j + 2, :]
                            rp.drain(nc.vector.tensor_tensor(
                                rows, rows, rp.bank(m)[0:T, :].rearrange("p (b d) -> p b d", b=2), ALU.add), m)
                        for j in range(2):
                            rp.wait_drained(v, g, m0 + j)

                    nc.vector.memset(zeros_i, 0.0).then_inc(t2, 1)
                    nc.vector.memset(V2, 0.0)
                    nc.vector.memset(total, 0.0)
                    nc.vector.memset(ones, 1.0).then_inc(t2, 1)
                    v.wait_ge(w2_loaded, 16 * (len(c2) + 3))
                    nc.vector.tensor_copy(identb, ident[0:T, 0:T]).then_inc(t2, 1)
                    nc.vector.tensor_copy(causalb, c2["causal"].unsqueeze(1).broadcast_to([T, GB, T])).then_inc(t2, 1)
                    v.wait_ge(t2, 4)
                    start(0)
                    body(0, False, True)
                    with v.Fori(1, G - 1) as g:
                        body(g, True, True)
                    body(G - 1, True, False)
                    l = norm_index(G - 1)
                    ln_vector_stats(xres, G - 1, l)
                    ln_vector_mean(v, l)
                    v.wait_ge(zz_stored, 16 * (G - 1) + 1)
                    ln_vector_rows(v, xres, False, G - 1, l, rp, LN_M)
                    gate_top(G - 1, True)
                    gate_place(G - 1, True)

                @block.gpsimd
                def _(pool):
                    def scatter(g):
                        pool.wait_ge(pos_ready, g + 1)
                        pool.sem_inc(dma_turn, 1)
                        for b in range(GB):
                            for k in range(TOPK):
                                nc.gpsimd.indirect_dma_start(
                                    list_d, bass.IndirectOffsetOnAxis(ap=pos[:, b, k:k + 1], axis=0),
                                    ids_g[:, b:b + 1], None).then_inc(scattered, 16)
                        pool.wait_ge(scattered, 16 * TOPK * GB * (g + 1))
                        pool.sem_inc(places_free, 1)

                    def body(g, norm):
                        nc.gpsimd.tensor_tensor(xres[:, g], xres[:, g], c2["bpb"].unsqueeze(1).broadcast_to([T, GB, D]),
                                                ALU.add).then_inc(bp_added, 1)
                        for n in range(NH):
                            if norm and n == 3:
                                ln_pool_rstd(pool, norm_index(g - 1))
                            attention_pool_norm(pool, seq2, g, n)
                            if norm and n == 7:
                                ln_pool_add(pool, True, g - 1, norm_index(g - 1))
                        if norm:
                            scatter(g - 1)

                    pool.wait_ge(w2_loaded, 16 * (len(c2) + 3))
                    pool.wait_ge(list_zero, 16)
                    pool.sem_inc(places_free, 1)
                    body(0, False)
                    with pool.Fori(1, G) as g:
                        body(g, True)
                    ln_pool_rstd(pool, norm_index(G - 1))
                    ln_pool_add(pool, True, G - 1, norm_index(G - 1))
                    scatter(G - 1)

                @block.scalar
                def _(act):
                    def pair(g):
                        def wait(c):
                            if c >= 0:
                                rv.wait_filled(act, g, pair_item(c))
                            elif not (isinstance(g, int) and g == 0):
                                rv.wait_filled(act, g - 1, pair_item(c + NCH))
                        return wait

                    def lagging(g, n):
                        if 0 <= n - LT < NH:
                            attention_scalar_T(act, rt, seq2, g, n - LT, pair(g))
                        if 0 <= n - LAV < NH and (n - LAV) % HC == HC - 1:
                            m = (n - LAV) // HC
                            rv.wait_filled(act, g, pair_item(n_pairs * m + n_pairs - 1))
                            nc.scalar.activation(yT[:, m, :], rv.banks[m][:, 0:GT], ACT.Identity,
                                                 bias=bB[:, 2, m:m + 1]).then_inc(rv.drained[m], n_pairs)
                            act.wait_ge(rv.drained[m], rv.before(g, m) + n_pairs)
                            act.sem_inc(y_cols, 1)

                    def start(g, first, between):
                        r_, gg, m0 = start_items(g, first)
                        if not first:
                            rs.wait_filled(act, g - 1, NH - 1)
                        for m in range(4):
                            dst, done, bias = (qT, q_ready, bB[:, 0, m % 2:m % 2 + 1]) if m < 2 else (
                                kT, k_ready, bB[:, 1, m % 2:m % 2 + 1])
                            r_.wait_filled(act, gg, m0 + m)
                            r_.drain(nc.scalar.activation(dst[:, m % 2, :], r_.bank(m)[:, 0:GT], ACT.Identity, bias=bias), m)
                            r_.wait_drained(act, gg, m0 + m)
                            act.sem_inc(done, 1)
                            between(m)
                        for j in range(2):
                            r_.wait_filled(act, gg, m0 + 4 + j)
                            src = r_.bank(4 + j)[0:T, :].rearrange("p (b n h d) -> p b n h d", b=2, n=NCH, h=2)
                            for bb in range(2):
                                for hh in range(2):
                                    last = nc.scalar.activation(
                                        V2[:, 2 * j + bb, :, hh, hh * DM:(hh + 1) * DM], src[:, bb, :, hh, :], ACT.Copy)
                            r_.drain(last, 4 + j)
                        attention_scalar_exp(act, rs, rt, seq2, g, 0)

                    def body(g, norm, more):
                        for n in range(NH):
                            if norm and n == LN2_STEP:
                                ln_scalar(act, rp, g, norm_index(g - 1), LN_M, 2, g - 1)
                            if norm and n == GATE1_STEP + 1:
                                act.wait_ge(gate_gap, g)
                                nc.scalar.activation(ew, gap, ACT.Exp).then_inc(gate_exp, 1)
                            if n + 1 < NH:
                                attention_scalar_exp(act, rs, rt, seq2, g, n + 1)
                            lagging(g, n)
                        if more:
                            start(g + 1, False, lambda k: lagging(g, NH + k))
                        else:
                            for k in range(4):
                                lagging(g, NH + k)

                    act.wait_ge(w2_loaded, 16 * (len(c2) + 3))
                    act.wait_ge(t2, 2)
                    start(0, True, lambda k: None)
                    body(0, False, True)
                    with act.Fori(1, G - 1) as g:
                        body(g, True, True)
                    body(G - 1, True, False)
                    l = norm_index(G - 1)
                    ln_scalar(act, rp, G - 1, l, OUT_LAST + 2, 2, G - 1)
                    act.wait_ge(gate_gap, G)
                    nc.scalar.activation(ew, gap, ACT.Exp).then_inc(gate_exp, 1)
                    act.wait_ge(ln_stored, 16 * (l + 1))

        AHEAD = 4
        QUADS = TILES // AHEAD
        low = Space(arena, 0, BIG)
        high = Space(arena, BIG + PERM, ARENA)
        W2 = low.take([P, E, KH, D])
        b2 = low.take([P, E, D])
        W1 = high.take([P, E, KD, HID])
        b1 = high.take([P, E, HID])
        route = Space(arena, low.at, BIG)
        X = high.take([P, AHEAD, D])
        xT = high.take([P, 2, KD, P])
        yt = high.take([P, 2, D])
        mid = low.take([P, 2, HID])
        midT = low.take([P, 2, KH, P])
        idx = high.take([P, AHEAD], I32)
        n1 = route.take([T, E])
        n1i = route.take([T, E], I32)
        n2i = route.take([T, E], I32)
        n2 = route.take([T, E])
        ends = route.take([T, E + 1])
        start = route.take([T, E])
        NTOK = G * GB * TOPK
        sel = route.take([T, NTOK, E])
        selv = route.take([T, NTOK, E])
        stok = route.take([T, NTOK])
        past = route.take([T, TILES, E])
        pastv = route.take([T, TILES, E])
        te = route.take([T, TILES])
        tef = route.take([T, TILES])
        tst = route.take([T, TILES])
        toff = route.take([T, TILES])
        toff2 = route.take([T, TILES])
        w3_loaded, routed, xT_ready, gelu_done, y_ready = (
            sem(n) for n in ("w3_loaded", "routed", "xT_ready", "gelu_done", "y_ready"))
        gathered = [sem(f"gathered{s}") for s in range(AHEAD)]
        idx_loaded = [sem(f"idx_loaded{s}") for s in range(AHEAD)]
        y_stored = [sem(f"y_stored{s}") for s in range(2)]
        ROUTE = 17 + E
        rx = ring(0, 2, 4, groups=QUADS)
        r1 = ring(2, 2, 8, groups=QUADS)
        rm = ring(4, 2, 8, groups=QUADS)
        r2 = ring(6, 2, 4, groups=QUADS)

        block = nc.Block()
        with block:
            @block.sync
            def _(sp):
                for e in range(E):
                    sp.dma_start(W1[:, e], a["W1"][:, e]).then_inc(w3_loaded, 16)
                    sp.dma_start(W2[:, e], a["W2"][:, e]).then_inc(w3_loaded, 16)
                sp.dma_start(b1, a["b1"]).then_inc(w3_loaded, 16)
                sp.dma_start(b2, a["b2"]).then_inc(w3_loaded, 16)
                sp.wait_ge(routed, ROUTE)

                def load_idx(i, s):
                    t = AHEAD * i + s
                    if not (isinstance(i, int) and t < AHEAD):
                        sp.wait_ge(gathered[s % AHEAD], 16 * (i + s // AHEAD))
                    at = sp.value_load(tile_at[0:1, bass.ds(t, 1)], min_val=0, max_val=LIST - P)
                    sp.dma_start(idx[:, s % AHEAD:s % AHEAD + 1], list_d[bass.ds(at, P), :]).then_inc(
                        idx_loaded[s % AHEAD], 16)

                def store(i, s):
                    t = AHEAD * i + s
                    sp.wait_ge(y_ready, t + 1)
                    sp.dma_start(y_d[bass.ds(t * P, P), :], yt[:, s % 2, :]).then_inc(y_stored[s % 2], 16)

                for s in range(AHEAD):
                    load_idx(0, s)
                with sp.Fori(0, QUADS - 1) as i:
                    for s in range(AHEAD):
                        load_idx(i, s + AHEAD)
                        store(i, s)
                for s in range(AHEAD):
                    store(QUADS - 1, s)
                for s in range(2):
                    sp.wait_ge(y_stored[s], 16 * TILES // 2)

            @block.gpsimd
            def _(pool):
                def gather(i, s):
                    pool.wait_ge(idx_loaded[s], 16 * i + 16)
                    if not (isinstance(i, int) and i == 0):
                        rx.wait_filled(pool, i, s - AHEAD)
                    pool.sem_inc(dma_turn, 1)
                    nc.gpsimd.indirect_dma_start(X[:, s, :], None, rows_d,
                                                 bass.IndirectOffsetOnAxis(ap=idx[:, s:s + 1], axis=0)
                                                 ).then_inc(gathered[s], 16)

                for s in range(AHEAD):
                    gather(0, s)
                with pool.Fori(1, QUADS) as i:
                    for s in range(AHEAD):
                        gather(i, s)

            @block.tensor
            def _(pe):
                def rows(i, s):
                    pe.wait_ge(gathered[s % AHEAD], 16 * (i + s // AHEAD) + 16)
                    rx.wait_free(pe, i, s)
                    for k in range(KD):
                        last = nc.tensor.transpose(rx.bank(s)[:, k * P:(k + 1) * P], X[:, s % AHEAD, k * P:(k + 1) * P],
                                                   ident[:])
                    rx.fill(last, s)

                def hidden(i, s):
                    pe.wait_ge(xT_ready, AHEAD * i + s + 1)
                    pe.sem_inc(load_turn, 1)
                    e = pe.value_load(tile_e[0:1, bass.ds(AHEAD * i + s, 1)], min_val=0, max_val=E - 1)
                    for f in range(2):
                        m = 2 * s + f
                        r1.wait_free(pe, i, m)
                        for k in range(KD):
                            last = nc.tensor.matmul(r1.bank(m)[:, 0:512], xT[:, s % 2, k, :],
                                                    W1[:, bass.ds(e, 1), k, f * 512:(f + 1) * 512],
                                                    start=(k == 0), stop=(k == KD - 1))
                        r1.fill(last, m)

                def turn(i, s):
                    pe.wait_ge(gelu_done, AHEAD * i + s + 1)
                    for f in range(2):
                        m = 2 * s + f
                        rm.wait_free(pe, i, m)
                        for j in range(4):
                            last = nc.tensor.transpose(rm.bank(m)[:, j * P:(j + 1) * P],
                                                       mid[:, s % 2, (4 * f + j) * P:(4 * f + j + 1) * P], ident[:])
                        rm.fill(last, m)

                def result(i, s):
                    for f in range(2):
                        m = 2 * s + f
                        pe.wait_ge(rm.drained[f], rm.before(i, m) + 1)
                    pe.sem_inc(load_turn, 1)
                    e = pe.value_load(tile_e[0:1, bass.ds(AHEAD * i + s, 1)], min_val=0, max_val=E - 1)
                    r2.wait_free(pe, i, s)
                    for k in range(KH):
                        last = nc.tensor.matmul(r2.bank(s)[:, 0:D], midT[:, s % 2, k, :], W2[:, bass.ds(e, 1), k, :],
                                                start=(k == 0), stop=(k == KH - 1))
                    r2.fill(last, s)

                pe.wait_ge(routed, ROUTE)
                rows(0, 0)
                rows(0, 1)
                pe.wait_ge(w3_loaded, 16 * (2 * E + 2))
                hidden(0, 0)
                with pe.Fori(0, QUADS - 1) as i:
                    for s in range(AHEAD):
                        rows(i, s + 2)
                        turn(i, s)
                        hidden(i, s + 1)
                        result(i, s)
                for s in range(AHEAD):
                    if s + 2 < AHEAD:
                        rows(QUADS - 1, s + 2)
                    turn(QUADS - 1, s)
                    if s + 1 < AHEAD:
                        hidden(QUADS - 1, s + 1)
                    result(QUADS - 1, s)

            @block.vector
            def _(v):
                vec = nc.vector
                done = [0]

                def chain(ins):
                    done[0] += 1
                    ins.then_inc(routed, 1)
                    v.wait_ge(routed, done[0])

                chain(vec.tensor_scalar(n1, total, float(P - 1), None, ALU.add))
                chain(vec.tensor_copy(n1i, n1))
                chain(vec.tensor_scalar(n2i, n1i, 7, None, ALU.arith_shift_right))
                chain(vec.tensor_copy(n2, n2i))
                chain(vec.memset(ends, 0.0))
                for e in range(E):
                    chain(vec.tensor_tensor(ends[:, e + 1:e + 2], ends[:, e:e + 1], n2[:, e:e + 1], ALU.add))
                chain(vec.tensor_scalar(start, ends[:, 0:E], float(P), None, ALU.mult))
                flat = expert.rearrange("p g b k -> p (g b k)")
                chain(vec.tensor_tensor(sel, iota8.unsqueeze(1).broadcast_to([T, NTOK, E]),
                                        flat.unsqueeze(2).broadcast_to([T, NTOK, E]), ALU.is_equal))
                chain(vec.tensor_tensor(selv, sel, start.unsqueeze(1).broadcast_to([T, NTOK, E]), ALU.mult))
                chain(vec.tensor_reduce(stok, selv, AX_X, ALU.add))
                vec.tensor_tensor(place_i.rearrange("p g b k -> p (g b k)"), stok,
                                  rank.rearrange("p g b k -> p (g b k)"), ALU.add)
                last_end = ends[:, 1:E + 1].unsqueeze(1).broadcast_to([T, TILES, E])
                chain(vec.tensor_tensor(past, iota_t.unsqueeze(2).broadcast_to([T, TILES, E]), last_end, ALU.is_ge))
                chain(vec.tensor_tensor(pastv, past, last_end, ALU.mult))
                vec.tensor_reduce(te, past, AX_X, ALU.add)
                chain(vec.tensor_reduce(tst, pastv, AX_X, ALU.max))
                chain(vec.tensor_scalar(tef, te, float(E - 1), None, ALU.min))
                vec.tensor_copy(tile_e, tef)
                chain(vec.tensor_tensor(toff, iota_t, tst, ALU.subtract))
                chain(vec.tensor_scalar(toff2, toff, float(P), None, ALU.mult))
                chain(vec.scalar_tensor_tensor(tile_at, tef, float(CAP), toff2, ALU.mult, ALU.add))
                assert done[0] == ROUTE - 1, done
                vec.memset(idx.bitcast(F32), 0.0).then_inc(routed, 1)
                v.wait_ge(routed, ROUTE)
                v.wait_ge(w3_loaded, 16 * (2 * E + 2))

                def add_b1(i, s):
                    e = v.value_load(tile_e[0:1, bass.ds(AHEAD * i + s, 1)], min_val=0, max_val=E - 1)
                    if not (isinstance(i, int) and AHEAD * i + s < 2):
                        for f in range(2):
                            rm.wait_filled(v, i, 2 * (s - 2) + f)
                    for f in range(2):
                        m = 2 * s + f
                        r1.wait_filled(v, i, m)
                        r1.drain(vec.tensor_tensor(mid[:, s % 2, f * 512:(f + 1) * 512], r1.bank(m)[:, 0:512],
                                                   b1[:, bass.ds(e, 1), f * 512:(f + 1) * 512], ALU.add), m)

                def midT_out(i, s):
                    m = 2 * s + 1
                    rm.wait_filled(v, i, m)
                    if not (isinstance(i, int) and AHEAD * i + s < 2):
                        r2.wait_filled(v, i, s - 2)
                    rm.drain(vec.tensor_copy(midT[:, s % 2, 4:8, :].rearrange("p k t -> p (k t)"), rm.bank(m)[:, 0:512]), m)

                def add_b2(i, s):
                    e = v.value_load(tile_e[0:1, bass.ds(AHEAD * i + s, 1)], min_val=0, max_val=E - 1)
                    if not (isinstance(i, int) and AHEAD * i + s < 2):
                        v.wait_ge(y_stored[s % 2], 16 * (AHEAD // 2 * i + s // 2))
                    r2.wait_filled(v, i, s)
                    r2.drain(vec.tensor_tensor(yt[:, s % 2, :], r2.bank(s)[:, 0:D], b2[:, bass.ds(e, 1), :], ALU.add), s)
                    v.wait_ge(r2.drained[s % 2], r2.before(i, s) + 1)
                    v.sem_inc(y_ready, 1)

                def step(i, s, more):
                    midT_out(i, s)
                    if more:
                        add_b1(i, s + 1)
                    add_b2(i, s)

                add_b1(0, 0)
                for s in range(AHEAD):
                    step(0, s, True)
                with v.Fori(1, QUADS - 1) as i:
                    for s in range(AHEAD):
                        step(i, s, True)
                for s in range(AHEAD):
                    step(QUADS - 1, s, s + 1 < AHEAD)

            @block.scalar
            def _(act):
                def rows_out(i, s):
                    rx.wait_filled(act, i, s)
                    if not (isinstance(i, int) and AHEAD * i + s < 2):
                        r1.wait_filled(act, i, 2 * (s - 2) + 1)
                    for k in range(KD):
                        last = nc.scalar.activation(xT[:, s % 2, k, :], rx.bank(s)[:, k * P:(k + 1) * P], ACT.Identity,
                                                    bias=gb[:, 2, 1, k:k + 1], scale=gb[:, 2, 0, k:k + 1])
                    rx.drain(last, s)
                    act.wait_ge(rx.drained[s % 2], rx.before(i, s) + 1)
                    act.sem_inc(xT_ready, 1)

                def gelu(i, s):
                    for f in range(2):
                        m = 2 * s + f
                        act.wait_ge(r1.drained[f], r1.before(i, m) + 1)
                    nc.scalar.activation(mid[:, s % 2, :], mid[:, s % 2, :], ACT.Gelu).then_inc(gelu_done, 1)

                def midT_out(i, s):
                    m = 2 * s
                    rm.wait_filled(act, i, m)
                    if not (isinstance(i, int) and AHEAD * i + s < 2):
                        r2.wait_filled(act, i, s - 2)
                    rm.drain(nc.scalar.activation(midT[:, s % 2, 0:4, :].rearrange("p k t -> p (k t)"),
                                                  rm.bank(m)[:, 0:512], ACT.Copy), m)

                def step(i, s, rows, more):
                    if rows:
                        rows_out(i, s + 2)
                    midT_out(i, s)
                    if more:
                        gelu(i, s + 1)

                rows_out(0, 0)
                rows_out(0, 1)
                gelu(0, 0)
                for s in range(AHEAD):
                    step(0, s, True, True)
                with act.Fori(1, QUADS - 1) as i:
                    for s in range(AHEAD):
                        step(i, s, True, True)
                for s in range(AHEAD):
                    step(QUADS - 1, s, s + 2 < AHEAD, s + 1 < AHEAD)

        late = Space(arena, BIG + PERM, ARENA)
        wg = late.take([P, KD, FFN])
        wu = late.take([P, KD, FFN])
        wd = late.take([P, KF, D])
        wave = Space(arena, late.at, ARENA)
        wqk = wave.take([P, KD, 4 * D])
        wout = wave.take([P, KD, D])
        bias4 = wave.take([T, 4 * D])
        biasqg = wave.take([P, 4])
        bout = wave.take([T, D])
        toep = wave.take([T, NH, T])
        mixT = wave.take([P, KD, D])
        yg = wave.take([T, GB, TOPK, D])
        pg = wave.take([T, GB, TOPK], I32)
        h_back, pg_ready, y_in, scaled = (sem(n) for n in ("h_back", "pg_ready", "y_in", "scaled"))

        def gather(pool, g):
            pool.wait_ge(pg_ready, g + 1)
            pool.sem_inc(dma_turn, 1)
            for b in range(GB):
                for k in range(TOPK):
                    nc.gpsimd.indirect_dma_start(
                        yg[:, b, k, :], None, y_d,
                        bass.IndirectOffsetOnAxis(ap=pg[:, b, k:k + 1], axis=0)).then_inc(y_in, 16)

        setup = Space(arena, wave.at, ARENA)
        TT = T + FIELD // P
        lag = setup.take([P, TT])
        keep = setup.take([T, T])
        pw = setup.take([P, 3, NH])
        fc = setup.take([NH, NH])
        dmask = setup.take([P, DM])
        sp_ = setup.take([P, 8, NH])
        arg = setup.take([P, NH, TT])
        turns = setup.take([P, NH, TT])
        env = setup.take([P, NH, TT])
        env2 = setup.take([P, NH, TT])
        ab = setup.take([P, NH])
        nrm = setup.take([T, 2, NH])
        ones4 = setup.take([P, T])
        cst = setup.take([NH, 4])
        cx = setup.take([NH, 2, NH])
        cb = setup.take([NH, NH, DM])
        w4_loaded, raw_loaded, built, act_in, act_built, pe_built = (
            sem(n) for n in ("w4_loaded", "raw_loaded", "built", "act_in", "act_built", "pe_built"))
        ENV_AT, ARG_AT, SUM_AT, CX_AT, CB_AT = 10, 20, 25, 31, 34
        PI2 = 2 * np.pi
        C1 = 6.28125
        C2 = float(np.float32(np.floor((PI2 - C1) * 2 ** 21) / 2 ** 21))
        C3 = float(np.float32(PI2 - C1 - C2))
        ROUND = 12582912.0

        block = nc.Block()
        with block:
            loads = [(wqk, "wqk"), (wout, "wout4"), (bias4, "bias4"), (bout, "bout"), (lag, "lag"), (keep, "keep"),
                     (pw, "pw"), (fc, "fc"), (dmask, "dmask"), (biasqg, "biasqg")]
            raws = [(wg, "wg_i"), (wu, "wu_i"), (wd, "wd_i")]

            @block.sync
            def _(sp):
                for dst, n in loads:
                    sp.dma_start(dst, a[n]).then_inc(w4_loaded, 16)
                for g in range(G):
                    sp.dma_start(h[:, g].rearrange("p b d -> p (b d)"), h_d[g]).then_inc(h_back, 16)
                for dst, n in raws:
                    sp.dma_start(dst.bitcast(I32), a[n]).then_inc(raw_loaded, 16)
                sp.wait_ge(h_back, 16 * G)
                sp.wait_ge(w4_loaded, 16 * len(loads))
                sp.wait_ge(raw_loaded, 16 * len(raws))

            @block.gpsimd
            def _(pool):
                gather(pool, 0)
                pool.wait_ge(raw_loaded, 16 * len(raws))
                for dst, n in raws:
                    nc.gpsimd.tensor_scalar(dst, dst.bitcast(I32), float(np.float32(1.0 / 127.0)), None,
                                            ALU.mult).then_inc(scaled, 1)

            @block.vector
            def _(v):
                vec = nc.vector
                n = [0]

                def chain(ins):
                    n[0] += 1
                    ins.then_inc(built, 1)
                    v.wait_ge(built, n[0])

                def heads(x):
                    return x.unsqueeze(2).broadcast_to([P, NH, TT])

                vec.tensor_copy(pg, place_i[:, 0]).then_inc(pg_ready, 1)
                v.wait_ge(w4_loaded, 16 * len(loads))
                damp = pw[:, 1, :]
                chain(vec.tensor_scalar(sp_[:, 0], damp, -1.0, None, ALU.mult))
                chain(vec.tensor_tensor(sp_[:, 1], sp_[:, 0], damp, ALU.min))
                v.wait_ge(act_built, 1)
                chain(vec.tensor_scalar(sp_[:, 4], sp_[:, 2], 1.0, -1.0, ALU.add, ALU.add))
                chain(vec.tensor_scalar(sp_[:, 5], sp_[:, 4], 0.0, None, ALU.is_equal))
                vec.tensor_tensor(sp_[:, 4], sp_[:, 4], sp_[:, 5], ALU.add)
                chain(vec.tensor_tensor(sp_[:, 3], sp_[:, 3], sp_[:, 5], ALU.add))
                chain(vec.reciprocal(sp_[:, 6], sp_[:, 4]))
                chain(vec.tensor_tensor(sp_[:, 3], sp_[:, 3], sp_[:, 6], ALU.mult))
                chain(vec.tensor_tensor(sp_[:, 3], sp_[:, 3], sp_[:, 2], ALU.mult))
                chain(vec.scalar_tensor_tensor(sp_[:, 7], damp, 0.0, sp_[:, 3], ALU.max, ALU.add))
                lags = lag.unsqueeze(1).broadcast_to([P, NH, TT])
                chain(vec.tensor_tensor(env, lags, heads(sp_[:, 7]), ALU.mult))
                assert n[0] == ENV_AT
                chain(vec.tensor_tensor(arg, lags, heads(pw[:, 0, :]), ALU.mult))
                chain(vec.tensor_tensor(arg, arg, heads(pw[:, 2, :]), ALU.add))
                chain(vec.tensor_scalar(turns, arg, float(1 / PI2), ROUND, ALU.mult, ALU.add))
                chain(vec.tensor_scalar(turns, turns, -ROUND, None, ALU.add))
                for c in (C1, C2, C3):
                    chain(vec.scalar_tensor_tensor(arg, turns, -c, arg, ALU.mult, ALU.add))
                chain(vec.tensor_scalar(turns, arg, -1.0, None, ALU.mult))
                chain(vec.tensor_tensor(arg, arg, turns, ALU.min))
                chain(vec.tensor_scalar(arg, arg, float(np.pi / 2), float(-np.pi / 2), ALU.add, ALU.max))
                assert n[0] == ARG_AT
                v.wait_ge(act_built, 3)
                chain(vec.tensor_tensor(arg, env2, turns, ALU.mult))
                chain(vec.tensor_scalar(turns, arg, -1.0, None, ALU.mult))
                chain(vec.tensor_tensor(env, arg, turns, ALU.max))
                chain(vec.tensor_reduce(ab, env[:, :, T:TT], AX_X, ALU.add))
                chain(vec.memset(ones4, 1.0))
                assert n[0] == SUM_AT
                v.wait_ge(pe_built, 1)
                chain(vec.tensor_scalar(nrm[:, 0], banks[0][0:T, 0:NH], 1e-8, None, ALU.max))
                chain(vec.reciprocal(nrm[:, 1], nrm[:, 0]))
                chain(vec.tensor_tensor(toep, arg[0:T, :, 0:T], nrm[:, 1].unsqueeze(2).broadcast_to([T, NH, T]), ALU.mult))
                chain(vec.tensor_tensor(toep, toep, keep.unsqueeze(1).broadcast_to([T, NH, T]), ALU.mult))
                chain(vec.tensor_reduce(cst[:, 0:1], fc, AX_X, ALU.max))
                chain(vec.tensor_scalar(cx[:, 0], fc, cst[:, 0:1], None, ALU.subtract))
                assert n[0] == CX_AT
                v.wait_ge(act_built, 4)
                chain(vec.tensor_reduce(cst[:, 1:2], cx[:, 1], AX_X, ALU.add))
                chain(vec.reciprocal(cst[:, 2:3], cst[:, 1:2]))
                chain(vec.tensor_scalar(cb, cx[:, 1].unsqueeze(2).broadcast_to([NH, NH, DM]), cst[:, 2:3], None, ALU.mult))
                assert n[0] == CB_AT
                v.wait_ge(pe_built, 2)
                for k in range(KD):
                    last = vec.tensor_tensor(mixT[:, k, :].rearrange("p (i d) -> p i d", d=DM),
                                             banks[1][:, k * NH:(k + 1) * NH].unsqueeze(2).broadcast_to([P, NH, DM]),
                                             dmask.unsqueeze(1).broadcast_to([P, NH, DM]), ALU.mult)
                chain(last)

            @block.scalar
            def _(act):
                act.wait_ge(built, 2)
                nc.scalar.activation(sp_[:, 2], sp_[:, 1], ACT.Exp).then_inc(act_in, 1)
                act.wait_ge(act_in, 1)
                nc.scalar.activation(sp_[:, 3], sp_[:, 2], ACT.Ln, bias=1.0).then_inc(act_built, 1)
                act.wait_ge(built, ENV_AT)
                nc.scalar.activation(env2, env, ACT.Exp, scale=-1.0).then_inc(act_built, 1)
                act.wait_ge(built, ARG_AT)
                nc.scalar.activation(turns, arg, ACT.Sin).then_inc(act_built, 1)
                act.wait_ge(built, CX_AT)
                nc.scalar.activation(cx[:, 1], cx[:, 0], ACT.Exp).then_inc(act_built, 1)

            @block.tensor
            def _(pe):
                pe.wait_ge(built, SUM_AT)
                nc.tensor.matmul(banks[0][0:T, 0:NH], ones4, ab, start=True, stop=True).then_inc(pe_built, 1)
                pe.wait_ge(built, CB_AT)
                for k in range(KD):
                    last = nc.tensor.transpose(banks[1][:, k * NH:(k + 1) * NH],
                                               cb.rearrange("p j d -> p (j d)")[:, k * P:(k + 1) * P], ident[0:NH, 0:NH])
                last.then_inc(pe_built, 1)

        tile4 = Space(arena, wave.at, ARENA)
        slab = tile4.take([P, KD, GT])
        kv = tile4.take([T, GB, 2 * D])
        ek = tile4.take([T, GB, D])
        dep = tile4.take([T, GB, D])
        eq = tile4.take([P, KD, GT])
        rq = tile4.take([P, KD, GT])
        gq = tile4.take([P, KD, GT])
        qg = tile4.take([P, KD, GT])
        conv = tile4.take([T, GB, D])
        convT = tile4.take([P, KD, GT])
        f = tile4.take([P, KD, GT])
        (mixed, slab_ready, ek_steps, kf_ready, dep_ready, q_parts, qf_ready, qg_ready, bout_added, hn_stored) = (
            sem(n) for n in ("mixed", "slab_ready", "ek_steps", "kf_ready", "dep_ready", "q_parts", "qf_ready",
                             "qg_ready", "bout_added", "hn_stored"))

        def is0(g):
            return isinstance(g, int) and g == 0

        class Norm:

            def __init__(self, tag, r, dst):
                self.r, self.dst = r, dst
                self.stats = tile4.take([T, GB, 6])
                self.mv = tile4.take([T, GB, 2])
                self.w = tile4.take([T, 2, GB])
                self.zz = tile4.take([T, GB, D])
                self.stat, self.mean, self.rstd, self.row = (
                    sem(tag + n) for n in ("_stat", "_mean", "_rstd", "_row"))

            def vector_stats(self, v, g):
                v.sem_inc(ln_turn, 1)
                for b in range(GB):
                    last = nc.vector.bn_stats(self.stats[:, b, :], h[:, g, b, :])
                last.then_inc(self.stat, 1)
                v.wait_ge(self.stat, g + 1)
                if not is0(g):
                    v.wait_ge(self.rstd, 2 * g)
                v.sem_inc(ln_turn, 1)
                for b in range(GB):
                    last = nc.vector.bn_aggr(self.mv[:, b, :], self.stats[:, b, :])
                last.then_inc(self.mean, 1)

            def pool_rstd(self, pool, g):
                pool.wait_ge(self.mean, g + 1)
                if not is0(g):
                    pool.wait_ge(self.row, g)
                nc.gpsimd.tensor_tensor(self.w[:, 0, :], self.mv[:, :, 1], pows[:, 2, :], ALU.add).then_inc(self.rstd, 1)
                pool.wait_ge(self.rstd, 2 * g + 1)
                nc.gpsimd.tensor_tensor(self.w[:, 1, :], self.w[:, 0, :], pows[:, 0, :], ALU.pow).then_inc(self.rstd, 1)

            def vector_rows(self, v, g):
                v.wait_ge(self.rstd, 2 * g + 2)
                if not is0(g):
                    self.r.wait_filled(v, g - 1, 1)
                for b in range(GB):
                    last = nc.vector.tensor_scalar(self.zz[:, b, :], h[:, g, b, :], self.mv[:, b, 0:1],
                                                   self.w[:, 1, b:b + 1], ALU.subtract, ALU.mult)
                last.then_inc(self.row, 1)

            def tensor_turn(self, pe, g):
                pe.wait_ge(self.row, g + 1)
                for k in range(KD):
                    self.r.wait_free(pe, g, k)
                    for b in range(GB):
                        last = nc.tensor.transpose(self.r.bank(k)[:, b * T:(b + 1) * T],
                                                   self.zz[:, b, k * P:(k + 1) * P], ident[0:T, 0:T])
                    self.r.fill(last, k)

            def scalar_out(self, act, g):
                for k in range(KD):
                    self.r.wait_filled(act, g, k)
                    self.r.drain(nc.scalar.activation(self.dst[:, k, :], self.r.bank(k)[:, 0:GT], ACT.Copy), k)
                self.r.wait_drained(act, g, KD - 1)

        rb = ring(0, 4, 8)
        rc = ring(4, 2, 8)
        first = Norm("first", ring(6, 1, 2), slab)
        second = Norm("second", ring(7, 1, 2), lnT)

        block = nc.Block()
        with block:
            @block.sync
            def _(sp):
                def store(g):
                    second.r.wait_drained(sp, g, KD - 1)
                    sp.dma_start(hnT[:, :, g, :], lnT).then_inc(hn_stored, 16)

                store(0)
                with sp.Fori(1, G) as g:
                    store(g)
                sp.wait_ge(hn_stored, 16 * G)

            @block.tensor
            def _(pe):
                def keys_values(g):
                    pe.wait_ge(slab_ready, g + 1)
                    for b in range(GB):
                        rb.wait_free(pe, g, b)
                        for k in range(KD):
                            last = nc.tensor.matmul(rb.bank(b)[0:T, 0:512], slab[:, k, b * T:(b + 1) * T],
                                                    wqk[:, k, D:3 * D], start=(k == 0), stop=(k == KD - 1))
                        rb.fill(last, b)

                def queries_gates(g):
                    for j in range(4):
                        m = 4 + j
                        at = (0, P, 3 * D, 3 * D + P)[j]
                        rb.wait_free(pe, g, m)
                        for k in range(KD):
                            last = nc.tensor.matmul(rb.bank(m)[:, 0:GT], wqk[:, k, at:at + P], slab[:, k, :],
                                                    start=(k == 0), stop=(k == KD - 1))
                        rb.fill(last, m)

                def turn(g, head, tail):
                    if head:
                        first.tensor_turn(pe, g + 1)
                    pe.wait_ge(dep_ready, g + 1)
                    for k in range(2):
                        rc.wait_free(pe, g, k)
                        for jj in range(HC):
                            j = HC * k + jj
                            last = nc.tensor.matmul(rc.bank(k)[0:T, jj * GB * DM:(jj + 1) * GB * DM], toep[:, j, :],
                                                    dep[:, :, j * DM:(j + 1) * DM], start=True, stop=True)
                        rc.fill(last, k)
                    if head:
                        keys_values(g + 1)
                    for k in range(2):
                        rc.wait_drained(pe, g, k)
                    for k in range(KD):
                        rc.wait_free(pe, g, 2 + k)
                        for b in range(GB):
                            last = nc.tensor.transpose(rc.bank(2 + k)[:, b * T:(b + 1) * T],
                                                       conv[:, b, k * P:(k + 1) * P], ident[0:T, 0:T])
                        rc.fill(last, 2 + k)
                    if tail:
                        second.tensor_turn(pe, g - 1)
                    for k in range(KD):
                        rc.wait_drained(pe, g, 2 + k)
                    for i in range(KD):
                        rc.wait_free(pe, g, 4 + i)
                        for k in range(KD):
                            last = nc.tensor.matmul(rc.bank(4 + i)[:, 0:GT], mixT[:, k, i * P:(i + 1) * P], convT[:, k, :],
                                                    start=(k == 0), stop=(k == KD - 1))
                        rc.fill(last, 4 + i)
                    if head:
                        queries_gates(g + 1)
                    for k in range(KD):
                        rc.wait_drained(pe, g, 4 + k)
                    for j in range(2):
                        rc.wait_free(pe, g, 6 + j)
                        for bb in range(2):
                            b = 2 * j + bb
                            for k in range(KD):
                                last = nc.tensor.matmul(rc.bank(6 + j)[0:T, bb * D:(bb + 1) * D],
                                                        f[:, k, b * T:(b + 1) * T], wout[:, k, :],
                                                        start=(k == 0), stop=(k == KD - 1))
                        rc.fill(last, 6 + j)

                first.tensor_turn(pe, 0)
                keys_values(0)
                queries_gates(0)
                turn(0, True, False)
                with pe.Fori(1, G - 3) as g:
                    turn(g, True, True)
                turn(G - 3, True, True)
                turn(G - 2, True, True)
                turn(G - 1, False, True)
                second.tensor_turn(pe, G - 1)

            @block.vector
            def _(v):
                vec = nc.vector

                def experts_in(g, more):
                    v.wait_ge(y_in, 16 * GB * TOPK * (g + 1))
                    for k in range(TOPK):
                        for b in range(GB):
                            last = vec.scalar_tensor_tensor(h[:, g, b, :], yg[:, b, k, :], weight[:, g, b, k:k + 1],
                                                            h[:, g, b, :], ALU.mult, ALU.add)
                        last.then_inc(mixed, 1)
                        v.wait_ge(mixed, TOPK * g + k + 1)
                    if more:
                        vec.tensor_copy(pg, place_i[:, g + 1]).then_inc(pg_ready, 1)

                def keys_values(g):
                    for b in range(GB):
                        if b == 0 and not is0(g):
                            v.wait_ge(dep_ready, g)
                        rb.wait_filled(v, g, b)
                        rb.drain(vec.tensor_tensor(kv[:, b, :], rb.bank(b)[0:T, 0:512], bias4[:, D:3 * D], ALU.add), b)

                def deposits(g):
                    v.wait_ge(ek_steps, 2 * g + 2)
                    vec.scalar_tensor_tensor(ek, kv[:, :, 0:D], 0.0, ek, ALU.max, ALU.add).then_inc(kf_ready, 1)
                    v.wait_ge(kf_ready, g + 1)
                    if not is0(g):
                        rc.wait_filled(v, g - 1, 1)
                    vec.tensor_tensor(dep, ek, kv[:, :, D:2 * D], ALU.mult).then_inc(dep_ready, 1)

                def queries(g):
                    v.wait_ge(q_parts, 6 * g + 6)
                    vec.scalar_tensor_tensor(rq, eq, 1.0, rq, ALU.min, ALU.add).then_inc(qf_ready, 1)
                    v.wait_ge(qf_ready, g + 1)
                    vec.tensor_tensor(qg, rq, gq, ALU.mult).then_inc(qg_ready, 1)

                def turn(g, head, ahead, more, tail):
                    if tail:
                        second.vector_rows(v, g - 1)
                    if head:
                        keys_values(g + 1)
                    if ahead:
                        experts_in(g + 2, more)
                    if head:
                        deposits(g + 1)
                    v.wait_ge(qg_ready, g + 1)
                    for k in range(KD):
                        if not is0(g):
                            rc.wait_filled(v, g - 1, 7)
                        rc.wait_filled(v, g, 4 + k)
                        rc.drain(vec.tensor_tensor(f[:, k, :], qg[:, k, :], rc.bank(4 + k)[:, 0:GT], ALU.mult), 4 + k)
                    if ahead:
                        first.vector_stats(v, g + 2)
                    if head:
                        queries(g + 1)
                    if ahead:
                        first.vector_rows(v, g + 2)
                    v.wait_ge(bout_added, g + 1)
                    for j in range(2):
                        rc.wait_filled(v, g, 6 + j)
                        rows = h[:, g, 2 * j:2 * j + 2, :]
                        rc.drain(vec.tensor_tensor(rows, rows, rc.bank(6 + j)[0:T, :].rearrange("p (b d) -> p b d", b=2),
                                                   ALU.add), 6 + j)
                    for j in range(2):
                        rc.wait_drained(v, g, 6 + j)
                    second.vector_stats(v, g)

                for g in range(2):
                    experts_in(g, True)
                    first.vector_stats(v, g)
                    first.vector_rows(v, g)
                    if g == 0:
                        keys_values(0)
                        deposits(0)
                        queries(0)
                turn(0, True, True, True, False)
                with v.Fori(1, G - 3) as g:
                    turn(g, True, True, True, True)
                turn(G - 3, True, True, False, True)
                turn(G - 2, True, False, False, True)
                turn(G - 1, False, False, False, True)
                second.vector_rows(v, G - 1)

            @block.scalar
            def _(act):
                def slab_out(g):
                    first.scalar_out(act, g)
                    act.sem_inc(slab_ready, 1)

                def keys(g):
                    for b in range(GB):
                        rb.wait_drained(act, g, b)
                    if not is0(g):
                        act.wait_ge(dep_ready, g)
                    nc.scalar.activation(ek, kv[:, :, 0:D], ACT.Relu, scale=-1.0).then_inc(ek_steps, 1)
                    act.wait_ge(ek_steps, 2 * g + 1)
                    nc.scalar.activation(ek, ek, ACT.Exp, scale=-1.0).then_inc(ek_steps, 1)

                def queries(g):
                    if not is0(g):
                        act.wait_ge(qg_ready, g)
                    for k in range(KD):
                        m = 4 + k
                        src = rb.bank(m)[:, 0:GT]
                        rb.wait_filled(act, g, m)
                        nc.scalar.activation(eq[:, k, :], src, ACT.Exp, bias=biasqg[:, k:k + 1]).then_inc(q_parts, 1)
                        rb.drain(nc.scalar.activation(rq[:, k, :], src, ACT.Relu, bias=biasqg[:, k:k + 1]), m)
                    for k in range(KD):
                        m = 6 + k
                        rb.wait_filled(act, g, m)
                        rb.drain(nc.scalar.activation(gq[:, k, :], rb.bank(m)[:, 0:GT], ACT.Sigmoid,
                                                      bias=biasqg[:, 2 + k:3 + k]), m)
                    for m in range(4, 8):
                        rb.wait_drained(act, g, m)
                        act.sem_inc(q_parts, 1)

                def turn(g, head, tail):
                    if head:
                        slab_out(g + 1)
                    for k in range(2):
                        rc.wait_filled(act, g, k)
                        rc.drain(nc.scalar.activation(
                            conv.rearrange("p b (j d) -> p b j d", d=DM)[:, :, k * HC:(k + 1) * HC, :],
                            rc.bank(k)[0:T, :].rearrange("p (j b d) -> p b j d", j=HC, b=GB), ACT.Copy), k)
                    for k in range(KD):
                        rc.wait_filled(act, g, 2 + k)
                        rc.drain(nc.scalar.activation(convT[:, k, :], rc.bank(2 + k)[:, 0:GT], ACT.Copy), 2 + k)
                    if head:
                        keys(g + 1)
                    if tail:
                        norm_out(g - 1)
                    if head:
                        queries(g + 1)

                def norm_out(g):
                    if not is0(g):
                        act.wait_ge(hn_stored, 16 * g)
                    second.scalar_out(act, g)

                slab_out(0)
                keys(0)
                queries(0)
                turn(0, True, False)
                with act.Fori(1, G - 3) as g:
                    turn(g, True, True)
                turn(G - 3, True, True)
                turn(G - 2, True, True)
                turn(G - 1, False, True)
                norm_out(G - 1)

            @block.gpsimd
            def _(pool):
                def add_bout(g):
                    pool.wait_ge(first.row, g + 1)
                    nc.gpsimd.tensor_tensor(h[:, g], h[:, g], bout.unsqueeze(1).broadcast_to([T, GB, D]),
                                            ALU.add).then_inc(bout_added, 1)

                def turn(g, ahead, more, tail):
                    if tail:
                        second.pool_rstd(pool, g - 1)
                    add_bout(g)
                    if more:
                        gather(pool, g + 3)
                    if ahead:
                        first.pool_rstd(pool, g + 2)

                gather(pool, 1)
                first.pool_rstd(pool, 0)
                gather(pool, 2)
                first.pool_rstd(pool, 1)
                turn(0, True, True, False)
                with pool.Fori(1, G - 3) as g:
                    turn(g, True, True, True)
                turn(G - 3, True, False, True)
                turn(G - 2, False, False, True)
                turn(G - 1, False, False, True)
                second.pool_rstd(pool, G - 1)

        if upto < 5:
            final(nc, sem, h, out)
            return

        fin = Space(arena, late.at, ARENA)
        hid = fin.take([P, 2, KF, GT])
        sg = fin.take([P, 2, GT])
        hid_ready, rows_ready = sem("hid_ready"), sem("rows_ready")
        ru = ring(0, 4, 2 * KF)
        rd = ring(4, 4, 4, groups=G // 2)
        block = nc.Block()
        with block:
            @block.tensor
            def _(pe):
                def up(i, s):
                    g = 2 * i + s
                    for c in range(KF):
                        for j, w_ in enumerate((wg, wu)):
                            m = 2 * c + j
                            ru.wait_free(pe, g, m)
                            for k in range(KD):
                                last = nc.tensor.matmul(ru.bank(m)[:, 0:GT], w_[:, k, c * P:(c + 1) * P], hnT[:, k, g, :],
                                                        start=(k == 0), stop=(k == KD - 1))
                            ru.fill(last, m)

                def down(i, s):
                    g = 2 * i + s
                    pe.wait_ge(hid_ready, KF * g + KF)
                    for j in range(2):
                        m = 2 * (s % 2) + j
                        gg = i + s // 2
                        rd.wait_free(pe, gg, m)
                        for bb in range(2):
                            b = 2 * j + bb
                            for c in range(KF):
                                last = nc.tensor.matmul(rd.bank(m)[0:T, bb * D:(bb + 1) * D],
                                                        hid[:, s % 2, c, b * T:(b + 1) * T], wd[:, c, :],
                                                        start=(c == 0), stop=(c == KF - 1))
                        rd.fill(last, m)

                up(0, 0)
                with pe.Fori(0, G // 2 - 1) as i:
                    for s in range(2):
                        up(i, s + 1)
                        down(i, s)
                up(G // 2 - 1, 1)
                down(G // 2 - 1, 0)
                down(G // 2 - 1, 1)

            @block.scalar
            def _(act):
                with act.Fori(0, G) as g:
                    for c in range(KF):
                        m = 2 * c
                        ru.wait_filled(act, g, m)
                        if c >= 2:
                            act.wait_ge(hid_ready, KF * g + c - 1)
                        else:
                            act.wait_ge(hid_ready, KF * g)
                        ru.drain(nc.scalar.activation(sg[:, c % 2, :], ru.bank(m)[:, 0:GT], ACT.Silu), m)

            @block.vector
            def _(v):
                def mul(i, s):
                    g = 2 * i + s
                    if not (isinstance(i, int) and i == 0 and s < 2):
                        rd.wait_filled(v, i + s // 2 - 1, 2 * (s % 2) + 1)
                    for c in range(KF):
                        m = 2 * c + 1
                        v.wait_ge(ru.drained[(m - 1) % 4], ru.before(g, m - 1) + 1)
                        ru.wait_filled(v, g, m)
                        ru.drain(nc.vector.tensor_tensor(hid[:, s % 2, c, :], sg[:, c % 2, :], ru.bank(m)[:, 0:GT],
                                                         ALU.mult), m)
                        v.wait_ge(ru.drained[m % 4], ru.before(g, m) + 1)
                        v.sem_inc(hid_ready, 1)

                def add(i, s):
                    g = 2 * i + s
                    for j in range(2):
                        m = 2 * s + j
                        rd.wait_filled(v, i, m)
                        rows = h[:, g, 2 * j:2 * j + 2, :]
                        rd.drain(nc.vector.tensor_tensor(rows, rows, rd.bank(m)[0:T, :].rearrange("p (b d) -> p b d", b=2),
                                                         ALU.add), m)
                    for j in range(2):
                        v.wait_ge(rd.drained[2 * s + j], rd.before(i, 2 * s + j) + 1)
                    v.sem_inc(rows_ready, 1)

                mul(0, 0)
                with v.Fori(0, G // 2 - 1) as i:
                    for s in range(2):
                        mul(i, s + 1)
                        add(i, s)
                mul(G // 2 - 1, 1)
                add(G // 2 - 1, 0)
                add(G // 2 - 1, 1)

            @block.sync
            def _(sp):
                with sp.Fori(0, G) as g:
                    sp.wait_ge(rows_ready, g + 1)
                    sp.dma_start(out[:, bass.ds(GB * g, GB), :], h[:, g]).then_inc(out_stored, 16)
                sp.wait_ge(out_stored, 16 * G)


def final(nc, sem, h, out):
    out_stored = sem("dbg_stored")
    with nc.Block() as block:
        @block.sync
        def _(sp):
            for q in range(4):
                sp.dma_start(out[:, 8 * q:8 * q + 8, :], h[:, 2 * q:2 * q + 2].rearrange("p g b d -> p (g b) d")).then_inc(out_stored, 16)
            sp.wait_ge(out_stored, 64)


def layouts(x, txt, i):
    f = np.float32

    def chunks(m):
        k, n = m.shape
        return m.reshape(k // P, P, n).transpose(1, 0, 2)

    def column(v):
        return v.reshape(-1, P).T

    o = {}
    p = x.reshape(G, GB, 3, 8, 16, 8, 16).transpose(0, 4, 6, 2, 1, 3, 5)
    o["patches"] = p.reshape(G, KP, P, GB * IMG).transpose(0, 2, 1, 3)
    o["txt"] = txt.transpose(1, 0, 2)
    o["wpT"] = chunks(i["L0_tok_Wp"].T)
    o["tokb"] = np.broadcast_to(i["L0_tok_b"], (P, D))
    gh, gw = np.meshgrid(np.arange(8), np.arange(8), indexing="ij")
    quarter = D // 4
    factor = f(10000.0) ** (np.arange(quarter, dtype=f) / f(quarter))
    hh = gh.reshape(-1).astype(f)[:, None] / factor
    ww = gw.reshape(-1).astype(f)[:, None] / factor
    pos = np.concatenate([np.sin(hh), np.cos(hh), np.sin(ww), np.cos(ww)], axis=-1).astype(f)
    o["pos2"] = np.concatenate([pos, pos], axis=0)
    o["ident"] = np.eye(P, dtype=f)
    inv_freq = 1.0 / 10000.0 ** (np.arange(0, DH, 2, dtype=f) / DH)
    freqs = np.outer(np.arange(T, dtype=f), inv_freq)
    cos = np.concatenate([np.cos(freqs), np.cos(freqs)], -1)[:, ::2].astype(f).T
    sin = np.concatenate([np.sin(freqs), np.sin(freqs)], -1)[:, ::2].astype(f).T
    o["ropeC"] = np.concatenate([cos] * 4, axis=0)
    o["ropeS"] = np.concatenate([-sin, sin, -sin, sin], axis=0)
    o["ropeCq"] = o["ropeC"] * f(1 / np.sqrt(DH))
    o["ropeSq"] = o["ropeS"] * f(1 / np.sqrt(DH))
    o["gb"] = np.stack([np.stack([column(i[s]), column(i[t])], 1) for s, t in (
        ("L0_attn_ln_scale", "L0_attn_ln_bias"), ("L0_ffn_ln1_g", "L0_ffn_ln1_b"), ("L0_ffn_ln2_g", "L0_ffn_ln2_b"))], 1)
    n = np.arange(HID).reshape(NH, DH)
    straight = np.concatenate([n[:, 0::2], n[:, 1::2]], 1).reshape(-1)
    swapped = np.concatenate([n[:, 1::2], n[:, 0::2]], 1).reshape(-1)
    o["wdq"] = chunks(i["L0_attn_w_down_q"].T)
    o["wdkv"] = chunks(i["L0_attn_w_down_kv"].T)
    o["wuq"] = i["L0_attn_w_up_q"][straight].T
    o["wuqs"] = i["L0_attn_w_up_q"][swapped].T
    o["wuk"] = i["L0_attn_w_up_k"][straight].T
    o["wuks"] = i["L0_attn_w_up_k"][swapped].T
    o["wuv"] = i["L0_attn_w_up_v"].T
    o["woT"] = chunks(i["L0_attn_w_out"].T)
    for k, s in (("wq2", "Wq"), ("wk2", "Wk"), ("wv2", "Wv"), ("wp2", "Wp")):
        o[k] = chunks(i["L0_ffn_" + s])
    o["bB"] = np.stack([column(i["L0_ffn_" + s]) for s in ("bq", "bk", "bv")], 1)
    o["hmask"] = (np.arange(P)[:, None] // DM == np.arange(HC)[None, :]).astype(f) * f(1 / np.sqrt(DM))
    o["causal"] = np.where(np.arange(T)[None, :] <= np.arange(T)[:, None], f(0), f(NEG))
    o["tri"] = (np.arange(T)[:, None] < np.arange(T)[None, :]).astype(f)
    o["bpb"] = np.broadcast_to(i["L0_ffn_bp"], (T, D))
    o["gateW"] = chunks(i["L0_ffn_gate_W"])
    o["gateb"] = np.broadcast_to(i["L0_ffn_gate_b"], (T, E))
    o["ids"] = (np.arange(T)[:, None, None] + T * np.arange(B).reshape(1, G, GB)).astype(np.int32)
    o["iota8"] = np.broadcast_to(np.arange(E, dtype=f), (T, E))
    o["iota_t"] = np.broadcast_to(np.arange(TILES, dtype=f), (T, TILES))
    o["W1"] = i["L0_ffn_exp_W1"].reshape(E, KD, P, HID).transpose(2, 0, 1, 3)
    o["W2"] = i["L0_ffn_exp_W2"].reshape(E, KH, P, D).transpose(2, 0, 1, 3)
    o["b1"] = np.broadcast_to(i["L0_ffn_exp_b1"], (P, E, HID))
    o["b2"] = np.broadcast_to(i["L0_ffn_exp_b2"], (P, E, D))
    o["wqk"] = chunks(i["L1_attn_Wqkvg"].T)
    o["wout4"] = chunks(i["L1_attn_Wout"].T)
    o["bias4"] = np.broadcast_to(i["L1_attn_bqkvg"], (T, 4 * D))
    o["biasqg"] = column(np.concatenate([i["L1_attn_bqkvg"][:D], i["L1_attn_bqkvg"][3 * D:]]))
    o["bout"] = np.broadcast_to(i["L1_attn_bout"], (T, D))
    s_, t_ = np.arange(T)[:, None], np.arange(T)[None, :]
    lag = np.zeros((P, T + FIELD // P), f)
    lag[0:T, 0:T] = np.maximum(t_ - s_, 0)
    lag[:, T:] = np.arange(FIELD).reshape(FIELD // P, P).T
    o["lag"] = lag
    o["keep"] = (t_ >= s_).astype(f)
    o["pw"] = np.broadcast_to(np.stack([i["L1_attn_wave_frequency"], i["L1_attn_wave_damping"], i["L1_attn_wave_phase"]]),
                              (P, 3, NH))
    o["fc"] = i["L1_attn_field_coupling"]
    o["dmask"] = (np.arange(P)[:, None] % DM == np.arange(DM)[None, :]).astype(f)
    o["wg_i"] = chunks(i["L1_ffn_w_gate"].T)
    o["wu_i"] = chunks(i["L1_ffn_w_up"].T)
    o["wd_i"] = chunks(i["L1_ffn_w_down"].T)
    return {k: np.ascontiguousarray(v) for k, v in o.items()}


UPTO = 9


def kernel(x, txt, **inputs):
    import concourse.bacc as _bacc
    from concourse.bass_utils import run_bass_kernel_spmd as _run

    nc = _bacc.Bacc("TRN2", target_bir_lowering=False, num_devices=1)
    arrays = layouts(np.asarray(x), np.asarray(txt), {k: np.asarray(v) for k, v in inputs.items()})
    aps = {k: nc.dram_tensor("in_" + k, v.shape, mybir.dt.from_np(v.dtype), kind="ExternalInput").ap()
           for k, v in arrays.items()}
    out = nc.dram_tensor("out", (T, B, D), F32, kind="ExternalOutput").ap()
    program(nc, aps, out, UPTO)
    r = _run(nc, [{"in_" + k: v for k, v in arrays.items()}], core_ids=[0])
    return np.ascontiguousarray(r.results[0]["out"].transpose(1, 0, 2))
```

```python
from contextlib import ExitStack

import numpy as np
import concourse.bass as bass
from concourse import mybir

F32 = mybir.dt.float32
BF16 = mybir.dt.bfloat16
I32 = mybir.dt.int32
U32 = mybir.dt.uint32
ALU = mybir.AluOpType
ACT = mybir.ActivationFunctionType
AX_X = mybir.AxisListType.X

P = 128
B = 32
T = 96
IMG = 64
TXT = 32
D = 256
KD = D // P
GB = 4
G = B // GB
GT = GB * T
PATCH = 768
KP = PATCH // P
NH = 16
DH = 64
NCH = NH // 2
DM = 16
HC = P // DM
E = 8
HID = 1024
KH = HID // P
EPS = 1e-5
TOPK = 2
CAP = B * T
TILES = B * T * TOPK // P + E
LIST = (E * CAP + TILES * P + P - 1) // P * P
FFN = 768
KF = FFN // P
FIELD = 512
NEG = -1e30
RING = 4


BIG = 2 * B * D + KD * B * T
PERM = 2700
ARENA = 53200


class Space:

    def __init__(self, arena, at, end):
        self.arena, self.at, self.end = arena, at, end

    def take(self, shape, dt=F32):
        words = int(np.prod(shape[1:]))
        if dt == BF16:
            assert words % 2 == 0
            words //= 2
        v = self.arena[0:shape[0], self.at:self.at + words]
        self.at += words
        assert self.at <= self.end, (self.at, self.end)
        if dt != F32:
            v = v.bitcast(dt)
        if len(shape) > 2:
            names = "abcd"[:len(shape) - 1]
            v = v.rearrange(f"p ({' '.join(names)}) -> p {' '.join(names)}",
                            **{n: k for n, k in zip(names, shape[1:])})
        return v


class Ring:

    def __init__(self, banks, filled, drained, base, per_group, gap=None, late=2, groups=G):
        self.groups = groups
        self.banks, self.filled, self.drained, self.base = banks, filled, drained, base
        self.n, self.per_group, self.gap, self.late = len(banks), per_group, gap, late
        assert per_group % self.n == 0 and late % self.n == 0 or gap is None
        assert gap is None or gap % self.n == 0

    def before(self, g, m):
        late = self.gap is not None and not (isinstance(g, int) and g == 0 and m < self.gap)
        count = self.base[m % self.n] + (self.per_group // self.n) * g + m // self.n - (self.late // self.n if late else 0)
        return count

    def bank(self, m):
        return self.banks[m % self.n]

    def wait_free(self, eng, g, m):
        eng.wait_ge(self.drained[m % self.n], self.before(g, m))

    def wait_drained(self, eng, g, m):
        eng.wait_ge(self.drained[m % self.n], self.before(g, m) + 1)

    def wait_filled(self, eng, g, m):
        if m < 0 and isinstance(g, int) and g == 0:
            return
        eng.wait_ge(self.filled[m % self.n], self.before(g, m) + 1)

    def fill(self, ins, m):
        ins.then_inc(self.filled[m % self.n], 1)

    def drain(self, ins, m):
        ins.then_inc(self.drained[m % self.n], 1)

    def end(self):
        return [x + (self.per_group // self.n) * self.groups for x in self.base]


def program(nc, a, out):
    top = ExitStack()
    with top:
        arena = top.enter_context(nc.sbuf_tensor("arena", [P, ARENA], F32))

        def sem(name):
            return top.enter_context(nc.semaphore(name))

        banks = [top.enter_context(nc.psum_tensor(f"bank{i}", [P, 512], F32)) for i in range(8)]
        filled = [sem(f"filled{i}") for i in range(8)]
        drained = [sem(f"drained{i}") for i in range(8)]
        count = [0] * 8

        def ring(first, n, per_group, gap=None, late=2, groups=G):
            ids = range(first, first + n)
            r = Ring([banks[i] for i in ids], [filled[i] for i in ids], [drained[i] for i in ids],
                     [count[i] for i in ids], per_group, gap, late, groups)
            for i, c in zip(ids, r.end()):
                count[i] = c
            return r

        big = Space(arena, 0, BIG)
        perm = Space(arena, BIG, BIG + PERM)
        h = big.take([T, G, GB, D])
        xres = big.take([T, G, GB, D])
        hnT = big.take([P, KD, G, GT])
        ident = perm.take([P, P])
        pows = perm.take([T, 3, GB])
        lnT = perm.take([P, KD, GT])
        zz = perm.take([T, GB, D])
        stats = perm.take([T, GB, 6])
        mv = perm.take([T, GB, 2])
        lnw = perm.take([T, 7, GB])
        gb = perm.take([P, 3, 2, KD])

        ln_stat, ln_mean, ln_chain, ln_row, ln_added = (
            sem(n) for n in ("ln_stat", "ln_mean", "ln_chain", "ln_row", "ln_added"))
        ln_out, ln_stored = sem("ln_out"), sem("ln_stored")
        ln_turn, dma_turn, load_turn = (sem(n) for n in ("ln_turn", "dma_turn", "load_turn"))
        const_ready = sem("const_ready")
        made = sem("made")
        out_stored = sem("out_stored")

        CH = 7

        def ln_vector_stats(src, g, l):
            if not (isinstance(l, int) and l == 0):
                nc.vector.wait_ge(ln_mean, l)
            nc.vector.sem_inc(ln_turn, 1)
            for b in range(GB):
                last = nc.vector.bn_stats(stats[:, b, :], src[:, g, b, :])
            last.then_inc(ln_stat, 1)

        def ln_vector_mean(v, l):
            v.wait_ge(ln_stat, l + 1)
            if not (isinstance(l, int) and l == 0):
                v.wait_ge(ln_chain, CH * l)
                v.wait_ge(ln_row, l)
            v.sem_inc(ln_turn, 1)
            for b in range(GB):
                last = nc.vector.bn_aggr(mv[:, b, :], stats[:, b, :])
            last.then_inc(ln_mean, 1)

        def ln_pool_rstd(pool, l, twice=True):
            gp = nc.gpsimd
            var = mv[:, :, 1]
            pool.wait_ge(ln_mean, l + 1)
            pool.wait_ge(ln_row, l)
            w = lnw

            def step(k, ins):
                ins.then_inc(ln_chain, 1)
                pool.wait_ge(ln_chain, CH * l + k)
            step(1, gp.tensor_tensor(w[:, 0, :], var, pows[:, 2, :], ALU.add))
            if not twice:
                gp.tensor_tensor(w[:, 1, :], w[:, 0, :], pows[:, 0, :], ALU.pow).then_inc(ln_chain, CH - 1)
                return
            step(2, gp.tensor_tensor(w[:, 1, :], w[:, 0, :], pows[:, 0, :], ALU.pow))
            step(3, gp.tensor_tensor(w[:, 2, :], w[:, 1, :], w[:, 1, :], ALU.mult))
            step(4, gp.tensor_tensor(w[:, 3, :], var, w[:, 2, :], ALU.mult))
            step(5, gp.tensor_tensor(w[:, 4, :], w[:, 3, :], pows[:, 2, :], ALU.add))
            step(6, gp.tensor_tensor(w[:, 5, :], w[:, 4, :], pows[:, 0, :], ALU.pow))
            gp.tensor_tensor(w[:, 6, :], w[:, 1, :], w[:, 5, :], ALU.mult).then_inc(ln_chain, 1)

        def ln_vector_rows(v, src, twice, g, l):
            v.wait_ge(ln_chain, CH * l + CH)
            if not (isinstance(l, int) and l == 0):
                v.wait_ge(ln_out, 2 * l)
            for b in range(GB):
                if twice:
                    nc.vector.tensor_scalar(xres[:, g, b, :], src[:, g, b, :], mv[:, b, 0:1], lnw[:, 1, b:b + 1],
                                            ALU.subtract, ALU.mult)
                r = lnw[:, 6 if twice else 1, b:b + 1]
                last = nc.vector.tensor_scalar(zz[:, b, :], src[:, g, b, :], mv[:, b, 0:1], r,
                                               ALU.subtract, ALU.mult)
            last.then_inc(ln_row, 1)

        def ln_pool_add(pool, add, g, l):
            pool.wait_ge(ln_row, l + 1)
            if add:
                nc.gpsimd.tensor_tensor(h[:, g, :, :], h[:, g, :, :], xres[:, g, :, :], ALU.add).then_inc(ln_added, 1)
            else:
                pool.sem_inc(ln_added, 1)

        def ln_tensor(pe, r, g, l, m):
            pe.wait_ge(ln_row, l + 1)
            for k in range(KD):
                r.wait_free(pe, g, m + k)
                for b in range(GB):
                    last = nc.tensor.transpose(r.bank(m + k)[:, b * T:(b + 1) * T], zz[:, b, k * P:(k + 1) * P],
                                               ident[0:T, 0:T])
                r.fill(last, m + k)

        def ln_scalar(act, r, g, l, m, which, dst_g=None):
            if dst_g is not None and not (isinstance(l, int) and l == 0):
                act.wait_ge(ln_stored, 16 * l)
            for k in range(KD):
                r.wait_filled(act, g, m + k)
                r.drain(nc.scalar.activation(lnT[:, k, :], r.bank(m + k)[:, 0:GT], ACT.Identity,
                                             bias=gb[:, which, 1, k:k + 1], scale=gb[:, which, 0, k:k + 1]), m + k)
                r.wait_drained(act, g, m + k)
                act.sem_inc(ln_out, 1)
            if dst_g is not None:
                act.dma_start(hnT[:, :, dst_g, :], lnT[:]).then_inc(ln_stored, 16)

        both = Space(arena, BIG + PERM, ARENA)
        prob = both.take([T, RING, GB, T])
        probT = both.take([T, RING, GT])
        mx = both.take([T, RING, GB])
        sm = both.take([T, RING, GB])
        inv = both.take([T, RING, GB])

        wB = {n: both.take([P, KD, D]) for n in ("wq2", "wk2", "wv2", "wp2")}
        bB = both.take([P, 3, KD])
        wB_loaded = sem("wB_loaded")
        work1 = Space(arena, both.at, ARENA)
        w = {n: work1.take(s) for n, s in (
            ("wdq", [P, KD, P]), ("wdkv", [P, KD, P]), ("wuq", [P, HID]), ("wuqs", [P, HID]),
            ("wuk", [P, HID]), ("wuks", [P, HID]), ("wuv", [P, HID]), ("woT", [P, NCH, D]),
            ("ropeC", [P, T]), ("ropeS", [P, T]), ("ropeCq", [P, T]), ("ropeSq", [P, T]))}
        scratch1 = work1.at
        cq = work1.take([P, GT])
        ckv = work1.take([P, GT])
        V = work1.take([T, GB, HID])
        qprod = work1.take([P, 2, GT])
        kprod = work1.take([P, 2, GT])
        qrot = work1.take([P, 2, GT])
        krot = work1.take([P, 2, 2, GT])
        oT = work1.take([P, NCH, GT])
        w1_loaded = sem("w1_loaded")
        work = Space(arena, scratch1, ARENA)
        wpT = work.take([P, KP, D])
        posb = work.take([P, D])
        tokb = work.take([P, D])
        patches = work.take([P, 2, KP, GB * IMG])
        x_loaded = [sem(f"x_loaded{i}") for i in range(2)]
        wp_loaded = sem("wp_loaded")
        re = ring(0, 2, 2)
        rn = ring(2, 2, 2)
        LAST = G // 2 - 1
        block = nc.Block()
        with block:
            @block.sync
            def _(sp):
                sp.dma_start(wpT, a["wpT"]).then_inc(wp_loaded, 16)
                sp.dma_start(patches[:, 0], a["patches"][0]).then_inc(x_loaded[0], 16)
                for dst, src in ((posb, "pos2"), (tokb, "tokb"), (ident, "ident"), (gb, "gb")):
                    sp.dma_start(dst, a[src]).then_inc(const_ready, 16)
                sp.dma_start(h[IMG:T].rearrange("p g b d -> p (g b) d"), a["txt"]).then_inc(const_ready, 16)
                sp.dma_start(patches[:, 1], a["patches"][1]).then_inc(x_loaded[1], 16)
                with sp.Fori(1, G // 2) as i:
                    for s in range(2):
                        sp.wait_ge(filled[1], 2 * i + s - 1)
                        sp.dma_start(patches[:, s], a["patches"][2 * i + s]).then_inc(x_loaded[s], 16)
                for n in w:
                    sp.dma_start(w[n], a[n]).then_inc(w1_loaded, 16)
                sp.wait_ge(w1_loaded, 16 * len(w))

            @block.tensor
            def _(pe):
                def embed(i, s):
                    g = 2 * i + s
                    pe.wait_ge(x_loaded[s % 2], 16 * (i + s // 2) + 16)
                    for p in range(2):
                        re.wait_free(pe, g, p)
                        for k in range(KP):
                            last = nc.tensor.matmul(re.bank(p)[:, 0:D], patches[:, s % 2, k, p * P:(p + 1) * P],
                                                    wpT[:, k, :], start=(k == 0), stop=(k == KP - 1))
                        re.fill(last, p)

                def pair(i, more):
                    for s in range(2):
                        if more:
                            embed(i, s + 2)
                        ln_tensor(pe, rn, 2 * i + s, 2 * i + s, 0)

                pe.wait_ge(wp_loaded, 16)
                embed(0, 0)
                embed(0, 1)
                pe.wait_ge(const_ready, 80)
                pair(0, True)
                with pe.Fori(1, LAST) as i:
                    pair(i, True)
                pair(LAST, False)

            @block.vector
            def _(v):
                def rows_in(g):
                    for p in range(2):
                        re.wait_filled(v, g, p)
                        for j in range(2):
                            rows = slice(j * IMG, (j + 1) * IMG)
                            last = nc.vector.tensor_tensor(h[0:IMG, g, 2 * p + j, :], re.bank(p)[rows, 0:D],
                                                           posb[rows, :], ALU.add)
                        re.drain(last, p)
                    for p in range(2):
                        re.wait_drained(v, g, p)
                    ln_vector_stats(h, g, g)

                def pair(i, more):
                    for s in range(2):
                        g = 2 * i + s
                        if s == 0 or more:
                            rows_in(g + 1)
                        ln_vector_rows(v, h, True, g, g)
                        if s == 0 or more:
                            ln_vector_mean(v, g + 1)

                v.wait_ge(const_ready, 80)
                nc.vector.memset(pows[:, 0, :], -0.5)
                nc.vector.memset(pows[:, 2, :], EPS)
                nc.vector.memset(pows[:, 1, :], -1.0).then_inc(made, 1)
                nc.vector.tensor_tensor(posb[:], posb[:], tokb[:], ALU.add).then_inc(made, 1)
                v.wait_ge(made, 2)
                rows_in(0)
                ln_vector_mean(v, 0)
                pair(0, True)
                with v.Fori(1, LAST) as i:
                    pair(i, True)
                pair(LAST, False)

            @block.gpsimd
            def _(pool):
                def turn(g, more):
                    if more:
                        ln_pool_rstd(pool, g + 1)
                    ln_pool_add(pool, True, g, g)

                pool.wait_ge(made, 1)
                ln_pool_rstd(pool, 0)
                turn(0, True)
                with pool.Fori(1, G - 1) as g:
                    turn(g, True)
                turn(G - 1, False)

            @block.scalar
            def _(act):
                act.wait_ge(const_ready, 80)
                ln_scalar(act, rn, 0, 0, 0, 0, 0)
                with act.Fori(1, G) as g:
                    ln_scalar(act, rn, g, g, 0, 0, g)
                act.wait_ge(ln_stored, 16 * G)

        att_max, att_sum, att_inv, att_norm, att_T = (
            sem(n) for n in ("att_max", "att_sum", "att_inv", "att_norm", "att_T"))
        def attention_vector_max(v, rs, seq, g, n):
            rs.wait_filled(v, g, n)
            sc = rs.bank(n)[0:T, 0:GT].rearrange("p (b k) -> p b k", b=GB)
            nc.vector.tensor_reduce(mx[:, n % RING, :], sc, AX_X, ALU.max, negate=True).then_inc(att_max, 1)

        def attention_scalar_exp(act, rs, rt, seq, g, n):
            s = n % RING
            act.wait_ge(att_max, seq(g, n) + 1)
            rt.wait_filled(act, g, n - RING)
            for b in range(GB):
                last = nc.scalar.activation(prob[:, s, b, :], rs.bank(n)[0:T, b * T:(b + 1) * T], ACT.Exp,
                                            bias=mx[:, s, b:b + 1])
            rs.drain(last, n)

        def attention_vector_sum(v, rs, seq, g, n):
            s = n % RING
            rs.wait_drained(v, g, n)
            nc.vector.tensor_reduce(sm[:, s, :], prob[:, s], AX_X, ALU.add).then_inc(att_sum, 1)
            v.wait_ge(att_sum, seq(g, n) + 1)
            nc.vector.reciprocal(inv[:, s, :], sm[:, s, :]).then_inc(att_inv, 1)

        def attention_pool_norm(pool, seq, g, n):
            s = n % RING
            pool.wait_ge(att_inv, seq(g, n) + 1)
            nc.gpsimd.tensor_tensor(prob[:, s], prob[:, s], inv[:, s, :].unsqueeze(2).broadcast_to([T, GB, T]),
                                    ALU.mult).then_inc(att_norm, 1)

        def attention_tensor_T(pe, rt, seq, g, n):
            s = n % RING
            pe.wait_ge(att_norm, seq(g, n) + 1)
            rt.wait_free(pe, g, n)
            for b in range(GB):
                last = nc.tensor.transpose(rt.bank(n)[0:T, b * T:(b + 1) * T], prob[:, s, b, :], ident[0:T, 0:T])
            rt.fill(last, n)

        def attention_scalar_T(act, rt, seq, g, n, pair):
            rt.wait_filled(act, g, n)
            pair((n - RING) // 2)
            nc.scalar.activation(probT[:, n % RING, :], rt.bank(n)[0:T, 0:GT], ACT.Copy).then_inc(att_T, 1)
            act.wait_ge(att_T, seq(g, n) + 1)
            act.sem_inc(rt.drained[n % rt.n], 1)

        rows_d = nc.dram_tensor("norm_rows", (B * T, D), F32, kind="Internal").ap()
        h_d = nc.dram_tensor("stream_rows", (G, T, GB * D), F32, kind="Internal").ap()
        list_d = nc.dram_tensor("token_list", (LIST, 1), I32, kind="Internal").ap()
        y_d = nc.dram_tensor("expert_rows", (TILES * P, D), F32, kind="Internal").ap()

        down, q_rot, k_rot, o_cols, z_made = (
            sem(n) for n in ("down", "q_rot", "k_rot", "o_cols", "z_made"))
        LT, LAV = 3, 5
        LN_STEP = 12
        LN_M = 4 * (NCH - 2)
        START_M = 4 * (NCH - 2) + 2
        N_START = 2 + 8 + 2 * GB
        ra = ring(0, 2, N_START, groups=1)
        rp = ring(0, 2, START_M + N_START, LN_M)
        for bank in range(2):
            count[bank] -= N_START // 2
        rs = ring(2, 2, NH)
        rt = ring(4, 1, NH)
        count[5] = 1
        ro = ring(5, 1, GB)
        rv = ring(6, 2, NCH)

        def start_items(g, first):
            return (ra, 0, 0) if first else (rp, g - 1, START_M)

        def proj_item(g, c, i, first):
            if c < 2:
                r_, gg, m0 = start_items(g, first)
                return r_, gg, m0 + (2, 8)[c] + i
            m = 4 * (c - 2) + i
            return rp, g, m if m < LN_M else m + 2

        def v_item(g, f, b, first):
            r_, gg, m0 = start_items(g, first)
            return r_, gg, m0 + (14 + b if f else 6 + b if b < 2 else 10 + b)

        START_AT = {13: "down", 14: "chunk0", 15: "V0", 16: "chunk1", 17: "V1", 20: "V2"}
        V_PARTS = {"V0": [(0, 0), (0, 1)], "V1": [(0, 2), (0, 3)], "V2": [(1, b) for b in range(GB)]}
        TAIL = LAV

        def seq(g, n):
            return NH * g + n

        block = nc.Block()
        with block:
            @block.sync
            def _(sp):
                for n in wB:
                    sp.dma_start(wB[n][:], a[n]).then_inc(wB_loaded, 16)
                sp.dma_start(bB[:], a["bB"]).then_inc(wB_loaded, 16)
                sp.wait_ge(wB_loaded, 16 * len(wB) + 16)

            @block.tensor
            def _(pe):
                def proj(g, c, i, first):
                    r_, gg, m = proj_item(g, c, i, first)
                    r_.wait_free(pe, gg, m)
                    lhsT = w[("wuq", "wuqs", "wuk", "wuks")[i]][:, c * P:(c + 1) * P]
                    r_.fill(nc.tensor.matmul(r_.bank(m)[:, 0:GT], lhsT, (cq, cq, ckv, ckv)[i][:],
                                             start=True, stop=True), m)

                def scores(g, n):
                    c, hh = n // 2, n % 2
                    if hh == 0:
                        pe.wait_ge(q_rot, NCH * g + c + 1)
                        pe.wait_ge(k_rot, NCH * g + c + 1)
                    rs.wait_free(pe, g, n)
                    for b in range(GB):
                        cols = slice(b * T, (b + 1) * T)
                        last = nc.tensor.matmul(rs.bank(n)[0:T, cols], qrot[:, c % 2, cols],
                                                krot[:, c % 2, hh, cols], start=True, stop=True)
                    rs.fill(last, n)

                def values(g, c):
                    rv.wait_free(pe, g, c)
                    pe.wait_ge(att_T, seq(g, 2 * c + 1) + 1)
                    for hh in range(2):
                        n = 2 * c + hh
                        for b in range(GB):
                            last = nc.tensor.matmul(
                                rv.bank(c)[hh * DH:(hh + 1) * DH, b * T:(b + 1) * T],
                                V[:, b, n * DH:(n + 1) * DH], probT[:, n % RING, b * T:(b + 1) * T],
                                start=True, stop=True)
                    rv.fill(last, c)

                def start(g, first, part):
                    r_, gg, m0 = start_items(g, first)
                    if part == "down":
                        for j, name in enumerate(("wdq", "wdkv")):
                            r_.wait_free(pe, gg, m0 + j)
                            for k in range(KD):
                                last = nc.tensor.matmul(r_.bank(m0 + j)[:, 0:GT], w[name][:, k, :], hnT[:, k, g, :],
                                                        start=(k == 0), stop=(k == KD - 1))
                            r_.fill(last, m0 + j)
                    elif part[:5] == "chunk":
                        pe.wait_ge(down, 2 * g + 2)
                        for i in range(4):
                            proj(g, int(part[5]), i, first)
                    else:
                        for f, b in V_PARTS[part]:
                            r_, gg, m = v_item(g, f, b, first)
                            r_.wait_free(pe, gg, m)
                            r_.fill(nc.tensor.matmul(r_.bank(m)[0:T, 0:512], ckv[:, b * T:(b + 1) * T],
                                                     w["wuv"][:, f * 512:(f + 1) * 512], start=True, stop=True), m)

                def lagging(g, n):
                    if 0 <= n - LT < NH:
                        attention_tensor_T(pe, rt, seq, g, n - LT)
                    if 0 <= n - LAV < NH and (n - LAV) % 2 == 1:
                        values(g, (n - LAV) // 2)

                def output(g, b):
                    pe.wait_ge(o_cols, NCH * g + NCH)
                    ro.wait_free(pe, g, b)
                    for c in range(NCH):
                        last = nc.tensor.matmul(ro.bank(b)[0:T, 0:D], oT[:, c, b * T:(b + 1) * T], w["woT"][:, c, :],
                                                start=(c == 0), stop=(c == NCH - 1))
                    ro.fill(last, b)

                def steps_end(g, n, more):
                    lagging(g, n)
                    if more and n in START_AT:
                        start(g + 1, False, START_AT[n])

                def body(g, norm, more):
                    for n in range(NH):
                        if n == LN_STEP and norm:
                            ln_tensor(pe, rp, g, G + g - 1, LN_M)
                        if n + 1 < NH:
                            scores(g, n + 1)
                        if n // 2 + 2 < NCH:
                            for i in range(2):
                                proj(g, n // 2 + 2, 2 * (n % 2) + i, False)
                        if n < GB and norm:
                            output(g - 1, n)
                        steps_end(g, n, more)
                    for n in range(NH, NH + TAIL):
                        steps_end(g, n, more)
                    if more:
                        scores(g + 1, 0)

                pe.wait_ge(w1_loaded, 16 * len(w))
                pe.wait_ge(z_made, 1)
                pe.sem_inc(filled[5], 1)
                for part in START_AT.values():
                    start(0, True, part)
                scores(0, 0)
                body(0, False, True)
                with pe.Fori(1, G - 1) as g:
                    body(g, True, True)
                body(G - 1, True, False)
                for b in range(GB):
                    output(G - 1, b)
                ln_tensor(pe, rp, G - 1, 2 * G - 1, START_M)

            @block.vector
            def _(v):
                def rope(g, c, i, first):
                    prod = (qprod, kprod)[i]
                    if not (first and c == 0):
                        v.wait_ge((q_rot, k_rot)[i], NCH * g + c)
                    for j, table in enumerate((("ropeCq", "ropeSq"), ("ropeC", "ropeS"))[i]):
                        r_, gg, m = proj_item(g, c, 2 * i + j, first)
                        r_.wait_filled(v, gg, m)
                        ins = nc.vector.tensor_tensor(
                            prod[:, j, :].rearrange("p (b t) -> p b t", b=GB),
                            r_.bank(m)[:, 0:GT].rearrange("p (b t) -> p b t", b=GB),
                            w[table][:].unsqueeze(1).broadcast_to([P, GB, T]), ALU.mult)
                        r_.drain(ins, m)
                    if i == 1:
                        for j in range(2):
                            r_, gg, m = proj_item(g, c, 2 * i + j, first)
                            r_.wait_drained(v, gg, m)
                        if not (first and c < 2):
                            rs.wait_filled(v, g, 2 * (c - 2) + 1)
                        for hh in range(2):
                            rows = slice(hh * DH, (hh + 1) * DH)
                            last = nc.vector.tensor_tensor(krot[rows, c % 2, hh, :], kprod[rows, 0, :],
                                                           kprod[rows, 1, :], ALU.add)
                        last.then_inc(k_rot, 1)

                def output(g, b):
                    ro.wait_filled(v, g, b)
                    ro.drain(nc.vector.tensor_tensor(h[:, g, b, :], h[:, g, b, :], ro.bank(b)[0:T, 0:D], ALU.add), b)
                    if b == GB - 1:
                        ro.wait_drained(v, g, b)

                def body(g, norm, more):
                    for n in range(NH):
                        if norm and n == 6:
                            ln_vector_stats(h, g - 1, G + g - 1)
                        if norm and n == 7:
                            ln_vector_mean(v, G + g - 1)
                        if norm and n == 9:
                            ln_vector_rows(v, h, True, g - 1, G + g - 1)
                        if 0 < n <= GB and norm:
                            output(g - 1, n - 1)
                        if n + 1 < NH:
                            attention_vector_max(v, rs, seq, g, n + 1)
                        if n // 2 + 2 < NCH:
                            rope(g, n // 2 + 2, n % 2, False)
                        elif n >= 14 and more:
                            rope(g + 1, 0, n % 2, False)
                        attention_vector_sum(v, rs, seq, g, n)
                    if more:
                        for i in range(2):
                            rope(g + 1, 1, i, False)
                        attention_vector_max(v, rs, seq, g + 1, 0)

                v.sem_inc(drained[5], 1)
                nc.vector.memset(krot[:], 0.0).then_inc(z_made, 1)
                v.wait_ge(z_made, 1)
                v.wait_ge(w1_loaded, 16 * len(w))
                v.wait_ge(ln_added, G)
                for c in range(2):
                    for i in range(2):
                        rope(0, c, i, True)
                attention_vector_max(v, rs, seq, 0, 0)
                body(0, False, True)
                with v.Fori(1, G - 1) as g:
                    body(g, True, True)
                body(G - 1, True, False)
                for b in range(GB):
                    output(G - 1, b)
                l = 2 * G - 1
                ln_vector_stats(h, G - 1, l)
                ln_vector_mean(v, l)
                ln_vector_rows(v, h, True, G - 1, l)

            @block.gpsimd
            def _(pool):
                def add_q(g, c, first):
                    for j in range(2):
                        r_, gg, m = proj_item(g, c, j, first)
                        r_.wait_drained(pool, gg, m)
                    if not (first and c < 2):
                        rs.wait_filled(pool, g, 2 * (c - 2) + 1)
                    nc.gpsimd.tensor_tensor(qrot[:, c % 2, :], qprod[:, 0, :], qprod[:, 1, :],
                                            ALU.add).then_inc(q_rot, 1)

                def body(g, norm, more):
                    for n in range(NH):
                        if n % 2 == 0 and n // 2 + 2 < NCH:
                            add_q(g, n // 2 + 2, False)
                        if norm and n == 7:
                            ln_pool_rstd(pool, G + g - 1)
                        if norm and n == 11:
                            ln_pool_add(pool, False, g - 1, G + g - 1)
                        if n == 15 and more:
                            add_q(g + 1, 0, False)
                        attention_pool_norm(pool, seq, g, n)
                    if more:
                        add_q(g + 1, 1, False)

                add_q(0, 0, True)
                add_q(0, 1, True)
                body(0, False, True)
                with pool.Fori(1, G - 1) as g:
                    body(g, True, True)
                body(G - 1, True, False)
                ln_pool_rstd(pool, 2 * G - 1)
                ln_pool_add(pool, False, G - 1, 2 * G - 1)

            @block.scalar
            def _(act):
                def lagging(g, n):
                    if 0 <= n - LT < NH:
                        attention_scalar_T(act, rt, seq, g, n - LT, lambda c: rv.wait_filled(act, g, c))
                    if 0 <= n - LAV < NH and (n - LAV) % 2 == 1:
                        c = (n - LAV) // 2
                        rv.wait_filled(act, g, c)
                        rv.drain(nc.scalar.activation(oT[:, c, :], rv.bank(c)[:, 0:GT], ACT.Copy), c)
                        rv.wait_drained(act, g, c)
                        act.sem_inc(o_cols, 1)

                def start(g, first, part):
                    r_, gg, m0 = start_items(g, first)
                    if part == "down":
                        for j, dst in enumerate((cq, ckv)):
                            r_.wait_filled(act, gg, m0 + j)
                            r_.drain(nc.scalar.activation(dst[:], r_.bank(m0 + j)[:, 0:GT], ACT.Copy), m0 + j)
                            r_.wait_drained(act, gg, m0 + j)
                            act.sem_inc(down, 1)
                    elif part in V_PARTS:
                        for f, b in V_PARTS[part]:
                            r_, gg, m = v_item(g, f, b, first)
                            r_.wait_filled(act, gg, m)
                            r_.drain(nc.scalar.activation(V[:, b, f * 512:(f + 1) * 512],
                                                          r_.bank(m)[0:T, 0:512], ACT.Copy), m)

                def steps_end(g, n, more):
                    lagging(g, n)
                    if more and n in START_AT:
                        start(g + 1, False, START_AT[n])

                def body(g, norm, more):
                    for n in range(NH):
                        if norm and n == LAV + 1:
                            ro.wait_filled(act, g - 1, GB - 1)
                        if n + 1 < NH:
                            attention_scalar_exp(act, rs, rt, seq, g, n + 1)
                        steps_end(g, n, more)
                        if norm and n == LN_STEP:
                            ln_scalar(act, rp, g, G + g - 1, LN_M, 1, g - 1)
                    for n in range(NH, NH + TAIL):
                        steps_end(g, n, more)
                    if more:
                        attention_scalar_exp(act, rs, rt, seq, g + 1, 0)

                act.wait_ge(w1_loaded, 16 * len(w))
                for part in START_AT.values():
                    start(0, True, part)
                attention_scalar_exp(act, rs, rt, seq, 0, 0)
                body(0, False, True)
                with act.Fori(1, G - 1) as g:
                    body(g, True, True)
                body(G - 1, True, False)
                ln_scalar(act, rp, G - 1, 2 * G - 1, START_M, 1, G - 1)
                act.wait_ge(ln_stored, 16 * 2 * G)

        low = Space(arena, 0, BIG)
        high = Space(arena, BIG + PERM, ARENA - E * KD * HID)
        W2 = low.take([P, E, KH, D])
        W1 = Space(arena, ARENA - E * KD * HID, ARENA).take([P, E, KD, HID])
        w1_early, w2_early = sem("w1_early"), sem("w2_early")

        rank = perm.take([T, G, GB, TOPK])
        expert = perm.take([T, G, GB, TOPK])
        weight = perm.take([T, G, GB, TOPK])
        total = perm.take([T, E])
        iota8 = perm.take([T, E])
        place_i = perm.take([T, G, GB, TOPK], I32)
        tile_e = perm.take([T, TILES], I32)
        tile_at = perm.take([T, TILES], I32)
        iota_t = perm.take([T, TILES])
        work = Space(arena, both.at, ARENA)
        slab = work.take([P, KD, GT])
        qT = work.take([P, KD, GT])
        kT = work.take([P, KD, GT])
        kmask = work.take([P, 2, GT])
        V2 = work.take([T, GB, NCH, 2, 2 * DM])
        yT = work.take([P, KD, GT])
        c2 = {n: work.take(sh) for n, sh in (
            ("hmask", [P, HC]), ("causal", [T, T]), ("bpb", [T, D]),
            ("gateW", [P, KD, E]), ("gateb", [T, E]), ("tri", [T, T]))}
        ones = work.take([T, T])
        ids = work.take([T, G, GB], I32)
        ids_g = work.take([T, GB], I32)
        identb = work.take([T, T], BF16)
        causalb = work.take([T, GB, T], BF16)
        lg = work.take([T, GB, E])
        best = work.take([T, GB, 8])
        topi = work.take([T, GB, 8], U32)
        gap = work.take([T, GB])
        ew = work.take([T, GB])
        den = work.take([T, GB])
        oh = work.take([T, TOPK, GB, E])
        ohs = work.take([T, GB, E])
        tot = work.take([T, GB, E])
        base = work.take([T, GB, E])
        rk = work.take([T, GB, E])
        picked = work.take([T, TOPK, GB, E])
        pos = work.take([T, GB, TOPK], I32)
        zeros_i = work.take([P, LIST // P])
        assert work.at <= ARENA - (E - 1) * KD * HID
        (w2_loaded, slab_loaded, q_ready, k_ready, kmasked, y_cols, bp_added, zz_stored, h_stored,
         gate_lg, gate_chain, gate_gap, gate_exp, gate_oh, pos_ready, scattered, list_zero, projected, t2) = (
            sem(n) for n in (
                "w2_loaded", "slab_loaded", "q_ready", "k_ready", "kmasked", "y_cols", "bp_added",
                "zz_stored", "h_stored", "gate_lg", "gate_chain", "gate_gap", "gate_exp", "gate_oh",
                "pos_ready", "scattered", "list_zero", "projected", "t2"))
        places_free = sem("places_free")
        LN_M, GATE_M, START_M, N_START = 2, 4, 6, 6
        LN2_STEP, GATE1_STEP, GATE2_STEP = 6, 8, 12
        ra = ring(0, 2, N_START, groups=1)
        rp = ring(0, 2, START_M + N_START, 0, START_M)
        for bank in range(2):
            count[bank] -= START_M // 2
        rs = ring(2, 2, NH)
        rt = ring(4, 2, NH)
        rv = ring(6, 2, NCH)

        def start_items(g, first):
            return (ra, 0, 0) if first else (rp, g - 1, START_M)

        def norm_items(g, last):
            return (rp, g, START_M) if last else (rp, g + 1, 0)

        n_pairs = NCH // KD

        def pair_item(j):
            return 2 * (j % n_pairs) + j // n_pairs

        GC = 15

        def seq2(g, n):
            return NH * (G + g) + n

        def norm_index(g):
            return 2 * G + g

        block = nc.Block()
        with block:
            @block.sync
            def _(sp):
                sp.dma_start(slab, hnT[:, :, 0, :]).then_inc(slab_loaded, 16)
                for n in c2:
                    sp.dma_start(c2[n], a[n]).then_inc(w2_loaded, 16)
                sp.dma_start(ids, a["ids"]).then_inc(w2_loaded, 16)
                sp.dma_start(iota8, a["iota8"]).then_inc(w2_loaded, 16)
                sp.dma_start(iota_t, a["iota_t"]).then_inc(w2_loaded, 16)
                sp.wait_ge(t2, 1)
                sp.dma_start(list_d.rearrange("(p n) o -> p (n o)", p=P), zeros_i.bitcast(I32)).then_inc(
                    list_zero, 16)

                def after(g):
                    sp.wait_ge(ln_row, norm_index(g) + 1)
                    sp.dma_start(rows_d.rearrange("(g b p) d -> g p b d", b=GB, p=T)[g], zz[:]).then_inc(zz_stored, 16)
                    sp.wait_ge(ln_added, norm_index(g) + 1)
                    sp.dma_start(h_d[g], h[:, g].rearrange("p b d -> p (b d)")).then_inc(h_stored, 16)

                def load_w2(e):
                    sp.wait_ge(h_stored, 32 * (e + 1))
                    for e_ in (e, E // 2 + e):
                        sp.dma_start(W2[:, e_], a["W2"][:, e_]).then_inc(w2_early, 16)

                sp.sem_inc(zz_stored, 1)
                sp.wait_ge(projected, 1)
                sp.dma_start(slab, hnT[:, :, 1, :]).then_inc(slab_loaded, 16)
                for e in range(1, E):
                    sp.dma_start(W1[:, e], a["W1"][:, e]).then_inc(w1_early, 16)
                for g in range(1, G - 1):
                    after(g - 1)
                    sp.wait_ge(projected, g + 1)
                    sp.dma_start(slab, hnT[:, :, g + 1, :]).then_inc(slab_loaded, 16)
                    if g >= 3 and g % 2:
                        load_w2((g - 3) // 2)
                load_w2(G // 2 - 2)
                after(G - 2)
                after(G - 1)
                load_w2(G // 2 - 1)
                sp.wait_ge(zz_stored, 16 * G + 1)
                sp.wait_ge(h_stored, 16 * G)

            @block.tensor
            def _(pe):
                def scores(g, n):
                    pe.wait_ge(kmasked, NH * g + n + 1)
                    rs.wait_free(pe, g, n)
                    nc.tensor.matmul(rs.bank(n)[0:T, 0:GT], identb, causalb.rearrange("p b k -> p (b k)"),
                                     start=True, stop=False)
                    for b in range(GB):
                        cols = slice(b * T, (b + 1) * T)
                        last = nc.tensor.matmul(rs.bank(n)[0:T, cols], qT[:, n // HC, cols],
                                                kmask[:, n % 2, cols], start=False, stop=(b == GB - 1))
                    rs.fill(last, n)

                def values(g, j):
                    m = 2 * j // HC
                    if 2 * j % HC == 0:
                        rv.wait_free(pe, g, pair_item(j))
                    pe.wait_ge(att_T, seq2(g, 2 * j + 1) + 1)
                    quad = (j % (HC // 2)) * 2 * DM
                    for b in range(GB):
                        for hh in range(2):
                            n = 2 * j + hh
                            last = nc.tensor.matmul(
                                rv.banks[m][quad:quad + 2 * DM, b * T:(b + 1) * T], V2[:, b, j, hh, :],
                                probT[:, n % RING, b * T:(b + 1) * T], start=(hh == 0), stop=(hh == 1))
                    rv.fill(last, pair_item(j))

                def gate(g, last_):
                    pe.wait_ge(ln_out, 2 * norm_index(g) + 2)
                    _, gg, m0 = norm_items(g, last_)
                    m = m0 + GATE_M
                    rp.wait_free(pe, gg, m)
                    for b in range(GB):
                        for k in range(KD):
                            last = nc.tensor.matmul(rp.bank(m)[0:T, b * E:(b + 1) * E],
                                                    lnT[:, k, b * T:(b + 1) * T], c2["gateW"][:, k, :],
                                                    start=(k == 0), stop=(k == KD - 1))
                    rp.fill(last, m)

                def prefix(g, last_):
                    pe.wait_ge(gate_oh, g + 1)
                    _, gg, m0 = norm_items(g, last_)
                    m = m0 + GATE_M + 1
                    rp.wait_free(pe, gg, m)
                    cols = ohs.rearrange("p b e -> p (b e)")
                    nc.tensor.matmul(rp.bank(m)[0:T, 0:GB * E], c2["tri"], cols, start=True, stop=True)
                    rp.fill(nc.tensor.matmul(rp.bank(m)[0:T, GB * E:2 * GB * E], ones, cols, start=True, stop=True), m)

                def lagging(g, n):
                    if 0 <= n - LT < NH:
                        attention_tensor_T(pe, rt, seq2, g, n - LT)
                    if 0 <= n - LAV < NH and (n - LAV) % 2 == 1:
                        values(g, (n - LAV) // 2)

                def start(g, first, between):
                    r_, gg, m0 = start_items(g, first)
                    pe.wait_ge(slab_loaded, 16 * g + 16)
                    for m in range(4):
                        r_.wait_free(pe, gg, m0 + m)
                        for k in range(KD):
                            last = nc.tensor.matmul(r_.bank(m)[:, 0:GT],
                                                    wB[("wq2", "wk2")[m // 2]][:, k, (m % 2) * P:(m % 2 + 1) * P],
                                                    slab[:, k, :], start=(k == 0), stop=(k == KD - 1))
                        r_.fill(last, m0 + m)
                        between(m)
                    between(4)
                    for j in range(2):
                        r_.wait_free(pe, gg, m0 + 4 + j)
                        for bb in range(2):
                            b = 2 * j + bb
                            for k in range(KD):
                                last = nc.tensor.matmul(r_.bank(4 + j)[0:T, bb * D:(bb + 1) * D],
                                                        slab[:, k, b * T:(b + 1) * T], wB["wv2"][:, k, :],
                                                        start=(k == 0), stop=(k == KD - 1))
                        r_.fill(last, m0 + 4 + j)
                    r_.wait_filled(pe, gg, m0 + 5)
                    pe.sem_inc(projected, 1)
                    pe.wait_ge(q_ready, KD * g + KD)
                    if first:
                        pe.wait_ge(w2_loaded, 16 * (len(c2) + 3))
                        pe.wait_ge(t2, 4)
                    scores(g, 0)

                def output(g, j, last_):
                    pe.wait_ge(y_cols, KD * g + KD)
                    _, gg, m0 = norm_items(g, last_)
                    rp.wait_free(pe, gg, m0 + j)
                    for bb in range(2):
                        b = 2 * j + bb
                        for k in range(KD):
                            last = nc.tensor.matmul(rp.bank(j)[0:T, bb * D:(bb + 1) * D],
                                                    yT[:, k, b * T:(b + 1) * T], wB["wp2"][:, k, :],
                                                    start=(k == 0), stop=(k == KD - 1))
                    rp.fill(last, m0 + j)

                def body(g, norm, more):
                    for n in range(NH):
                        if norm and n == LN2_STEP:
                            ln_tensor(pe, rp, g, norm_index(g - 1), LN_M)
                        if norm and n == GATE1_STEP:
                            gate(g - 1, False)
                        if norm and n == GATE2_STEP:
                            prefix(g - 1, False)
                        if n + 1 < NH:
                            scores(g, n + 1)
                        if norm and n < 2:
                            output(g - 1, n, False)
                        lagging(g, n)
                    if more:
                        start(g + 1, False, lambda k: lagging(g, NH + k))
                    else:
                        for k in range(LAV):
                            lagging(g, NH + k)

                start(0, True, lambda k: None)
                body(0, False, True)
                with pe.Fori(1, G - 1) as g:
                    body(g, True, True)
                body(G - 1, True, False)
                for j in range(2):
                    output(G - 1, j, True)
                ln_tensor(pe, rp, G - 1, norm_index(G - 1), START_M + LN_M)
                gate(G - 1, True)
                prefix(G - 1, True)

            @block.vector
            def _(v):
                def mask_keys(g, n):
                    if n % HC == 0:
                        v.wait_ge(k_ready, KD * g + n // HC + 1)
                    if not (n < 2 and isinstance(g, int) and g == 0):
                        rs.wait_filled(v, g, n - 2)
                    nc.vector.tensor_scalar(kmask[:, n % 2, :], kT[:, n // HC, :], c2["hmask"][:, n % HC:n % HC + 1],
                                            None, ALU.mult).then_inc(kmasked, 1)

                def gate_top(g, last_):
                    _, gg, m0 = norm_items(g, last_)
                    m = m0 + GATE_M
                    rp.wait_filled(v, gg, m)
                    rp.drain(nc.vector.tensor_tensor(
                        lg, rp.bank(m)[0:T, 0:GB * E].rearrange("p (b e) -> p b e", b=GB),
                        c2["gateb"].unsqueeze(1).broadcast_to([T, GB, E]), ALU.add), m)
                    rp.wait_drained(v, gg, m)
                    v.sem_inc(ln_turn, 1)
                    for b in range(GB):
                        last = nc.vector.max(best[:, b, :], lg[:, b, :])
                    last.then_inc(gate_lg, 1)

                def gate_index(g):
                    v.wait_ge(gate_lg, 2 * g + 1)
                    v.sem_inc(ln_turn, 1)
                    for b in range(GB):
                        last = nc.vector.max_index(topi[:, b, :], best[:, b, :], lg[:, b, :])
                    last.then_inc(gate_lg, 1)
                    nc.vector.tensor_tensor(gap, best[:, :, 1], best[:, :, 0], ALU.subtract).then_inc(gate_gap, 1)

                def gate_onehot(g):
                    v.wait_ge(gate_lg, 2 * g + 2)
                    ex = expert[:, g]
                    chain(v, g, 1, nc.vector.tensor_copy(ex, topi[:, :, 0:TOPK]))
                    for k in range(TOPK):
                        last = nc.vector.tensor_tensor(
                            oh[:, k], iota8.unsqueeze(1).broadcast_to([T, GB, E]),
                            expert[:, g, :, k].unsqueeze(2).broadcast_to([T, GB, E]), ALU.is_equal)
                    chain(v, g, 2, last)
                    nc.vector.tensor_tensor(ohs, oh[:, 0], oh[:, 1], ALU.add).then_inc(gate_oh, 1)

                def chain(v, g, k, ins):
                    ins.then_inc(gate_chain, 1)
                    v.wait_ge(gate_chain, GC * g + k)

                def gate_weights(g):
                    v.wait_ge(gate_exp, g + 1)
                    chain(v, g, 3, nc.vector.tensor_scalar(den, ew, 1.0, None, ALU.add))
                    chain(v, g, 4, nc.vector.reciprocal(weight[:, g, :, 0], den))
                    chain(v, g, 5, nc.vector.tensor_tensor(weight[:, g, :, 1], weight[:, g, :, 0], ew, ALU.mult))

                def gate_base(g, last_):
                    _, gg, m0 = norm_items(g, last_)
                    m = m0 + GATE_M + 1
                    rp.wait_filled(v, gg, m)
                    chain(v, g, 6, nc.vector.tensor_copy(
                        tot, rp.bank(m)[0:T, GB * E:2 * GB * E].rearrange("p (b e) -> p b e", b=GB)))
                    chain(v, g, 7, nc.vector.tensor_copy(base[:, 0], total))
                    for b in range(1, GB):
                        chain(v, g, 7 + b, nc.vector.tensor_tensor(base[:, b], base[:, b - 1], tot[:, b - 1], ALU.add))
                    chain(v, g, 11, nc.vector.tensor_tensor(total, base[:, GB - 1], tot[:, GB - 1], ALU.add))

                def gate_rank(g, last_):
                    _, gg, m0 = norm_items(g, last_)
                    m = m0 + GATE_M + 1
                    rp.drain(nc.vector.tensor_tensor(
                        rk, rp.bank(m)[0:T, 0:GB * E].rearrange("p (b e) -> p b e", b=GB), base, ALU.add), m)
                    rp.wait_drained(v, gg, m)
                    for k in range(TOPK):
                        last = nc.vector.tensor_tensor(picked[:, k], oh[:, k], rk, ALU.mult)
                    chain(v, g, 12, last)
                    for k in range(TOPK):
                        last = nc.vector.tensor_reduce(rank[:, g, :, k], picked[:, k], AX_X, ALU.add)
                    chain(v, g, 13, last)

                def gate_place(g):
                    v.wait_ge(places_free, g + 1)
                    chain(v, g, 14, nc.vector.scalar_tensor_tensor(
                        pos, expert[:, g], float(CAP), rank[:, g], ALU.mult, ALU.add))
                    chain(v, g, 15, nc.vector.tensor_copy(ids_g, ids[:, g]))
                    v.sem_inc(pos_ready, 1)

                def start(g):
                    mask_keys(g, 0)
                    mask_keys(g, 1)
                    attention_vector_max(v, rs, seq2, g, 0)

                def output(g, j, last_):
                    _, gg, m0 = norm_items(g, last_)
                    v.wait_ge(bp_added, g + 1)
                    rp.wait_filled(v, gg, m0 + j)
                    rows = xres[:, g, 2 * j:2 * j + 2, :]
                    rp.drain(nc.vector.tensor_tensor(
                        rows, rows, rp.bank(j)[0:T, :].rearrange("p (b d) -> p b d", b=2), ALU.add), m0 + j)
                    rp.wait_drained(v, gg, m0 + j)

                def body(g, norm, more):
                    for n in range(NH):
                        if norm and n == 2:
                            ln_vector_stats(xres, g - 1, norm_index(g - 1))
                        if norm and n == 3:
                            ln_vector_mean(v, norm_index(g - 1))
                        if norm and n == 5:
                            v.wait_ge(zz_stored, 16 * (g - 1) + 1)
                            ln_vector_rows(v, xres, False, g - 1, norm_index(g - 1))
                        if n + 2 < NH:
                            mask_keys(g, n + 2)
                        if n + 1 < NH:
                            attention_vector_max(v, rs, seq2, g, n + 1)
                        attention_vector_sum(v, rs, seq2, g, n)
                        if norm and n < 2:
                            output(g - 1, n, False)
                        if norm and n == GATE1_STEP:
                            gate_top(g - 1, False)
                        if norm and n == GATE1_STEP + 1:
                            gate_index(g - 1)
                        if norm and n == GATE1_STEP + 2:
                            gate_onehot(g - 1)
                        if norm and n == GATE2_STEP:
                            gate_weights(g - 1)
                        if norm and n == GATE2_STEP + 1:
                            gate_base(g - 1, False)
                        if norm and n == GATE2_STEP + 2:
                            gate_rank(g - 1, False)
                        if norm and n == GATE2_STEP + 3:
                            gate_place(g - 1)
                    if more:
                        start(g + 1)

                nc.vector.memset(zeros_i, 0.0).then_inc(t2, 1)
                nc.vector.memset(V2, 0.0)
                nc.vector.memset(total, 0.0)
                nc.vector.memset(ones, 1.0).then_inc(t2, 1)
                v.wait_ge(w2_loaded, 16 * (len(c2) + 3))
                nc.vector.tensor_copy(identb, ident[0:T, 0:T]).then_inc(t2, 1)
                nc.vector.tensor_copy(causalb, c2["causal"].unsqueeze(1).broadcast_to([T, GB, T])).then_inc(t2, 1)
                v.wait_ge(t2, 4)
                start(0)
                body(0, False, True)
                with v.Fori(1, G - 1) as g:
                    body(g, True, True)
                body(G - 1, True, False)
                for j in range(2):
                    output(G - 1, j, True)
                l = norm_index(G - 1)
                ln_vector_stats(xres, G - 1, l)
                ln_vector_mean(v, l)
                v.wait_ge(zz_stored, 16 * (G - 1) + 1)
                ln_vector_rows(v, xres, False, G - 1, l)
                gate_top(G - 1, True)
                gate_index(G - 1)
                gate_onehot(G - 1)
                gate_weights(G - 1)
                gate_base(G - 1, True)
                gate_rank(G - 1, True)
                gate_place(G - 1)

            @block.gpsimd
            def _(pool):
                def scatter(g):
                    pool.wait_ge(pos_ready, g + 1)
                    pool.sem_inc(dma_turn, 1)
                    for b in range(GB):
                        for k in range(TOPK):
                            nc.gpsimd.indirect_dma_start(
                                list_d, bass.IndirectOffsetOnAxis(ap=pos[:, b, k:k + 1], axis=0),
                                ids_g[:, b:b + 1], None).then_inc(scattered, 16)
                    pool.wait_ge(scattered, 16 * TOPK * GB * (g + 1))
                    pool.sem_inc(places_free, 1)

                def body(g, norm):
                    nc.gpsimd.tensor_tensor(xres[:, g], xres[:, g], c2["bpb"].unsqueeze(1).broadcast_to([T, GB, D]),
                                            ALU.add).then_inc(bp_added, 1)
                    for n in range(NH):
                        if norm and n == 4:
                            ln_pool_rstd(pool, norm_index(g - 1), twice=False)
                        attention_pool_norm(pool, seq2, g, n)
                        if norm and n == 7:
                            ln_pool_add(pool, True, g - 1, norm_index(g - 1))
                    if norm:
                        scatter(g - 1)

                pool.wait_ge(w2_loaded, 16 * (len(c2) + 3))
                pool.wait_ge(list_zero, 16)
                pool.sem_inc(places_free, 1)
                body(0, False)
                with pool.Fori(1, G) as g:
                    body(g, True)
                ln_pool_rstd(pool, norm_index(G - 1), twice=False)
                ln_pool_add(pool, True, G - 1, norm_index(G - 1))
                scatter(G - 1)

            @block.scalar
            def _(act):
                def pair(g):
                    def wait(c):
                        if c >= 0:
                            rv.wait_filled(act, g, pair_item(c))
                        elif not (isinstance(g, int) and g == 0):
                            rv.wait_filled(act, g - 1, pair_item(c + NCH))
                    return wait

                def lagging(g, n):
                    if 0 <= n - LT < NH:
                        attention_scalar_T(act, rt, seq2, g, n - LT, pair(g))
                    if 0 <= n - LAV < NH and (n - LAV) % HC == HC - 1:
                        m = (n - LAV) // HC
                        rv.wait_filled(act, g, pair_item(n_pairs * m + n_pairs - 1))
                        nc.scalar.activation(yT[:, m, :], rv.banks[m][:, 0:GT], ACT.Identity,
                                             bias=bB[:, 2, m:m + 1]).then_inc(rv.drained[m], n_pairs)
                        act.wait_ge(rv.drained[m], rv.before(g, m) + n_pairs)
                        act.sem_inc(y_cols, 1)

                def start(g, first, between):
                    r_, gg, m0 = start_items(g, first)
                    if not first:
                        rs.wait_filled(act, g - 1, NH - 1)
                    for m in range(4):
                        dst, done, bias = (qT, q_ready, bB[:, 0, m % 2:m % 2 + 1]) if m < 2 else (
                            kT, k_ready, bB[:, 1, m % 2:m % 2 + 1])
                        r_.wait_filled(act, gg, m0 + m)
                        r_.drain(nc.scalar.activation(dst[:, m % 2, :], r_.bank(m)[:, 0:GT], ACT.Identity, bias=bias), m)
                        r_.wait_drained(act, gg, m0 + m)
                        act.sem_inc(done, 1)
                        between(m)
                    between(4)
                    for j in range(2):
                        r_.wait_filled(act, gg, m0 + 4 + j)
                        src = r_.bank(4 + j)[0:T, :].rearrange("p (b n h d) -> p b n h d", b=2, n=NCH, h=2)
                        for bb in range(2):
                            for hh in range(2):
                                last = nc.scalar.activation(
                                    V2[:, 2 * j + bb, :, hh, hh * DM:(hh + 1) * DM], src[:, bb, :, hh, :], ACT.Copy)
                        r_.drain(last, 4 + j)
                    attention_scalar_exp(act, rs, rt, seq2, g, 0)

                def body(g, norm, more):
                    for n in range(NH):
                        if norm and n == GATE1_STEP + 3:
                            act.wait_ge(gate_gap, g)
                            nc.scalar.activation(ew, gap, ACT.Exp).then_inc(gate_exp, 1)
                        if n + 1 < NH:
                            attention_scalar_exp(act, rs, rt, seq2, g, n + 1)
                        lagging(g, n)
                        if norm and n == LN2_STEP:
                            ln_scalar(act, rp, g, norm_index(g - 1), LN_M, 2)
                    if more:
                        start(g + 1, False, lambda k: lagging(g, NH + k))
                    else:
                        for k in range(LAV):
                            lagging(g, NH + k)

                act.wait_ge(w2_loaded, 16 * (len(c2) + 3))
                act.wait_ge(t2, 2)
                start(0, True, lambda k: None)
                body(0, False, True)
                with act.Fori(1, G - 1) as g:
                    body(g, True, True)
                body(G - 1, True, False)
                ln_scalar(act, rp, G - 1, norm_index(G - 1), START_M + LN_M, 2)
                act.wait_ge(gate_gap, G)
                nc.scalar.activation(ew, gap, ACT.Exp).then_inc(gate_exp, 1)

        AHEAD = 4
        QUADS = TILES // AHEAD
        b2 = low.take([P, E, D])
        b1 = high.take([P, E, HID])
        route = Space(arena, low.at, BIG)
        X = high.take([P, AHEAD, D])
        xT = high.take([P, 2, KD, P])
        yt = high.take([P, 2, D])
        mid = low.take([P, 2, HID])
        midT = low.take([P, 2, KH, P])
        idx = high.take([P, AHEAD], I32)
        n1 = route.take([T, E])
        n1i = route.take([T, E], I32)
        n2i = route.take([T, E], I32)
        n2 = route.take([T, E])
        ends = route.take([T, E + 1])
        start = route.take([T, E])
        NTOK = G * GB * TOPK
        sel = route.take([T, NTOK, E])
        selv = route.take([T, NTOK, E])
        stok = route.take([T, NTOK])
        past = route.take([T, TILES, E])
        pastv = route.take([T, TILES, E])
        te = route.take([T, TILES])
        tef = route.take([T, TILES])
        tst = route.take([T, TILES])
        toff = route.take([T, TILES])
        toff2 = route.take([T, TILES])
        hidden_loaded, b2_loaded, routed, xT_ready, gelu_done, y_ready = (
            sem(n) for n in ("hidden_loaded", "b2_loaded", "routed", "xT_ready", "gelu_done", "y_ready"))
        gathered = [sem(f"gathered{s}") for s in range(AHEAD)]
        idx_loaded = [sem(f"idx_loaded{s}") for s in range(AHEAD)]
        y_stored = [sem(f"y_stored{s}") for s in range(2)]
        ROUTE = 17 + E
        rx = ring(0, 2, 4, groups=QUADS)
        r1 = ring(2, 2, 8, groups=QUADS)
        rm = ring(4, 2, 8, groups=QUADS)
        r2 = ring(6, 2, 4, groups=QUADS)

        block = nc.Block()
        with block:
            @block.sync
            def _(sp):
                sp.dma_start(W1[:, 0], a["W1"][:, 0]).then_inc(hidden_loaded, 16)
                sp.dma_start(b1, a["b1"]).then_inc(hidden_loaded, 16)
                sp.dma_start(b2, a["b2"]).then_inc(b2_loaded, 16)
                sp.wait_ge(routed, ROUTE)

                def load_idx(i, s):
                    t = AHEAD * i + s
                    if not (isinstance(i, int) and t < AHEAD):
                        sp.wait_ge(gathered[s % AHEAD], 16 * (i + s // AHEAD))
                    at = sp.value_load(tile_at[0:1, bass.ds(t, 1)], min_val=0, max_val=LIST - P)
                    sp.dma_start(idx[:, s % AHEAD:s % AHEAD + 1], list_d[bass.ds(at, P), :]).then_inc(
                        idx_loaded[s % AHEAD], 16)

                def store(i, s):
                    t = AHEAD * i + s
                    sp.wait_ge(y_ready, t + 1)
                    sp.dma_start(y_d[bass.ds(t * P, P), :], yt[:, s % 2, :]).then_inc(y_stored[s % 2], 16)

                for s in range(AHEAD):
                    load_idx(0, s)
                with sp.Fori(0, QUADS - 1) as i:
                    for s in range(AHEAD):
                        load_idx(i, s + AHEAD)
                        store(i, s)
                for s in range(AHEAD):
                    store(QUADS - 1, s)
                for s in range(2):
                    sp.wait_ge(y_stored[s], 16 * TILES // 2)

            @block.gpsimd
            def _(pool):
                def gather(i, s):
                    pool.wait_ge(idx_loaded[s], 16 * i + 16)
                    if not (isinstance(i, int) and i == 0):
                        rx.wait_filled(pool, i, s - AHEAD)
                    pool.sem_inc(dma_turn, 1)
                    nc.gpsimd.indirect_dma_start(X[:, s, :], None, rows_d,
                                                 bass.IndirectOffsetOnAxis(ap=idx[:, s:s + 1], axis=0)
                                                 ).then_inc(gathered[s], 16)

                for s in range(AHEAD):
                    gather(0, s)
                with pool.Fori(1, QUADS) as i:
                    for s in range(AHEAD):
                        gather(i, s)

            @block.tensor
            def _(pe):
                def rows(i, s):
                    pe.wait_ge(gathered[s % AHEAD], 16 * (i + s // AHEAD) + 16)
                    rx.wait_free(pe, i, s)
                    for k in range(KD):
                        last = nc.tensor.transpose(rx.bank(s)[:, k * P:(k + 1) * P], X[:, s % AHEAD, k * P:(k + 1) * P],
                                                   ident[:])
                    rx.fill(last, s)

                def hidden(i, s):
                    pe.wait_ge(xT_ready, AHEAD * i + s + 1)
                    pe.sem_inc(load_turn, 1)
                    e = pe.value_load(tile_e[0:1, bass.ds(AHEAD * i + s, 1)], min_val=0, max_val=E - 1)
                    for f in range(2):
                        m = 2 * s + f
                        r1.wait_free(pe, i, m)
                        for k in range(KD):
                            last = nc.tensor.matmul(r1.bank(m)[:, 0:512], xT[:, s % 2, k, :],
                                                    W1[:, bass.ds(e, 1), k, f * 512:(f + 1) * 512],
                                                    start=(k == 0), stop=(k == KD - 1))
                        r1.fill(last, m)

                def turn(i, s):
                    pe.wait_ge(gelu_done, AHEAD * i + s + 1)
                    for f in range(2):
                        m = 2 * s + f
                        rm.wait_free(pe, i, m)
                        for j in range(4):
                            last = nc.tensor.transpose(rm.bank(m)[:, j * P:(j + 1) * P],
                                                       mid[:, s % 2, (4 * f + j) * P:(4 * f + j + 1) * P], ident[:])
                        rm.fill(last, m)

                def result(i, s):
                    for f in range(2):
                        m = 2 * s + f
                        pe.wait_ge(rm.drained[f], rm.before(i, m) + 1)
                    pe.sem_inc(load_turn, 1)
                    e = pe.value_load(tile_e[0:1, bass.ds(AHEAD * i + s, 1)], min_val=0, max_val=E - 1)
                    r2.wait_free(pe, i, s)
                    for k in range(KH):
                        last = nc.tensor.matmul(r2.bank(s)[:, 0:D], midT[:, s % 2, k, :], W2[:, bass.ds(e, 1), k, :],
                                                start=(k == 0), stop=(k == KH - 1))
                    r2.fill(last, s)

                pe.wait_ge(routed, ROUTE)
                rows(0, 0)
                rows(0, 1)
                pe.wait_ge(w1_early, 16 * (E - 1))
                pe.wait_ge(hidden_loaded, 32)
                hidden(0, 0)
                pe.wait_ge(w2_early, 16 * E)
                with pe.Fori(0, QUADS - 1) as i:
                    for s in range(AHEAD):
                        rows(i, s + 2)
                        turn(i, s)
                        hidden(i, s + 1)
                        result(i, s)
                for s in range(AHEAD):
                    if s + 2 < AHEAD:
                        rows(QUADS - 1, s + 2)
                    turn(QUADS - 1, s)
                    if s + 1 < AHEAD:
                        hidden(QUADS - 1, s + 1)
                    result(QUADS - 1, s)

            @block.vector
            def _(v):
                vec = nc.vector
                done = [0]

                def chain(ins):
                    done[0] += 1
                    ins.then_inc(routed, 1)
                    v.wait_ge(routed, done[0])

                chain(vec.tensor_scalar(n1, total, float(P - 1), None, ALU.add))
                chain(vec.tensor_copy(n1i, n1))
                chain(vec.tensor_scalar(n2i, n1i, 7, None, ALU.arith_shift_right))
                chain(vec.tensor_copy(n2, n2i))
                chain(vec.memset(ends, 0.0))
                for e in range(E):
                    chain(vec.tensor_tensor(ends[:, e + 1:e + 2], ends[:, e:e + 1], n2[:, e:e + 1], ALU.add))
                chain(vec.tensor_scalar(start, ends[:, 0:E], float(P), None, ALU.mult))
                flat = expert.rearrange("p g b k -> p (g b k)")
                chain(vec.tensor_tensor(sel, iota8.unsqueeze(1).broadcast_to([T, NTOK, E]),
                                        flat.unsqueeze(2).broadcast_to([T, NTOK, E]), ALU.is_equal))
                chain(vec.tensor_tensor(selv, sel, start.unsqueeze(1).broadcast_to([T, NTOK, E]), ALU.mult))
                chain(vec.tensor_reduce(stok, selv, AX_X, ALU.add))
                vec.tensor_tensor(place_i.rearrange("p g b k -> p (g b k)"), stok,
                                  rank.rearrange("p g b k -> p (g b k)"), ALU.add)
                last_end = ends[:, 1:E + 1].unsqueeze(1).broadcast_to([T, TILES, E])
                chain(vec.tensor_tensor(past, iota_t.unsqueeze(2).broadcast_to([T, TILES, E]), last_end, ALU.is_ge))
                chain(vec.tensor_tensor(pastv, past, last_end, ALU.mult))
                vec.tensor_reduce(te, past, AX_X, ALU.add)
                chain(vec.tensor_reduce(tst, pastv, AX_X, ALU.max))
                chain(vec.tensor_scalar(tef, te, float(E - 1), None, ALU.min))
                vec.tensor_copy(tile_e, tef)
                chain(vec.tensor_tensor(toff, iota_t, tst, ALU.subtract))
                chain(vec.tensor_scalar(toff2, toff, float(P), None, ALU.mult))
                chain(vec.scalar_tensor_tensor(tile_at, tef, float(CAP), toff2, ALU.mult, ALU.add))
                assert done[0] == ROUTE - 1, done
                vec.memset(idx.bitcast(F32), 0.0).then_inc(routed, 1)
                v.wait_ge(routed, ROUTE)
                v.wait_ge(hidden_loaded, 32)
                v.wait_ge(b2_loaded, 16)

                def add_b1(i, s):
                    e = v.value_load(tile_e[0:1, bass.ds(AHEAD * i + s, 1)], min_val=0, max_val=E - 1)
                    if not (isinstance(i, int) and AHEAD * i + s < 2):
                        for f in range(2):
                            rm.wait_filled(v, i, 2 * (s - 2) + f)
                    for f in range(2):
                        m = 2 * s + f
                        r1.wait_filled(v, i, m)
                        r1.drain(vec.tensor_tensor(mid[:, s % 2, f * 512:(f + 1) * 512], r1.bank(m)[:, 0:512],
                                                   b1[:, bass.ds(e, 1), f * 512:(f + 1) * 512], ALU.add), m)

                def midT_out(i, s):
                    m = 2 * s + 1
                    rm.wait_filled(v, i, m)
                    if not (isinstance(i, int) and AHEAD * i + s < 2):
                        r2.wait_filled(v, i, s - 2)
                    rm.drain(vec.tensor_copy(midT[:, s % 2, 4:8, :].rearrange("p k t -> p (k t)"), rm.bank(m)[:, 0:512]), m)

                def add_b2(i, s):
                    e = v.value_load(tile_e[0:1, bass.ds(AHEAD * i + s, 1)], min_val=0, max_val=E - 1)
                    if not (isinstance(i, int) and AHEAD * i + s < 2):
                        v.wait_ge(y_stored[s % 2], 16 * (AHEAD // 2 * i + s // 2))
                    r2.wait_filled(v, i, s)
                    r2.drain(vec.tensor_tensor(yt[:, s % 2, :], r2.bank(s)[:, 0:D], b2[:, bass.ds(e, 1), :], ALU.add), s)
                    v.wait_ge(r2.drained[s % 2], r2.before(i, s) + 1)
                    v.sem_inc(y_ready, 1)

                def step(i, s, more):
                    midT_out(i, s)
                    if more:
                        add_b1(i, s + 1)
                    add_b2(i, s)

                add_b1(0, 0)
                for s in range(AHEAD):
                    step(0, s, True)
                with v.Fori(1, QUADS - 1) as i:
                    for s in range(AHEAD):
                        step(i, s, True)
                for s in range(AHEAD):
                    step(QUADS - 1, s, s + 1 < AHEAD)

            @block.scalar
            def _(act):
                def rows_out(i, s):
                    rx.wait_filled(act, i, s)
                    if not (isinstance(i, int) and AHEAD * i + s < 2):
                        r1.wait_filled(act, i, 2 * (s - 2) + 1)
                    for k in range(KD):
                        last = nc.scalar.activation(xT[:, s % 2, k, :], rx.bank(s)[:, k * P:(k + 1) * P], ACT.Identity,
                                                    bias=gb[:, 2, 1, k:k + 1], scale=gb[:, 2, 0, k:k + 1])
                    rx.drain(last, s)
                    act.wait_ge(rx.drained[s % 2], rx.before(i, s) + 1)
                    act.sem_inc(xT_ready, 1)

                def gelu(i, s):
                    for f in range(2):
                        m = 2 * s + f
                        act.wait_ge(r1.drained[f], r1.before(i, m) + 1)
                    nc.scalar.activation(mid[:, s % 2, :], mid[:, s % 2, :], ACT.Gelu).then_inc(gelu_done, 1)

                def midT_out(i, s):
                    m = 2 * s
                    rm.wait_filled(act, i, m)
                    if not (isinstance(i, int) and AHEAD * i + s < 2):
                        r2.wait_filled(act, i, s - 2)
                    rm.drain(nc.scalar.activation(midT[:, s % 2, 0:4, :].rearrange("p k t -> p (k t)"),
                                                  rm.bank(m)[:, 0:512], ACT.Copy), m)

                def step(i, s, rows, more):
                    if rows:
                        rows_out(i, s + 2)
                    midT_out(i, s)
                    if more:
                        gelu(i, s + 1)

                rows_out(0, 0)
                rows_out(0, 1)
                gelu(0, 0)
                for s in range(AHEAD):
                    step(0, s, True, True)
                with act.Fori(1, QUADS - 1) as i:
                    for s in range(AHEAD):
                        step(i, s, True, True)
                for s in range(AHEAD):
                    step(QUADS - 1, s, s + 2 < AHEAD, s + 1 < AHEAD)

        late = Space(arena, BIG + PERM, ARENA)
        wg = late.take([P, KD, FFN])
        wu = late.take([P, KD, FFN])
        wd = late.take([P, KF, D])
        wave = Space(arena, late.at, ARENA)
        wqk = wave.take([P, KD, 4 * D])
        wout = wave.take([P, KD, D])
        bias_kv = wave.take([T, 2 * D])
        biasqg = wave.take([P, 4])
        bout = wave.take([T, D])
        toep = wave.take([T, NH, T])
        mixT = wave.take([P, KD, D])
        yg = wave.take([T, GB, TOPK, D])
        pg = wave.take([T, GB, TOPK], I32)
        h_first, h_back, kernel_loaded, pg_ready, y_in = (
            sem(n) for n in ("h_first", "h_back", "kernel_loaded", "pg_ready", "y_in"))

        def gather(pool, g):
            pool.wait_ge(pg_ready, g + 1)
            pool.sem_inc(dma_turn, 1)
            for b in range(GB):
                for k in range(TOPK):
                    nc.gpsimd.indirect_dma_start(
                        yg[:, b, k, :], None, y_d,
                        bass.IndirectOffsetOnAxis(ap=pg[:, b, k:k + 1], axis=0)).then_inc(y_in, 16)

        setup = Space(arena, B * D, 2 * B * D)
        LAGS = 2 * T
        lag = setup.take([NH, FIELD])
        pw = setup.take([NH, 3])
        fc = setup.take([NH, NH])
        dmask = setup.take([P, DM])
        sp_ = setup.take([NH, 8])
        arg = setup.take([NH, FIELD])
        turns = setup.take([NH, FIELD])
        env = setup.take([NH, FIELD])
        kernel_rows = setup.take([NH, LAGS])
        nrm = setup.take([NH, 3])
        cst = setup.take([NH, 4])
        cx = setup.take([NH, 2, NH])
        cb = setup.take([NH, NH, DM])
        toep_d = nc.dram_tensor("toeplitz", (NH, T * LAGS), F32, kind="Internal").ap()
        w4_loaded, raw_loaded, built, act_in, act_built, pe_built, toep_stored, toep_loaded = (
            sem(n) for n in ("w4_loaded", "raw_loaded", "built", "act_in", "act_built", "pe_built", "toep_stored",
                             "toep_loaded"))
        ARG_AT, CX_AT, ALPHA_AT, CB_AT, KERNEL_AT, MIX_AT = 11, 13, 21, 24, 32, 33
        PI2 = 2 * np.pi
        C1 = 6.28125
        C2 = float(np.float32(np.floor((PI2 - C1) * 2 ** 21) / 2 ** 21))
        C3 = float(np.float32(PI2 - C1 - C2))
        ROUND = 12582912.0
        kernel_loads = [(lag, "lag"), (pw, "pw"), (fc, "fc"), (dmask, "dmask")]
        loads = [(wqk, "wqk"), (bias_kv, "bias_kv"), (biasqg, "biasqg"), (wout, "wout4"), (bout, "bout")]
        raws = [(wg, "wg_i"), (wu, "wu_i"), (wd, "wd_i")]

        def kernels_vector(v):
            vec = nc.vector
            n = [0]

            def chain(ins):
                n[0] += 1
                ins.then_inc(built, 1)
                v.wait_ge(built, n[0])

            col = sp_
            damp = pw[:, 1:2]
            chain(vec.tensor_scalar(col[:, 0:1], damp, -1.0, None, ALU.mult))
            chain(vec.tensor_tensor(col[:, 1:2], col[:, 0:1], damp, ALU.min))
            chain(vec.tensor_scalar(arg, lag, pw[:, 0:1], pw[:, 2:3], ALU.mult, ALU.add))
            chain(vec.tensor_scalar(turns, arg, float(1 / PI2), ROUND, ALU.mult, ALU.add))
            chain(vec.tensor_scalar(turns, turns, -ROUND, None, ALU.add))
            for c in (C1, C2, C3):
                chain(vec.scalar_tensor_tensor(arg, turns, -c, arg, ALU.mult, ALU.add))
            chain(vec.tensor_scalar(turns, arg, -1.0, None, ALU.mult))
            chain(vec.tensor_tensor(arg, arg, turns, ALU.min))
            chain(vec.tensor_scalar(arg, arg, float(np.pi / 2), float(-np.pi / 2), ALU.add, ALU.max))
            assert n[0] == ARG_AT
            chain(vec.tensor_reduce(cst[:, 0:1], fc, AX_X, ALU.max))
            chain(vec.tensor_scalar(cx[:, 0], fc, cst[:, 0:1], None, ALU.subtract))
            assert n[0] == CX_AT
            v.wait_ge(act_built, 1)
            chain(vec.tensor_scalar(col[:, 4:5], col[:, 2:3], 1.0, -1.0, ALU.add, ALU.add))
            chain(vec.tensor_scalar(col[:, 5:6], col[:, 4:5], 0.0, None, ALU.is_equal))
            vec.tensor_tensor(col[:, 4:5], col[:, 4:5], col[:, 5:6], ALU.add)
            chain(vec.tensor_tensor(col[:, 3:4], col[:, 3:4], col[:, 5:6], ALU.add))
            chain(vec.reciprocal(col[:, 6:7], col[:, 4:5]))
            chain(vec.tensor_tensor(col[:, 3:4], col[:, 3:4], col[:, 6:7], ALU.mult))
            chain(vec.tensor_tensor(col[:, 3:4], col[:, 3:4], col[:, 2:3], ALU.mult))
            chain(vec.scalar_tensor_tensor(col[:, 7:8], damp, 0.0, col[:, 3:4], ALU.max, ALU.add))
            chain(vec.tensor_scalar(col[:, 6:7], col[:, 7:8], -1.0, None, ALU.mult))
            assert n[0] == ALPHA_AT
            v.wait_ge(act_built, 2)
            chain(vec.tensor_reduce(cst[:, 1:2], cx[:, 1], AX_X, ALU.add))
            chain(vec.reciprocal(cst[:, 2:3], cst[:, 1:2]))
            chain(vec.tensor_scalar(cb, cx[:, 1].unsqueeze(2).broadcast_to([NH, NH, DM]), cst[:, 2:3], None, ALU.mult))
            assert n[0] == CB_AT
            v.wait_ge(act_built, 4)
            chain(vec.tensor_tensor(arg, env, turns, ALU.mult))
            chain(vec.tensor_scalar(turns, arg, -1.0, None, ALU.mult))
            chain(vec.tensor_tensor(env, arg, turns, ALU.max))
            chain(vec.tensor_reduce(nrm[:, 0:1], env, AX_X, ALU.add))
            chain(vec.tensor_scalar(nrm[:, 1:2], nrm[:, 0:1], 1e-8, None, ALU.max))
            chain(vec.reciprocal(nrm[:, 2:3], nrm[:, 1:2]))
            chain(vec.memset(kernel_rows, 0.0))
            chain(vec.tensor_scalar(kernel_rows[:, 0:T], arg[:, 0:T], nrm[:, 2:3], None, ALU.mult))
            assert n[0] == KERNEL_AT
            v.wait_ge(pe_built, 1)
            for k in range(KD):
                last = vec.tensor_tensor(mixT[:, k, :].rearrange("p (i d) -> p i d", d=DM),
                                         banks[7][:, k * NH:(k + 1) * NH].unsqueeze(2).broadcast_to([P, NH, DM]),
                                         dmask.unsqueeze(1).broadcast_to([P, NH, DM]), ALU.mult)
            chain(last)
            assert n[0] == MIX_AT

        def kernels_scalar(act):
            act.wait_ge(built, 2)
            nc.scalar.activation(sp_[:, 2:3], sp_[:, 1:2], ACT.Exp).then_inc(act_in, 1)
            act.wait_ge(act_in, 1)
            nc.scalar.activation(sp_[:, 3:4], sp_[:, 2:3], ACT.Ln, bias=1.0).then_inc(act_built, 1)
            act.wait_ge(built, CX_AT)
            nc.scalar.activation(cx[:, 1], cx[:, 0], ACT.Exp).then_inc(act_built, 1)
            act.wait_ge(built, ALPHA_AT)
            nc.scalar.activation(env, lag, ACT.Exp, scale=sp_[:, 6:7]).then_inc(act_built, 1)
            nc.scalar.activation(turns, arg, ACT.Sin).then_inc(act_built, 1)

        def kernels_tensor(pe):
            pe.wait_ge(built, CB_AT)
            for k in range(KD):
                last = nc.tensor.transpose(banks[7][:, k * NH:(k + 1) * NH],
                                           cb.rearrange("p j d -> p (j d)")[:, k * P:(k + 1) * P], ident[0:NH, 0:NH])
            last.then_inc(pe_built, 1)

        def kernels_sync(sp):
            sp.wait_ge(built, KERNEL_AT)
            sp.dma_start(toep_d.rearrange("j (s l) -> j s l", l=LAGS),
                         kernel_rows.unsqueeze(1).broadcast_to([NH, T, LAGS])).then_inc(toep_stored, 16)
            sp.wait_ge(toep_stored, 16)
            sp.dma_start(toep, toep_d[:, 0:T * (LAGS - 1)].rearrange("j (s l) -> s j l", l=LAGS - 1)[:, :, 0:T]
                         ).then_inc(toep_loaded, 16)

        tile4 = Space(arena, wave.at, ARENA)
        slab = tile4.take([P, KD, GT])
        kv = tile4.take([T, GB, 2 * D])
        ek = tile4.take([T, GB, D])
        dep = tile4.take([T, GB, D])
        eq = tile4.take([P, KD, GT])
        rq = tile4.take([P, KD, GT])
        gq = tile4.take([P, KD, GT])
        qg = tile4.take([P, KD, GT])
        conv = tile4.take([T, GB, D])
        convT = tile4.take([P, KD, GT])
        f = tile4.take([P, KD, GT])
        (mixed, slab_ready, ek_steps, kf_ready, dep_ready, q_parts, qf_ready, qg_ready, bout_added, hn_stored) = (
            sem(n) for n in ("mixed", "slab_ready", "ek_steps", "kf_ready", "dep_ready", "q_parts", "qf_ready",
                             "qg_ready", "bout_added", "hn_stored"))

        def is0(g):
            return isinstance(g, int) and g == 0

        class Norm:

            def __init__(self, tag, r, dst):
                self.r, self.dst = r, dst
                self.stats = tile4.take([T, GB, 6])
                self.mv = tile4.take([T, GB, 2])
                self.w = tile4.take([T, 2, GB])
                self.zz = tile4.take([T, GB, D])
                self.stat, self.mean, self.rstd, self.row = (
                    sem(tag + n) for n in ("_stat", "_mean", "_rstd", "_row"))

            def vector_stats(self, v, g):
                v.sem_inc(ln_turn, 1)
                for b in range(GB):
                    last = nc.vector.bn_stats(self.stats[:, b, :], h[:, g, b, :])
                last.then_inc(self.stat, 1)
                v.wait_ge(self.stat, g + 1)
                if not is0(g):
                    v.wait_ge(self.rstd, 2 * g)
                v.sem_inc(ln_turn, 1)
                for b in range(GB):
                    last = nc.vector.bn_aggr(self.mv[:, b, :], self.stats[:, b, :])
                last.then_inc(self.mean, 1)

            def pool_rstd(self, pool, g):
                pool.wait_ge(self.mean, g + 1)
                if not is0(g):
                    pool.wait_ge(self.row, g)
                nc.gpsimd.tensor_tensor(self.w[:, 0, :], self.mv[:, :, 1], pows[:, 2, :], ALU.add).then_inc(self.rstd, 1)
                pool.wait_ge(self.rstd, 2 * g + 1)
                nc.gpsimd.tensor_tensor(self.w[:, 1, :], self.w[:, 0, :], pows[:, 0, :], ALU.pow).then_inc(self.rstd, 1)

            def vector_rows(self, v, g):
                v.wait_ge(self.rstd, 2 * g + 2)
                if not is0(g):
                    self.r.wait_filled(v, g - 1, 1)
                for b in range(GB):
                    last = nc.vector.tensor_scalar(self.zz[:, b, :], h[:, g, b, :], self.mv[:, b, 0:1],
                                                   self.w[:, 1, b:b + 1], ALU.subtract, ALU.mult)
                last.then_inc(self.row, 1)

            def tensor_turn(self, pe, g):
                pe.wait_ge(self.row, g + 1)
                for k in range(KD):
                    self.r.wait_free(pe, g, k)
                    for b in range(GB):
                        last = nc.tensor.transpose(self.r.bank(k)[:, b * T:(b + 1) * T],
                                                   self.zz[:, b, k * P:(k + 1) * P], ident[0:T, 0:T])
                    self.r.fill(last, k)

            def scalar_out(self, act, g):
                for k in range(KD):
                    self.r.wait_filled(act, g, k)
                    self.r.drain(nc.scalar.activation(self.dst[:, k, :], self.r.bank(k)[:, 0:GT], ACT.Copy), k)
                self.r.wait_drained(act, g, KD - 1)

        rb = ring(0, 4, 8)
        rc = ring(4, 2, 8)
        first = Norm("first", ring(6, 1, 2), slab)
        second = Norm("second", ring(7, 1, 2), lnT)

        block = nc.Block()
        with block:
            @block.sync
            def _(sp):
                def store(g):
                    second.r.wait_drained(sp, g, KD - 1)
                    sp.dma_start(hnT[:, :, g, :], lnT).then_inc(hn_stored, 16)

                for dst, n in kernel_loads:
                    sp.dma_start(dst, a[n]).then_inc(kernel_loaded, 16)
                for g in range(2):
                    sp.dma_start(h[:, g].rearrange("p b d -> p (b d)"), h_d[g]).then_inc(h_first, 16)
                for dst, n in loads:
                    sp.dma_start(dst, a[n]).then_inc(w4_loaded, 16)
                for g in range(2, G):
                    sp.dma_start(h[:, g].rearrange("p b d -> p (b d)"), h_d[g]).then_inc(h_back, 16)
                for dst, n in raws:
                    sp.dma_start(dst.bitcast(I32), a[n]).then_inc(raw_loaded, 16)
                kernels_sync(sp)
                store(0)
                with sp.Fori(1, G) as g:
                    store(g)
                sp.wait_ge(toep_loaded, 16)
                sp.wait_ge(hn_stored, 16 * G)

            @block.tensor
            def _(pe):
                def keys_values(g):
                    pe.wait_ge(slab_ready, g + 1)
                    for b in range(GB):
                        rb.wait_free(pe, g, b)
                        for k in range(KD):
                            last = nc.tensor.matmul(rb.bank(b)[0:T, 0:512], slab[:, k, b * T:(b + 1) * T],
                                                    wqk[:, k, D:3 * D], start=(k == 0), stop=(k == KD - 1))
                        rb.fill(last, b)

                def queries_gates(g):
                    for j in range(4):
                        m = 4 + j
                        at = (0, P, 3 * D, 3 * D + P)[j]
                        rb.wait_free(pe, g, m)
                        for k in range(KD):
                            last = nc.tensor.matmul(rb.bank(m)[:, 0:GT], wqk[:, k, at:at + P], slab[:, k, :],
                                                    start=(k == 0), stop=(k == KD - 1))
                        rb.fill(last, m)

                def turn(g, head, tail):
                    if head:
                        first.tensor_turn(pe, g + 1)
                    pe.wait_ge(dep_ready, g + 1)
                    for k in range(2):
                        rc.wait_free(pe, g, k)
                        for jj in range(HC):
                            j = HC * k + jj
                            last = nc.tensor.matmul(rc.bank(k)[0:T, jj * GB * DM:(jj + 1) * GB * DM], toep[:, j, :],
                                                    dep[:, :, j * DM:(j + 1) * DM], start=True, stop=True)
                        rc.fill(last, k)
                    if head:
                        keys_values(g + 1)
                    for k in range(2):
                        rc.wait_drained(pe, g, k)
                    for k in range(KD):
                        rc.wait_free(pe, g, 2 + k)
                        for b in range(GB):
                            last = nc.tensor.transpose(rc.bank(2 + k)[:, b * T:(b + 1) * T],
                                                       conv[:, b, k * P:(k + 1) * P], ident[0:T, 0:T])
                        rc.fill(last, 2 + k)
                    if tail:
                        second.tensor_turn(pe, g - 1)
                    for k in range(KD):
                        rc.wait_drained(pe, g, 2 + k)
                    for i in range(KD):
                        rc.wait_free(pe, g, 4 + i)
                        for k in range(KD):
                            last = nc.tensor.matmul(rc.bank(4 + i)[:, 0:GT], mixT[:, k, i * P:(i + 1) * P], convT[:, k, :],
                                                    start=(k == 0), stop=(k == KD - 1))
                        rc.fill(last, 4 + i)
                    if head:
                        queries_gates(g + 1)
                    for k in range(KD):
                        rc.wait_drained(pe, g, 4 + k)
                    for j in range(2):
                        rc.wait_free(pe, g, 6 + j)
                        for bb in range(2):
                            b = 2 * j + bb
                            for k in range(KD):
                                last = nc.tensor.matmul(rc.bank(6 + j)[0:T, bb * D:(bb + 1) * D],
                                                        f[:, k, b * T:(b + 1) * T], wout[:, k, :],
                                                        start=(k == 0), stop=(k == KD - 1))
                        rc.fill(last, 6 + j)

                kernels_tensor(pe)
                first.tensor_turn(pe, 0)
                pe.wait_ge(w4_loaded, 16 * len(loads))
                keys_values(0)
                queries_gates(0)
                pe.wait_ge(toep_loaded, 16)
                pe.wait_ge(built, MIX_AT)
                turn(0, True, False)
                with pe.Fori(1, G - 3) as g:
                    turn(g, True, True)
                turn(G - 3, True, True)
                turn(G - 2, True, True)
                turn(G - 1, False, True)
                second.tensor_turn(pe, G - 1)

            @block.vector
            def _(v):
                vec = nc.vector

                def experts_in(g, more):
                    v.wait_ge(y_in, 16 * GB * TOPK * (g + 1))
                    for k in range(TOPK):
                        for b in range(GB):
                            last = vec.scalar_tensor_tensor(h[:, g, b, :], yg[:, b, k, :], weight[:, g, b, k:k + 1],
                                                            h[:, g, b, :], ALU.mult, ALU.add)
                        last.then_inc(mixed, 1)
                        v.wait_ge(mixed, TOPK * g + k + 1)
                    if more:
                        vec.tensor_copy(pg, place_i[:, g + 1]).then_inc(pg_ready, 1)

                def keys_values(g):
                    for b in range(GB):
                        if b == 0 and not is0(g):
                            v.wait_ge(dep_ready, g)
                        rb.wait_filled(v, g, b)
                        rb.drain(vec.tensor_tensor(kv[:, b, :], rb.bank(b)[0:T, 0:512], bias_kv, ALU.add), b)

                def deposits(g):
                    v.wait_ge(ek_steps, 2 * g + 2)
                    vec.scalar_tensor_tensor(ek, kv[:, :, 0:D], 0.0, ek, ALU.max, ALU.add).then_inc(kf_ready, 1)
                    v.wait_ge(kf_ready, g + 1)
                    if not is0(g):
                        rc.wait_filled(v, g - 1, 1)
                    vec.tensor_tensor(dep, ek, kv[:, :, D:2 * D], ALU.mult).then_inc(dep_ready, 1)

                def queries(g):
                    v.wait_ge(q_parts, 6 * g + 6)
                    vec.scalar_tensor_tensor(rq, eq, 1.0, rq, ALU.min, ALU.add).then_inc(qf_ready, 1)
                    v.wait_ge(qf_ready, g + 1)
                    vec.tensor_tensor(qg, rq, gq, ALU.mult).then_inc(qg_ready, 1)

                def turn(g, head, ahead, more, tail):
                    if tail:
                        second.vector_rows(v, g - 1)
                    if head:
                        keys_values(g + 1)
                    if ahead:
                        experts_in(g + 2, more)
                    if head:
                        deposits(g + 1)
                    v.wait_ge(qg_ready, g + 1)
                    for k in range(KD):
                        if not is0(g):
                            rc.wait_filled(v, g - 1, 7)
                        rc.wait_filled(v, g, 4 + k)
                        rc.drain(vec.tensor_tensor(f[:, k, :], qg[:, k, :], rc.bank(4 + k)[:, 0:GT], ALU.mult), 4 + k)
                    if ahead:
                        first.vector_stats(v, g + 2)
                    if head:
                        queries(g + 1)
                    if ahead:
                        first.vector_rows(v, g + 2)
                    v.wait_ge(bout_added, g + 1)
                    for j in range(2):
                        rc.wait_filled(v, g, 6 + j)
                        rows = h[:, g, 2 * j:2 * j + 2, :]
                        rc.drain(vec.tensor_tensor(rows, rows, rc.bank(6 + j)[0:T, :].rearrange("p (b d) -> p b d", b=2),
                                                   ALU.add), 6 + j)
                    for j in range(2):
                        rc.wait_drained(v, g, 6 + j)
                    second.vector_stats(v, g)

                vec.tensor_copy(pg, place_i[:, 0]).then_inc(pg_ready, 1)
                v.wait_ge(kernel_loaded, 16 * len(kernel_loads))
                kernels_vector(v)
                v.wait_ge(h_first, 32)
                experts_in(0, True)
                first.vector_stats(v, 0)
                first.vector_rows(v, 0)
                v.wait_ge(w4_loaded, 16 * len(loads))
                keys_values(0)
                experts_in(1, True)
                first.vector_stats(v, 1)
                deposits(0)
                first.vector_rows(v, 1)
                queries(0)
                v.wait_ge(h_back, 16 * (G - 2))
                turn(0, True, True, True, False)
                with v.Fori(1, G - 3) as g:
                    turn(g, True, True, True, True)
                turn(G - 3, True, True, False, True)
                turn(G - 2, True, False, False, True)
                turn(G - 1, False, False, False, True)
                second.vector_rows(v, G - 1)

            @block.scalar
            def _(act):
                def slab_out(g):
                    first.scalar_out(act, g)
                    act.sem_inc(slab_ready, 1)

                def keys(g):
                    for b in range(GB):
                        rb.wait_drained(act, g, b)
                    if not is0(g):
                        act.wait_ge(dep_ready, g)
                    nc.scalar.activation(ek, kv[:, :, 0:D], ACT.Relu, scale=-1.0).then_inc(ek_steps, 1)
                    act.wait_ge(ek_steps, 2 * g + 1)
                    nc.scalar.activation(ek, ek, ACT.Exp, scale=-1.0).then_inc(ek_steps, 1)

                def queries(g):
                    if not is0(g):
                        act.wait_ge(qg_ready, g)
                    for k in range(KD):
                        m = 4 + k
                        src = rb.bank(m)[:, 0:GT]
                        rb.wait_filled(act, g, m)
                        nc.scalar.activation(eq[:, k, :], src, ACT.Exp, bias=biasqg[:, k:k + 1]).then_inc(q_parts, 1)
                        rb.drain(nc.scalar.activation(rq[:, k, :], src, ACT.Relu, bias=biasqg[:, k:k + 1]), m)
                    for k in range(KD):
                        m = 6 + k
                        rb.wait_filled(act, g, m)
                        rb.drain(nc.scalar.activation(gq[:, k, :], rb.bank(m)[:, 0:GT], ACT.Sigmoid,
                                                      bias=biasqg[:, 2 + k:3 + k]), m)
                    for m in range(4, 8):
                        rb.wait_drained(act, g, m)
                        act.sem_inc(q_parts, 1)

                def turn(g, head, tail):
                    if head:
                        slab_out(g + 1)
                    for k in range(2):
                        rc.wait_filled(act, g, k)
                        rc.drain(nc.scalar.activation(
                            conv.rearrange("p b (j d) -> p b j d", d=DM)[:, :, k * HC:(k + 1) * HC, :],
                            rc.bank(k)[0:T, :].rearrange("p (j b d) -> p b j d", j=HC, b=GB), ACT.Copy), k)
                    for k in range(KD):
                        rc.wait_filled(act, g, 2 + k)
                        rc.drain(nc.scalar.activation(convT[:, k, :], rc.bank(2 + k)[:, 0:GT], ACT.Copy), 2 + k)
                    if head:
                        keys(g + 1)
                    if tail:
                        norm_out(g - 1)
                    if head:
                        queries(g + 1)

                def norm_out(g):
                    if not is0(g):
                        act.wait_ge(hn_stored, 16 * g)
                    second.scalar_out(act, g)

                act.wait_ge(kernel_loaded, 16 * len(kernel_loads))
                kernels_scalar(act)
                slab_out(0)
                keys(0)
                queries(0)
                turn(0, True, False)
                with act.Fori(1, G - 3) as g:
                    turn(g, True, True)
                turn(G - 3, True, True)
                turn(G - 2, True, True)
                turn(G - 1, False, True)
                norm_out(G - 1)

            @block.gpsimd
            def _(pool):
                def add_bout(g):
                    pool.wait_ge(first.row, g + 1)
                    nc.gpsimd.tensor_tensor(h[:, g], h[:, g], bout.unsqueeze(1).broadcast_to([T, GB, D]),
                                            ALU.add).then_inc(bout_added, 1)

                def turn(g, ahead, more, tail):
                    if tail:
                        second.pool_rstd(pool, g - 1)
                    add_bout(g)
                    if more:
                        gather(pool, g + 3)
                    if ahead:
                        first.pool_rstd(pool, g + 2)

                gather(pool, 0)
                first.pool_rstd(pool, 0)
                gather(pool, 1)
                first.pool_rstd(pool, 1)
                pool.wait_ge(w4_loaded, 16 * len(loads))
                gather(pool, 2)
                turn(0, True, True, False)
                with pool.Fori(1, G - 3) as g:
                    turn(g, True, True, True)
                turn(G - 3, True, False, True)
                pool.wait_ge(raw_loaded, 16 * len(raws))
                for dst, n in raws:
                    nc.gpsimd.tensor_scalar(dst, dst.bitcast(I32), float(np.float32(1.0 / 127.0)), None,
                                            ALU.mult)
                turn(G - 2, False, False, True)
                turn(G - 1, False, False, True)
                second.pool_rstd(pool, G - 1)

        fin = Space(arena, late.at, ARENA)
        hid = fin.take([P, 2, KF, GT])
        sg = fin.take([P, 2, GT])
        hid_ready, rows_ready = sem("hid_ready"), sem("rows_ready")
        ru = ring(0, 4, 2 * KF)
        rd = ring(4, 4, 4, groups=G // 2)
        block = nc.Block()
        with block:
            @block.tensor
            def _(pe):
                def up(i, s):
                    g = 2 * i + s
                    for c in range(KF):
                        for j, w_ in enumerate((wg, wu)):
                            m = 2 * c + j
                            ru.wait_free(pe, g, m)
                            for k in range(KD):
                                last = nc.tensor.matmul(ru.bank(m)[:, 0:GT], w_[:, k, c * P:(c + 1) * P], hnT[:, k, g, :],
                                                        start=(k == 0), stop=(k == KD - 1))
                            ru.fill(last, m)

                def down(i, s):
                    g = 2 * i + s
                    pe.wait_ge(hid_ready, KF * g + KF)
                    for j in range(2):
                        m = 2 * (s % 2) + j
                        gg = i + s // 2
                        rd.wait_free(pe, gg, m)
                        for bb in range(2):
                            b = 2 * j + bb
                            for c in range(KF):
                                last = nc.tensor.matmul(rd.bank(m)[0:T, bb * D:(bb + 1) * D],
                                                        hid[:, s % 2, c, b * T:(b + 1) * T], wd[:, c, :],
                                                        start=(c == 0), stop=(c == KF - 1))
                        rd.fill(last, m)

                up(0, 0)
                with pe.Fori(0, G // 2 - 1) as i:
                    for s in range(2):
                        up(i, s + 1)
                        down(i, s)
                up(G // 2 - 1, 1)
                down(G // 2 - 1, 0)
                down(G // 2 - 1, 1)

            @block.scalar
            def _(act):
                def gates(g):
                    for c in range(KF):
                        m = 2 * c
                        ru.wait_filled(act, g, m)
                        if not (isinstance(g, int) and g == 0 and c < 2):
                            act.wait_ge(hid_ready, KF * g + c - 1)
                        ru.drain(nc.scalar.activation(sg[:, c % 2, :], ru.bank(m)[:, 0:GT], ACT.Silu), m)

                gates(0)
                with act.Fori(1, G) as g:
                    gates(g)

            @block.vector
            def _(v):
                def mul(i, s):
                    g = 2 * i + s
                    if not (isinstance(i, int) and i == 0 and s < 2):
                        rd.wait_filled(v, i + s // 2 - 1, 2 * (s % 2) + 1)
                    for c in range(KF):
                        m = 2 * c + 1
                        v.wait_ge(ru.drained[(m - 1) % 4], ru.before(g, m - 1) + 1)
                        ru.wait_filled(v, g, m)
                        ru.drain(nc.vector.tensor_tensor(hid[:, s % 2, c, :], sg[:, c % 2, :], ru.bank(m)[:, 0:GT],
                                                         ALU.mult), m)
                        v.wait_ge(ru.drained[m % 4], ru.before(g, m) + 1)
                        v.sem_inc(hid_ready, 1)

                def add(i, s):
                    g = 2 * i + s
                    for j in range(2):
                        m = 2 * s + j
                        rd.wait_filled(v, i, m)
                        rows = h[:, g, 2 * j:2 * j + 2, :]
                        rd.drain(nc.vector.tensor_tensor(rows, rows, rd.bank(m)[0:T, :].rearrange("p (b d) -> p b d", b=2),
                                                         ALU.add), m)
                    for j in range(2):
                        v.wait_ge(rd.drained[2 * s + j], rd.before(i, 2 * s + j) + 1)
                    v.sem_inc(rows_ready, 1)

                mul(0, 0)
                with v.Fori(0, G // 2 - 1) as i:
                    for s in range(2):
                        mul(i, s + 1)
                        add(i, s)
                mul(G // 2 - 1, 1)
                add(G // 2 - 1, 0)
                add(G // 2 - 1, 1)

            @block.sync
            def _(sp):
                with sp.Fori(0, G) as g:
                    sp.wait_ge(rows_ready, g + 1)
                    sp.dma_start(out[:, bass.ds(GB * g, GB), :], h[:, g]).then_inc(out_stored, 16)
                sp.wait_ge(out_stored, 16 * G)


def layouts(x, txt, i):
    f = np.float32

    def chunks(m):
        k, n = m.shape
        return m.reshape(k // P, P, n).transpose(1, 0, 2)

    def column(v):
        return v.reshape(-1, P).T

    o = {}
    p = x.reshape(G, GB, 3, 8, 16, 8, 16).transpose(0, 4, 6, 2, 1, 3, 5)
    o["patches"] = p.reshape(G, KP, P, GB * IMG).transpose(0, 2, 1, 3)
    o["txt"] = txt.transpose(1, 0, 2)
    o["wpT"] = chunks(i["L0_tok_Wp"].T)
    o["tokb"] = np.broadcast_to(i["L0_tok_b"], (P, D))
    gh, gw = np.meshgrid(np.arange(8), np.arange(8), indexing="ij")
    quarter = D // 4
    factor = f(10000.0) ** (np.arange(quarter, dtype=f) / f(quarter))
    hh = gh.reshape(-1).astype(f)[:, None] / factor
    ww = gw.reshape(-1).astype(f)[:, None] / factor
    pos = np.concatenate([np.sin(hh), np.cos(hh), np.sin(ww), np.cos(ww)], axis=-1).astype(f)
    o["pos2"] = np.concatenate([pos, pos], axis=0)
    o["ident"] = np.eye(P, dtype=f)
    inv_freq = 1.0 / 10000.0 ** (np.arange(0, DH, 2, dtype=f) / DH)
    freqs = np.outer(np.arange(T, dtype=f), inv_freq)
    cos = np.concatenate([np.cos(freqs), np.cos(freqs)], -1)[:, ::2].astype(f).T
    sin = np.concatenate([np.sin(freqs), np.sin(freqs)], -1)[:, ::2].astype(f).T
    o["ropeC"] = np.concatenate([cos] * 4, axis=0)
    o["ropeS"] = np.concatenate([-sin, sin, -sin, sin], axis=0)
    o["ropeCq"] = o["ropeC"] * f(1 / np.sqrt(DH))
    o["ropeSq"] = o["ropeS"] * f(1 / np.sqrt(DH))
    o["gb"] = np.stack([np.stack([column(i[s]), column(i[t])], 1) for s, t in (
        ("L0_attn_ln_scale", "L0_attn_ln_bias"), ("L0_ffn_ln1_g", "L0_ffn_ln1_b"), ("L0_ffn_ln2_g", "L0_ffn_ln2_b"))], 1)
    n = np.arange(HID).reshape(NH, DH)
    straight = np.concatenate([n[:, 0::2], n[:, 1::2]], 1).reshape(-1)
    swapped = np.concatenate([n[:, 1::2], n[:, 0::2]], 1).reshape(-1)
    o["wdq"] = chunks(i["L0_attn_w_down_q"].T)
    o["wdkv"] = chunks(i["L0_attn_w_down_kv"].T)
    o["wuq"] = i["L0_attn_w_up_q"][straight].T
    o["wuqs"] = i["L0_attn_w_up_q"][swapped].T
    o["wuk"] = i["L0_attn_w_up_k"][straight].T
    o["wuks"] = i["L0_attn_w_up_k"][swapped].T
    o["wuv"] = i["L0_attn_w_up_v"].T
    o["woT"] = chunks(i["L0_attn_w_out"].T)
    for k, s in (("wq2", "Wq"), ("wk2", "Wk"), ("wv2", "Wv"), ("wp2", "Wp")):
        o[k] = chunks(i["L0_ffn_" + s])
    o["bB"] = np.stack([column(i["L0_ffn_" + s]) for s in ("bq", "bk", "bv")], 1)
    o["hmask"] = (np.arange(P)[:, None] // DM == np.arange(HC)[None, :]).astype(f) * f(1 / np.sqrt(DM))
    o["causal"] = np.where(np.arange(T)[None, :] <= np.arange(T)[:, None], f(0), f(NEG))
    o["tri"] = (np.arange(T)[:, None] < np.arange(T)[None, :]).astype(f)
    o["bpb"] = np.broadcast_to(i["L0_ffn_bp"], (T, D))
    o["gateW"] = chunks(i["L0_ffn_gate_W"])
    o["gateb"] = np.broadcast_to(i["L0_ffn_gate_b"], (T, E))
    o["ids"] = (np.arange(T)[:, None, None] + T * np.arange(B).reshape(1, G, GB)).astype(np.int32)
    o["iota8"] = np.broadcast_to(np.arange(E, dtype=f), (T, E))
    o["iota_t"] = np.broadcast_to(np.arange(TILES, dtype=f), (T, TILES))
    o["W1"] = i["L0_ffn_exp_W1"].reshape(E, KD, P, HID).transpose(2, 0, 1, 3)
    o["W2"] = i["L0_ffn_exp_W2"].reshape(E, KH, P, D).transpose(2, 0, 1, 3)
    o["b1"] = np.broadcast_to(i["L0_ffn_exp_b1"], (P, E, HID))
    o["b2"] = np.broadcast_to(i["L0_ffn_exp_b2"], (P, E, D))
    o["wqk"] = chunks(i["L1_attn_Wqkvg"].T)
    o["wout4"] = chunks(i["L1_attn_Wout"].T)
    o["bias_kv"] = np.broadcast_to(i["L1_attn_bqkvg"][D:3 * D], (T, 2 * D))
    o["biasqg"] = column(np.concatenate([i["L1_attn_bqkvg"][:D], i["L1_attn_bqkvg"][3 * D:]]))
    o["bout"] = np.broadcast_to(i["L1_attn_bout"], (T, D))
    o["lag"] = np.broadcast_to(np.arange(FIELD, dtype=f), (NH, FIELD))
    o["pw"] = np.stack([i["L1_attn_wave_frequency"], i["L1_attn_wave_damping"], i["L1_attn_wave_phase"]], 1)
    o["fc"] = i["L1_attn_field_coupling"]
    o["dmask"] = (np.arange(P)[:, None] % DM == np.arange(DM)[None, :]).astype(f)
    o["wg_i"] = chunks(i["L1_ffn_w_gate"].T)
    o["wu_i"] = chunks(i["L1_ffn_w_up"].T)
    o["wd_i"] = chunks(i["L1_ffn_w_down"].T)
    return {k: np.ascontiguousarray(v) for k, v in o.items()}


def kernel(x, txt, **inputs):
    import concourse.bacc as _bacc
    from concourse.bass_utils import run_bass_kernel_spmd as _run

    nc = _bacc.Bacc("TRN2", target_bir_lowering=False, num_devices=1)
    arrays = layouts(np.asarray(x), np.asarray(txt), {k: np.asarray(v) for k, v in inputs.items()})
    aps = {k: nc.dram_tensor("in_" + k, v.shape, mybir.dt.from_np(v.dtype), kind="ExternalInput").ap()
           for k, v in arrays.items()}
    out = nc.dram_tensor("out", (T, B, D), F32, kind="ExternalOutput").ap()
    program(nc, aps, out)
    r = _run(nc, [{"in_" + k: v for k, v in arrays.items()}], core_ids=[0])
    return np.ascontiguousarray(r.results[0]["out"].transpose(1, 0, 2))
```
